# Optimizing a Trainium2 kernel written in Bass

```python
import numpy as np
import jax
import jax.numpy as jnp

def _softmax(x, axis=-1):
    return jax.nn.softmax(x, axis=axis)

def _gelu(x):
    return jax.nn.gelu(x, approximate=True)

def _silu(x):
    return jax.nn.silu(x)

def _sigmoid(x):
    return jax.nn.sigmoid(x)

def _layernorm(x, axis=-1, eps=1e-05):
    m = jnp.mean(x, axis=axis, keepdims=True)
    v = jnp.var(x, axis=axis, keepdims=True)
    return (x - m) / jnp.sqrt(v + eps)

def _scatter_add(tgt, idx, src, axis=0):
    return tgt.at[idx].add(src)

def _segment_sum(src, seg, n):
    return jax.ops.segment_sum(src, seg, n)
kernel_name = 'mk_vit_tower_cls_d1_tok_img1024_r4_9a590f'

def setup_inputs(seed: int=0):
    np.random.seed(seed)
    _w = jnp.asarray

    def _rec_inputs():
        import jax
        import jax.numpy as jnp
        _rk = jax.random.key(seed)
        x = -0.000125008 + 0.999885 * jax.random.normal(jax.random.fold_in(_rk, 1), (16, 512, 256, 4), jnp.float32)
        cls_tok = 0.02 * jax.random.normal(jax.random.fold_in(_rk, 5), (1, 1, 256), jnp.float32)
        return (x, cls_tok)
    x, cls_tok = _rec_inputs()

    def _L0_tok_setup():
        import jax, jax.numpy as jnp
        import numpy as np
        key = jax.random.key(seed)
        k1, k2, k3 = jax.random.split(key, 3)
        B, H, I, O, Dp1 = (4, 512, 256, 256, 4)
        x = jax.random.normal(k1, (B, H, I, Dp1), dtype=jnp.float32)
        weight = 0.1 * jax.random.normal(k2, (O, Dp1), dtype=jnp.float32)
        weighted_sum = 0.1 * jax.random.normal(k3, (O, I), dtype=jnp.float32)
        return {'x': x, 'weight': weight, 'weighted_sum': weighted_sum}
    _L0_tok_all = _L0_tok_setup()
    _L0_tok_in = {k: v for k, v in _L0_tok_all.items() if k in ('weight', 'weighted_sum')}
    del _L0_tok_all

    def _L0_attn_setup():
        import jax, jax.numpy as jnp
        import numpy as np
        import math
        D_MODEL, D_C, D_R, NH = (256, 128, 32, 16)
        HD = D_MODEL // NH
        B, T = (2, 512)

        def _rope_tables(T, d_R):
            inv_freq = 1.0 / 10000.0 ** (jnp.arange(0, d_R, 2, dtype=jnp.float32) / d_R)
            t = jnp.arange(T, dtype=jnp.float32)
            freqs = jnp.outer(t, inv_freq)
            return (jnp.cos(freqs), jnp.sin(freqs))

        def _rotary_apply(x, cos, sin):
            d = x.shape[-1]
            x1, x2 = (x[..., :d // 2], x[..., d // 2:])
            return jnp.concatenate([x1 * cos - x2 * sin, x2 * cos + x1 * sin], axis=-1)
        key = jax.random.key(seed)
        ks = jax.random.split(key, 8)
        s = lambda fan_in: 1.0 / math.sqrt(fan_in)
        return {'x': jax.random.normal(ks[0], (B, T, D_MODEL), jnp.float32), 'W_kv_down': jax.random.normal(ks[1], (D_MODEL, D_C), jnp.float32) * s(D_MODEL), 'W_k_up': jax.random.normal(ks[2], (D_C, D_MODEL), jnp.float32) * s(D_C), 'W_v_up': jax.random.normal(ks[3], (D_C, D_MODEL), jnp.float32) * s(D_C), 'W_q': jax.random.normal(ks[4], (D_MODEL, D_MODEL), jnp.float32) * s(D_MODEL), 'W_q_rope': jax.random.normal(ks[5], (D_MODEL, D_R), jnp.float32) * s(D_MODEL), 'W_k_rope': jax.random.normal(ks[6], (D_C, D_R), jnp.float32) * s(D_C), 'W_o': jax.random.normal(ks[7], (D_MODEL, D_MODEL), jnp.float32) * s(D_MODEL)}
    _L0_attn_all = _L0_attn_setup()
    _L0_attn_in = {k: v for k, v in _L0_attn_all.items() if k in ('W_kv_down', 'W_k_up', 'W_v_up', 'W_q', 'W_q_rope', 'W_k_rope', 'W_o')}
    del _L0_attn_all

    def _L0_ffn_setup():
        import jax, jax.numpy as jnp
        import numpy as np
        EPS = 1e-08

        def _ternary_linear(x, w):
            alpha = jnp.mean(jnp.abs(w))
            w_t = jnp.sign(w) * (jnp.abs(w) > 0.5 * alpha).astype(w.dtype)
            w_q = w + jax.lax.stop_gradient(w_t - w)
            d = x.shape[-1]
            rms = jnp.sqrt(jnp.sum(x * x, axis=-1, keepdims=True)) / jnp.sqrt(jnp.asarray(d, x.dtype))
            x_norm = x / (rms + EPS)
            return jnp.einsum('bsd,fd->bsf', x_norm, w_q)
        key = jax.random.key(seed)
        k1, k2, k3 = jax.random.split(key, 3)
        d_model, d_ff = (256, 1024)
        B, S = (4, 1024)
        x = jax.random.normal(k1, (B, S, d_model), dtype=jnp.float32)
        w_up = jax.random.normal(k2, (d_ff, d_model), dtype=jnp.float32) * 0.02
        w_down = jax.random.normal(k3, (d_model, d_ff), dtype=jnp.float32) * 0.02
        return {'x': x, 'w_up': w_up, 'w_down': w_down}
    _L0_ffn_all = _L0_ffn_setup()
    _L0_ffn_in = {k: v for k, v in _L0_ffn_all.items() if k in ('w_up', 'w_down')}
    del _L0_ffn_all
    return {'x': x, 'cls_tok': cls_tok, 'L0_tok_weight': _L0_tok_in['weight'], 'L0_tok_weighted_sum': _L0_tok_in['weighted_sum'], 'L0_attn_W_kv_down': _L0_attn_in['W_kv_down'], 'L0_attn_W_k_up': _L0_attn_in['W_k_up'], 'L0_attn_W_v_up': _L0_attn_in['W_v_up'], 'L0_attn_W_q': _L0_attn_in['W_q'], 'L0_attn_W_q_rope': _L0_attn_in['W_q_rope'], 'L0_attn_W_k_rope': _L0_attn_in['W_k_rope'], 'L0_attn_W_o': _L0_attn_in['W_o'], 'L0_ffn_w_up': _L0_ffn_in['w_up'], 'L0_ffn_w_down': _L0_ffn_in['w_down']}

def reference(x, cls_tok, L0_tok_weight, L0_tok_weighted_sum, L0_attn_W_kv_down, L0_attn_W_k_up, L0_attn_W_v_up, L0_attn_W_q, L0_attn_W_q_rope, L0_attn_W_k_rope, L0_attn_W_o, L0_ffn_w_up, L0_ffn_w_down):
    import jax
    import jax.numpy as jnp

    def _L0_tok_ref(x, weight, weighted_sum):
        import jax, jax.numpy as jnp
        import numpy as np
        return jnp.einsum('bhid,oi,od->bho', x, weighted_sum, weight)

    def _L0_attn_ref(x, W_kv_down, W_k_up, W_v_up, W_q, W_q_rope, W_k_rope, W_o):
        import jax, jax.numpy as jnp
        import numpy as np
        import math
        D_MODEL, D_C, D_R, NH = (256, 128, 32, 16)
        HD = D_MODEL // NH
        B, T = (2, 512)

        def _rope_tables(T, d_R):
            inv_freq = 1.0 / 10000.0 ** (jnp.arange(0, d_R, 2, dtype=jnp.float32) / d_R)
            t = jnp.arange(T, dtype=jnp.float32)
            freqs = jnp.outer(t, inv_freq)
            return (jnp.cos(freqs), jnp.sin(freqs))

        def _rotary_apply(x, cos, sin):
            d = x.shape[-1]
            x1, x2 = (x[..., :d // 2], x[..., d // 2:])
            return jnp.concatenate([x1 * cos - x2 * sin, x2 * cos + x1 * sin], axis=-1)
        Bb, Tt, _ = x.shape
        cos, sin = _rope_tables(Tt, D_R)
        cos = cos[None]
        sin = sin[None]
        c_kv = x @ W_kv_down
        k_rope = _rotary_apply(c_kv @ W_k_rope, cos, sin)
        k = (c_kv @ W_k_up).reshape(Bb, Tt, NH, HD)
        v = (c_kv @ W_v_up).reshape(Bb, Tt, NH, HD)
        q = (x @ W_q).reshape(Bb, Tt, NH, HD)
        q_rope = _rotary_apply(x @ W_q_rope, cos, sin)
        scale = math.sqrt(HD + D_R)
        scores = jnp.einsum('bqhd,bkhd->bhqk', q, k)
        scores = scores + jnp.einsum('bqr,bkr->bqk', q_rope, k_rope)[:, None]
        scores = scores / scale
        causal = jnp.triu(jnp.ones((Tt, Tt), dtype=bool), k=1)
        scores = jnp.where(causal[None, None], -jnp.inf, scores)
        w = jax.nn.softmax(scores, axis=-1)
        attn = jnp.einsum('bhqk,bkhd->bqhd', w, v).reshape(Bb, Tt, D_MODEL)
        return attn @ W_o

    def _L0_ffn_ref(x, w_up, w_down):
        import jax, jax.numpy as jnp
        import numpy as np
        EPS = 1e-08

        def _ternary_linear(x, w):
            alpha = jnp.mean(jnp.abs(w))
            w_t = jnp.sign(w) * (jnp.abs(w) > 0.5 * alpha).astype(w.dtype)
            w_q = w + jax.lax.stop_gradient(w_t - w)
            d = x.shape[-1]
            rms = jnp.sqrt(jnp.sum(x * x, axis=-1, keepdims=True)) / jnp.sqrt(jnp.asarray(d, x.dtype))
            x_norm = x / (rms + EPS)
            return jnp.einsum('bsd,fd->bsf', x_norm, w_q)
        h = jax.nn.gelu(_ternary_linear(x, w_up), approximate=False)
        return _ternary_linear(h, w_down)
    h = _L0_tok_ref(x, L0_tok_weight, L0_tok_weighted_sum)
    h = jnp.concatenate([jnp.broadcast_to(cls_tok, (h.shape[0], 1, h.shape[2])), h], axis=1)
    h = h + _L0_attn_ref(_layernorm(h, axis=-1), L0_attn_W_kv_down, L0_attn_W_k_up, L0_attn_W_v_up, L0_attn_W_q, L0_attn_W_q_rope, L0_attn_W_k_rope, L0_attn_W_o)
    h = h + _L0_ffn_ref(_layernorm(h, axis=-1), L0_ffn_w_up, L0_ffn_w_down)
    return h

_drawn_inputs = setup_inputs


def setup_inputs(seed=0):
    import zlib

    import numpy as np

    out = dict(_drawn_inputs(seed))
    spreads = {}
    factors = {}
    for name, (base, spread) in spreads.items():
        noise = np.random.default_rng([zlib.crc32(name.encode()), seed]).standard_normal(out[name].shape)
        drawn = base * np.exp(spread * noise) if base else spread * noise
        out[name] = jnp.asarray(drawn.astype(out[name].dtype))
    for name, factor in factors.items():
        out[name] = (out[name] * factor).astype(out[name].dtype)
    return out
```

```python
from contextlib import ExitStack

import concourse.bass as bass
from concourse import mybir

F32 = mybir.dt.float32
F32R = mybir.dt.float32r
BF16 = mybir.dt.bfloat16
ALU = mybir.AluOpType
ACT = mybir.ActivationFunctionType
AX_X = mybir.AxisListType.X

P = 128
LN_EPS = 1e-5
RMS_EPS = 1e-8
MASKED = -1e30


def constant_layout(head_count, tokens):
    widths = {"identity": P, "causal": P, "fold_q": 96, "fold_k": 96, "head_of": 2 * head_count,
              "ones": P, "powers": 8, "rope": tokens}
    at, first = {}, 0
    for name, width in widths.items():
        at[name] = (first, width)
        first += width
    return at, first


def vit_tower_kernel(nc, x, cls_tok, tok_weight, tok_sum, w_kv_down, w_k_up, w_v_up, w_q,
                     w_q_rope, w_k_rope, w_o, w_ffn_up, w_ffn_down, constants, out):
    B, T, _, DIN = x.shape
    D = cls_tok.shape[2]
    DC = w_kv_down.shape[1]
    DR = w_q_rope.shape[1]
    FF = w_ffn_up.shape[0]
    H = 16
    HD = D // H
    TT = T // P
    FT = D // P
    KT = D * DIN // P
    GT = FF // P
    HALF = DR // 2
    GH = 4
    NG = H // GH
    SCALE = float(HD + DR) ** -0.5
    CONTENT = 3 * HD
    ROWS = 80
    ROPE = 3 * DR
    VW = 32
    XRING, GRING = 3, 3
    at, n_const = constant_layout(H, T)

    bank_of, fill_of, read_of, before, fills, reads = {}, {}, {}, {}, [0] * 8, [0] * 8

    def place(unit, bank, own_fill=True, own_read=True):
        bank_of[unit], before[unit] = bank, reads[bank]
        fills[bank] += own_fill
        reads[bank] += own_read
        fill_of[unit], read_of[unit] = fills[bank], reads[bank]

    for kt in range(KT):
        place(("xT", kt), kt % 2)
    for i in range(TT):
        place(("h", i), 2 + i)
    for f in range(FT):
        place(("fT", 0, f), f)
    place(("c",), 6)
    for t in range(FT):
        place(("q", t), 2 + t)
    for t in range(FT):
        place(("k", t), 4 + t)
    place(("rot",), 7)
    for u in range(2):
        place(("v", u), u)
    place(("rope_q",), 6)
    place(("rope_k",), 7)
    place(("s0",), 2)
    for hd in range(H + 2):
        for u in range(3):
            if hd < H:
                place(("s", hd, u), 2 + (3 * hd + u) % 4)
        for u in range(3):
            if 1 <= hd <= H:
                place(("pT", hd - 1, u), (0, 1, 6)[u])
        if hd >= 2 and (hd - 2) % GH == 0:
            place(("o", (hd - 2) // GH), 7, own_fill=False)
    for i in range(TT):
        place(("oTok", i), 2 + i)
    for f in range(FT):
        place(("fT", 1, f), f)
    for i in range(TT):
        place(("y", i), 2 + i)
    for f in range(FT):
        place(("fT", 2, f), f)
    for ft in range(GT):
        place(("g", ft), 6 + ft % 2, own_read=False)
    for i in range(TT):
        place(("d", i), 2 + i)
    place(("ss",), 0)

    S_AT = {0: (0, 0), 2: (0, P), 3: (1, 0), 1: (2, 0)}
    PT_AT = {0: (0, 0), 1: (1, 0), 3: (1, 3 * P), 2: (2, 0)}
    S_ORDER = (0, 2, 3, 1)
    PW = 2 * 512 + 256

    ctx = ExitStack()
    with ctx:
        def sb(name, shape, dt=F32):
            return ctx.enter_context(nc.sbuf_tensor(name, shape, dt))

        def sem(name):
            return ctx.enter_context(nc.semaphore(name))

        bank = [ctx.enter_context(nc.psum_tensor(f"bank{n}", [P, 512], F32)) for n in range(8)]

        const = sb("const", [P, n_const])

        def table(name):
            first, width = at[name]
            return const[:, first:first + width]

        ident = table("identity")
        ones = table("ones")
        powers = table("powers").rearrange("p (k i) -> p k i", k=2)
        ident_b = sb("ident_b", [P, P], BF16)
        causal_b = sb("causal_b", [P, P], BF16)
        tok_hi = sb("tok_hi", [P, KT, D], F32R)
        tok_lo = sb("tok_lo", [P, KT, D], F32R)
        widths = {"kv_down": FT * DC, "k_up": D, "v_up": D, "q": FT * D, "o": FT * D,
                  "rot_q": FT * P, "rot_k": P}
        w_at, n_w = {}, 0
        for name, width in widths.items():
            w_at[name] = n_w
            n_w += width
        w_hi = sb("w_hi", [P, n_w], F32R)
        w_lo = sb("w_lo", [P, n_w], F32R)
        up_T = sb("up_T", [P, FT, FF], F32R)
        down_T = sb("down_T", [P, GT, D], F32R)
        k0_hi = sb("k0_hi", [P, FT, H], F32R)
        k0_lo = sb("k0_lo", [P, FT, H], F32R)
        k0_rope = sb("k0_rope", [P, H], F32R)
        v0_all = sb("v0_all", [P, D])

        def weight(half, name, tile, width, first, count):
            a = w_at[name] + tile * width + first
            return half[:, a:a + count]

        x_in = sb("x_in", [P, TT, D * DIN])
        xT_hi = sb("xT_hi", [P, XRING, T], F32R)
        xT_lo = sb("xT_lo", [P, XRING, T], F32R)
        h = sb("h", [P, TT, D])
        xn = sb("xn", [P, TT, D])
        fT_hi = sb("fT_hi", [P, FT, T], F32R)
        fT_lo = sb("fT_lo", [P, FT, T], F32R)
        latent = sb("latent", [P, 2, T], F32R)
        cT_hi, cT_lo = latent[:, 0, :], latent[:, 1, :]
        qk = sb("qk", [P, 2, 2, FT, T], F32R)
        q_stack = sb("q_stack", [P, 2 * GH, T], F32R)
        k_stack = sb("k_stack", [P, 2 * GH, T], F32R)
        prod = sb("prod", [P, T])
        rope_q = sb("rope_q", [P, T], F32R)
        rope_k = sb("rope_k", [P, T], F32R)
        v = sb("v", [P, TT, H, VW])
        probs = sb("probs", [P, 2, PW])
        probs_T = sb("probs_T", [P, 2, PW])
        oT = sb("oT", [P, NG, T])
        g_sb = sb("g_sb", [P, GRING, T])
        g_halves = qk[:, :, :, :, :].rearrange("p w a t n -> p (w a t) n")
        g_hi = g_halves[:, 0:GRING, :]
        g_lo = g_halves[:, GRING:2 * GRING, :]
        g_sq = oT[:, 0:GRING, :]
        g_acc = prod
        out_sb = sb("out_sb", [P, TT, D])
        stats = sb("stats", [P, TT, 6])
        moments = sb("moments", [P, TT, 2])
        col = sb("col", [P, 5, TT])
        base = sb("base", [P, 2, TT])
        root = sb("root", [P, 2, TT])
        neg_s0 = sb("neg_s0", [P, TT, H])
        row_max = sb("row_max", [P, H, TT])
        shift = sb("shift", [P, H, TT])
        p0 = sb("p0", [P, TT, H])
        p0_v0 = g_sb[:, :, :].rearrange("p s n -> p (s n)")[:, 0:TT * D] \
            .rearrange("p (i n) -> p i n", n=D)
        denom = sb("denom", [P, TT, H])
        recip = sb("recip", [P, TT, H])

        x_sum = h[:, :, :].rearrange("p i n -> p (i n)")[:, 0:FT * D] \
            .rearrange("p (t i) -> p t i", t=FT)
        x_wt = sb("x_wt", [P, FT, DIN])
        x_flat = x_in[:, :, :].rearrange("p i n -> p (i n)")
        tok_prod = x_flat[:, 0:FT * D * DIN].rearrange("p (t n) -> p t n", t=FT)
        down_raw = x_flat[:, FT * D * DIN:FT * D * DIN + FT * FF]
        up_raw = probs_T[:, :, :].rearrange("p s n -> p (s n)")[:, 0:GT * D]
        above = oT[:, :, :].rearrange("p g n -> p (g n)")
        w_raw = probs[:, :, :].rearrange("p s n -> p (s n)")[:, 0:n_w]
        row = out_sb
        tiny = sb("tiny", [P, 64])

        scratch = nc.dram_tensor("qk_scratch", [2, 2, FT, P, T], F32, kind="Internal").ap()

        s_weights = sem("weights_loaded")
        s_x = sem("x_loaded")
        s_stored = sem("rows_stored")
        s_tok_prod = sem("tok_product_ready")
        s_abs = sem("abs_sums_ready")
        s_total = sem("abs_total_ready")
        s_ternary = sem("ternary_ready")
        s_setup_full = sem("setup_bank_filled")
        s_setup_hi = sem("setup_bank_copied")
        s_setup_lo = sem("setup_low_half_ready")
        s_weight_raw = sem("rotary_weights_ready")
        s_weight_hi = sem("weight_hi_ready")
        s_weight_lo = sem("weight_lo_ready")
        s_const_b = sem("mask_constants_ready")
        s_setup_dve = sem("setup_vector_step")
        s_setup_base = sem("setup_power_base_ready")
        s_setup_root = sem("setup_power_ready")
        s_cls_pe = sem("cls_product_ready")
        s_cls_dve = sem("cls_operand_ready")
        s_cls_act = sem("cls_gelu_ready")

        filled = [sem(f"bank{n}_filled") for n in range(8)]
        drained = [sem(f"bank{n}_drained") for n in range(8)]
        s_xT_hi = sem("xT_hi_ready")
        s_tok_used = sem("xT_used")
        s_xn = sem("normed_ready")
        s_fT_hi = sem("fT_hi_ready")
        s_half = sem("proj_hi_ready")
        s_rot = sem("rotated_ready")
        s_scratch = sem("scratch_written")
        s_stack = [sem(f"stack{n}_loaded") for n in range(2)]
        s_shift = sem("shift_ready")
        s_pT = sem("probs_T_ready")
        s_pT_act = sem("probs_T_tail_ready")
        s_pv = sem("values_summed")
        s_oT = sem("oT_ready")
        s_p0_in = sem("p0_exponent_ready")
        s_p0 = sem("p0_ready")
        s_p0v0 = sem("p0_v0_ready")
        s_attn = sem("attn_ready")
        s_gelu = sem("gelu_ready")
        s_g_split = sem("g_split_ready")
        s_g_sq = sem("g_squares_ready")
        s_g_acc = sem("g_square_sum_ready")
        s_down = sem("down_used")
        s_out = sem("out_rows_ready")
        s_base = sem("power_base_ready")
        s_root = sem("power_ready")
        s_dve = sem("vector_step")
        cleared = [*filled, *drained, s_xT_hi, s_tok_used, s_xn, s_fT_hi, s_half, s_rot, s_scratch,
                   *s_stack, s_shift, s_pT, s_pT_act, s_pv, s_oT, s_p0_in, s_p0, s_p0v0, s_attn,
                   s_gelu, s_g_split, s_g_sq, s_g_acc, s_down, s_out, s_base, s_root, s_dve]
        numbers = sorted(s.num for s in cleared)
        assert numbers == list(range(numbers[0], numbers[0] + len(numbers)))

        HALVES = ((0, 0), (1, 0), (0, 1))
        w_half = (w_hi, w_lo)
        x_tiles = x.rearrange("b (i p) c d -> b p i (c d)", p=P)
        out_tiles = out[:, 1:T + 1, :].rearrange("b (i p) n -> b p i n", p=P)
        SETUP_UNITS = 4 + 8
        N_WEIGHTS = 13

        with nc.Block() as block:

            @block.sync
            def _(sp):
                def load(dst, src):
                    sp.dma_start(dst, src).then_inc(s_weights, 16)

                load(const[:, :], constants)
                load(x_sum, tok_sum.rearrange("(t p) i -> p t i", p=P))
                load(x_wt[:, :, :], tok_weight.rearrange("(t p) d -> p t d", p=P))
                load(up_raw.rearrange("p (t n) -> p t n", n=D),
                     w_ffn_up.rearrange("(t p) n -> p t n", p=P))
                load(down_raw.rearrange("p (t n) -> p t n", n=FF),
                     w_ffn_down.rearrange("(t p) n -> p t n", p=P))

                def raw(name, t, n):
                    return w_raw[:, w_at[name]:w_at[name] + t * n].rearrange("p (t n) -> p t n", n=n)

                load(raw("kv_down", FT, DC), w_kv_down.rearrange("(t p) n -> p t n", p=P))
                load(raw("k_up", 1, D)[:, 0, :], w_k_up)
                load(raw("v_up", 1, D)[:, 0, :], w_v_up)
                load(raw("q", FT, D), w_q.rearrange("(t p) n -> p t n", p=P))
                load(raw("o", FT, D), w_o.rearrange("(t p) n -> p t n", p=P))
                load(g_sb[:, 0, 0:FT * DR].rearrange("p (t n) -> p t n", n=DR),
                     w_q_rope.rearrange("(t p) n -> p t n", p=P))
                load(g_sb[:, 1, 0:DR], w_k_rope)
                load(row[0:1, 0, :], cls_tok[0])
                sp.wait_ge(s_setup_full, SETUP_UNITS)
                sp.dma_start(x_in[:, :, :],
                             x_tiles[0:1].rearrange("b p i n -> p (b i) n")).then_inc(s_x, 16)
                sp.wait_ge(s_cls_dve, 11)
                for b in range(B):
                    sp.dma_start(out[b, 0:1, :], row[0:1, 2, :]).then_inc(s_stored, 16)
                sp.wait_ge(s_stored, 16 * B)

            @block.gpsimd
            def _(pool):
                nc.gpsimd.memset(v[:, :, :, HD:VW], 0.0).then_inc(s_const_b, 1)
                pool.wait_ge(s_const_b, 1)
                nc.gpsimd.memset(v[:, :, :, HD:HD + 1], 1.0).then_inc(s_const_b, 1)
                pool.wait_ge(s_weights, 16 * N_WEIGHTS)
                for n in range(3):
                    pool.wait_ge(s_setup_base, n + 1)
                    nc.gpsimd.tensor_tensor(root[0:1, :, 0:1], base[0:1, :, 0:1], powers[0:1, :, 0:1],
                                            ALU.pow).then_inc(s_setup_root, 1)

            @block.vector
            def _(dve):
                steps = [0]

                def link(ins):
                    steps[0] += 1
                    ins.then_inc(s_setup_dve, 1)
                    dve.wait_ge(s_setup_dve, steps[0])

                dve.wait_ge(s_weights, 16 * N_WEIGHTS)
                for t in range(FT):
                    for d in range(DIN):
                        last = nc.vector.tensor_scalar(
                            tok_prod[:, t, :].rearrange("p (i d) -> p i d", d=DIN)[:, :, d],
                            x_sum[:, t, :], x_wt[:, t, d:d + 1], None, ALU.mult)
                last.then_inc(s_tok_prod, 1)
                nc.vector.tensor_reduce(tiny[:, 0:1], up_raw, AX_X, ALU.add,
                                        apply_absolute_value=True)
                nc.vector.tensor_reduce(tiny[:, 1:2], down_raw, AX_X, ALU.add,
                                        apply_absolute_value=True).then_inc(s_abs, 1)
                nc.vector.tensor_copy(ident_b[:, :], ident)
                nc.vector.tensor_copy(causal_b[:, :], table("causal"))
                a, k = w_at["rot_q"], w_at["rot_k"]
                nc.vector.memset(g_sb[:, 2, 0:P], 0.0)
                link(nc.vector.memset(w_raw[:, a:n_w], 0.0))
                rq = w_raw[:, a:a + FT * P].rearrange("p (t n) -> p t n", n=P)
                sq = g_sb[:, 0, 0:FT * DR].rearrange("p (t n) -> p t n", n=DR)
                nc.vector.tensor_copy(rq[:, :, 0:DR], sq)
                nc.vector.tensor_scalar(rq[:, :, DR:DR + HALF], sq[:, :, HALF:DR], -1.0, None, ALU.mult)
                nc.vector.tensor_copy(rq[:, :, DR + HALF:2 * DR], sq[:, :, 0:HALF])
                rk = w_raw[:, k + 2 * DR:k + 4 * DR]
                sk = g_sb[:, 1, 0:DR]
                nc.vector.tensor_copy(rk[:, 0:DR], sk)
                nc.vector.tensor_scalar(rk[:, DR:DR + HALF], sk[:, HALF:DR], -1.0, None, ALU.mult)
                nc.vector.tensor_copy(g_sb[:, 2, 0:3 * DR].rearrange("p (r n) -> p r n", r=3),
                                      sk.unsqueeze(1).broadcast_to([P, 3, DR]))
                nc.vector.tensor_copy(rk[:, DR + HALF:2 * DR], sk[:, 0:HALF]).then_inc(s_weight_raw, 1)
                dve.wait_ge(s_total, 1)
                link(nc.vector.tensor_scalar(tiny[:, 2:4], bank[7][:, 0:2], 1.0 / (D * FF), 0.5,
                                             ALU.mult, ALU.mult))
                link(nc.vector.tensor_scalar(tiny[:, 4:6], tiny[:, 2:4], -1.0, None, ALU.mult))
                for n, w in enumerate((up_raw, down_raw)):
                    link(nc.vector.tensor_scalar(above, w, tiny[:, 2 + n:3 + n], None, ALU.is_gt))
                    last = nc.vector.scalar_tensor_tensor(
                        out=w, in0=w, scalar=tiny[:, 4 + n:5 + n], in1=above,
                        op0=ALU.is_lt, op1=ALU.subtract)
                    link(last)
                    nc.vector.tensor_scalar(w, w, -1.0, None, ALU.mult).then_inc(s_ternary, 1)
                for n in range(4):
                    dve.wait_ge(s_setup_hi, n + 1)
                    kt = 2 * n
                    nc.vector.tensor_tensor(
                        tok_lo[:, kt:kt + 2, :],
                        bank[n][:, :].rearrange("p (k o) -> p k o", k=2),
                        tok_hi[:, kt:kt + 2, :].bitcast(F32), ALU.subtract).then_inc(s_setup_lo, 1)
                dve.wait_ge(s_weight_hi, 1)
                nc.vector.tensor_tensor(w_lo[:, :], w_raw[:, :], w_hi[:, :].bitcast(F32),
                                        ALU.subtract).then_inc(s_weight_lo, 1)
                dve.wait_ge(s_setup_full, SETUP_UNITS)
                nc.vector.memset(q_stack[:, :, :].bitcast(F32), 0.0)
                nc.vector.memset(k_stack[:, :, :].bitcast(F32), 0.0)

                raised = [0]

                def raise_base(values):
                    for n, (value, eps) in enumerate(values):
                        last = nc.vector.tensor_scalar(base[0:1, n, 0:1], value, eps, None, ALU.add)
                    last.then_inc(s_setup_base, 1)
                    raised[0] += 1
                    dve.wait_ge(s_setup_root, raised[0])

                def norm_row(src, dst, rms):
                    link(nc.vector.bn_stats(stats[0:1, 0, :], src))
                    link(nc.vector.bn_aggr(moments[0:1, 0, :], stats[0:1, 0, :]))
                    scale = root[0:1, 0, 0:1]
                    raise_base([(moments[0:1, 0, 1:2], LN_EPS), (moments[0:1, 0, 1:2], 0.0)])
                    if rms:
                        scale = col[0:1, 0, 0:1]
                        link(nc.vector.tensor_tensor(scale, root[0:1, 0, 0:1], root[0:1, 1, 0:1], ALU.mult))
                        link(nc.vector.tensor_scalar(scale, scale, RMS_EPS, None, ALU.add))
                        link(nc.vector.reciprocal(scale, scale))
                        link(nc.vector.tensor_tensor(scale, root[0:1, 0, 0:1], scale, ALU.mult))
                    nc.vector.tensor_scalar(dst, src, moments[0:1, 0, 0:1], scale,
                                            ALU.subtract, ALU.mult).then_inc(s_cls_dve, 1)

                norm_row(row[0:1, 0, :], row[0:1, 2, :], False)
                dve.wait_ge(s_cls_pe, 1)
                nc.vector.tensor_copy(tiny[:, 8:10], bank[7][:, 8:10]).then_inc(s_cls_dve, 1)
                dve.wait_ge(s_cls_pe, 2)
                nc.vector.tensor_copy(tiny[:, 10:11], bank[7][:, 10:11]).then_inc(s_cls_dve, 1)
                dve.wait_ge(s_cls_pe, 3)
                head_of = table("head_of").rearrange("p (t n) -> p t n", t=FT)
                blk = tiny[:, 16:48].rearrange("p (t n) -> p t n", t=FT)
                nc.vector.tensor_copy(tiny[:, 11:14], bank[7][:, 11:14])
                nc.vector.tensor_copy(tiny[:, 14:16], bank[7][:, 14:16])
                link(nc.vector.tensor_copy(row[0:1, 3, :], bank[7][0:1, 256:512]))
                for t in range(FT):
                    last = nc.vector.tensor_scalar(blk[:, t, :], head_of[:, t, :],
                                                   tiny[:, 11 + t:12 + t], None, ALU.mult)
                link(last)
                link(nc.vector.tensor_copy(k0_hi[:, :, :], blk))
                nc.vector.tensor_tensor(k0_lo[:, :, :], blk, k0_hi[:, :, :].bitcast(F32), ALU.subtract)
                rope0 = tiny[0:ROPE, 13:14].broadcast_to([ROPE, H])
                link(nc.vector.tensor_copy(k0_rope[0:ROPE, :], rope0))
                nc.vector.tensor_tensor(k0_rope[2 * DR:ROPE, :], tiny[2 * DR:ROPE, 13:14].broadcast_to([DR, H]),
                                        k0_rope[2 * DR:ROPE, :].bitcast(F32),
                                        ALU.subtract).then_inc(s_cls_dve, 1)
                dve.wait_ge(s_cls_pe, 4)
                nc.vector.tensor_copy(v0_all[:, :], bank[6][:, 0:D])
                link(nc.vector.tensor_tensor(row[0:1, 1, :], bank[6][0:1, 256:512], row[0:1, 0, :],
                                             ALU.add))
                norm_row(row[0:1, 1, :], row[0:1, 2, :], True)
                dve.wait_ge(s_cls_pe, 5)
                nc.vector.tensor_copy(tiny[:, 8:10], bank[7][:, 8:10]).then_inc(s_cls_dve, 1)
                dve.wait_ge(s_cls_act, 1)
                link(nc.vector.tensor_tensor(tiny[:, 56:64], tiny[:, 48:56], tiny[:, 48:56], ALU.mult))
                nc.vector.reduce_sum(tiny[:, 0:1], tiny[:, 56:64], AX_X).then_inc(s_cls_dve, 1)
                dve.wait_ge(s_cls_pe, 7)
                link(nc.vector.tensor_scalar(tiny[0:1, 1:2], bank[7][0:1, 20:21], 1.0 / FF, None,
                                             ALU.mult))
                raise_base([(tiny[0:1, 1:2], 1.0), (tiny[0:1, 1:2], 0.0)])
                link(nc.vector.tensor_scalar(tiny[0:1, 1:2], root[0:1, 1, 0:1], RMS_EPS, None, ALU.add))
                link(nc.vector.reciprocal(tiny[0:1, 2:3], tiny[0:1, 1:2]))
                last = nc.vector.scalar_tensor_tensor(
                    out=row[0:1, 2, :], in0=bank[7][0:1, 256:512], scalar=tiny[0:1, 2:3],
                    in1=row[0:1, 1, :], op0=ALU.mult, op1=ALU.add)
                link(last)
                for _ in range(4):
                    nc.vector.engine_nop().then_inc(s_cls_dve, 1)

            @block.scalar
            def _(act):
                for n in range(SETUP_UNITS):
                    act.wait_ge(s_setup_full, n + 1)
                    if n < 4:
                        dst = tok_hi[:, 2 * n:2 * n + 2, :]
                    elif n < 8:
                        t, half = divmod(n - 4, 2)
                        dst = up_T[:, t:t + 1, 512 * half:512 * half + 512]
                    else:
                        dst = down_T[:, 2 * (n - 8):2 * (n - 8) + 2, :]
                    src = bank[n % 4][:, :].rearrange("p (k o) -> p k o", k=dst.shape[1])
                    nc.scalar.activation(dst, src, ACT.Copy).then_inc(s_setup_hi, 1)
                    if n == 3:
                        act.wait_ge(s_weight_raw, 1)
                        nc.scalar.activation(w_hi[:, :], w_raw[:, :], ACT.Copy).then_inc(s_weight_hi, 1)
                act.wait_ge(s_cls_pe, 6)
                nc.scalar.activation(tiny[:, 48:56], bank[7][:, 48:56], ACT.Gelu).then_inc(s_cls_act, 1)

            @block.tensor
            def _(pe):
                pe.wait_ge(s_weights, 16 * N_WEIGHTS)
                pe.wait_ge(s_abs, 1)
                nc.tensor.matmul(bank[7][:, 0:2], ones, tiny[:, 0:2], start=True,
                                 stop=True).then_inc(s_total, 1)
                pe.wait_ge(s_tok_prod, 1)
                for n in range(SETUP_UNITS):
                    if n >= 4:
                        pe.wait_ge(s_setup_hi, n - 3)
                    if 4 <= n < 8:
                        pe.wait_ge(s_setup_lo, n - 3)
                    if n == 4:
                        pe.wait_ge(s_ternary, 1)
                    if n == 8:
                        pe.wait_ge(s_ternary, 2)
                    for j in range(4):
                        if n < 4:
                            kt, t = 2 * n + j // 2, j % 2
                            src = tok_prod[:, t, kt * P:kt * P + P]
                        elif n < 8:
                            t, half = divmod(n - 4, 2)
                            src = up_raw[:, (4 * half + j) * D + t * P:(4 * half + j) * D + t * P + P]
                        else:
                            gt, t = 2 * (n - 8) + j // 2, j % 2
                            src = down_raw[:, t * FF + gt * P:t * FF + gt * P + P]
                        last = nc.tensor.transpose(bank[n % 4][:, j * P:j * P + P], src, ident)
                    last.then_inc(s_setup_full, 1)

                def mm(dst, pairs):
                    for n, (a, b) in enumerate(pairs):
                        last = nc.tensor.matmul(dst, a, b, start=n == 0, stop=n == len(pairs) - 1)
                    return last

                def raw(name, tile, width, first, count):
                    return weight(w_raw, name, tile, width, first, count)

                one = ones[0:1, 0:1]
                pe.wait_ge(s_weight_raw, 1)
                pe.wait_ge(s_cls_dve, 1)
                for t in range(FT):
                    last = mm(bank[7][:, 8 + t:9 + t], [(row[0:1, 2, t * P:t * P + P], one)])
                last.then_inc(s_cls_pe, 1)
                pe.wait_ge(s_cls_dve, 2)
                mm(bank[7][:, 10:11], [(raw("kv_down", t, DC, 0, DC), tiny[:, 8 + t:9 + t])
                                       for t in range(FT)]).then_inc(s_cls_pe, 1)
                pe.wait_ge(s_cls_dve, 3)
                c0 = tiny[:, 10:11]
                mm(bank[7][0:1, 256:512], [(c0, raw("v_up", 0, D, 0, D))])
                for t in range(FT):
                    mm(bank[7][:, 11 + t:12 + t], [(raw("k_up", 0, D, t * P, P), c0)])
                for t in range(FT):
                    mm(bank[7][:, 14 + t:15 + t], [(raw("v_up", 0, D, t * P, P), c0)])
                mm(bank[7][:, 13:14], [(g_sb[:, 2, 0:P], c0)]).then_inc(s_cls_pe, 1)
                pe.wait_ge(s_cls_dve, 4)
                mm(bank[6][:, 0:D], [(ones[0:1, :], row[0:1, 3, :])])
                mm(bank[6][0:1, 256:512], [(tiny[:, 14 + t:15 + t], raw("o", t, D, 0, D))
                                           for t in range(FT)]).then_inc(s_cls_pe, 1)
                pe.wait_ge(s_cls_dve, 5)
                for t in range(FT):
                    last = mm(bank[7][:, 8 + t:9 + t], [(row[0:1, 2, t * P:t * P + P], one)])
                last.then_inc(s_cls_pe, 1)
                pe.wait_ge(s_cls_dve, 6)
                pe.wait_ge(s_setup_hi, SETUP_UNITS)
                for ft in range(GT):
                    last = mm(bank[7][:, 48 + ft:49 + ft],
                              [(up_T[:, t, ft * P:ft * P + P].bitcast(F32), tiny[:, 8 + t:9 + t])
                               for t in range(FT)])
                last.then_inc(s_cls_pe, 1)
                pe.wait_ge(s_cls_dve, 7)
                pe.wait_ge(s_cls_act, 1)
                mm(bank[7][0:1, 20:21], [(tiny[:, 0:1], ones[:, 0:1])])
                mm(bank[7][0:1, 256:512], [(tiny[:, 48 + ft:49 + ft], down_T[:, ft, :].bitcast(F32))
                                           for ft in range(GT)]).then_inc(s_cls_pe, 1)

        with nc.Fori(0, B) as b:
            with nc.Block() as block:

                def full(unit):
                    return filled[bank_of[unit]], fill_of[unit]

                def read(unit):
                    return drained[bank_of[unit]], read_of[unit]

                @block.sync
                def _(sp):
                    sp.wait_ge(*full(("xT", KT - 1)))
                    sp.dma_start(x_in[:, :, :], x_tiles[bass.ds((b + 1) % B, 1)]
                                 .rearrange("b p i n -> p (b i) n")).then_inc(s_x, 16)
                    for w, name in ((0, "q"), (1, "k")):
                        for t in range(FT):
                            sp.wait_ge(*read((name, t)))
                        sp.dma_start(scratch[w].rearrange("a t p n -> p (a t) n"),
                                     qk[:, w].bitcast(F32).rearrange("p a t n -> p (a t) n")
                                     ).then_inc(s_scratch, 16)
                    sp.wait_ge(s_scratch, 32)
                    for g in range(NG):
                        if g >= 2:
                            sp.wait_ge(*full(("s", GH * (g - 1) - 1, 2)))
                        t, first = divmod(g * GH * HD, P)
                        for w, stack, halves in ((0, q_stack, (0, 1, 0)), (1, k_stack, (0, 0, 1))):
                            for r, half in enumerate(halves):
                                sp.dma_start(
                                    stack[r * HD:(r + 1) * HD, (g % 2) * GH:(g % 2 + 1) * GH, :].bitcast(F32),
                                    scratch[w, half, t, first:first + GH * HD, :]
                                    .rearrange("(j p) n -> p j n", p=HD)).then_inc(s_stack[g % 2], 16)
                    for i in range(TT):
                        sp.wait_ge(s_out, i + 1)
                        sp.dma_start(out_tiles[bass.ds(b, 1), :, i, :].rearrange("b p n -> p (b n)"),
                                     out_sb[:, i, :]).then_inc(s_stored, 16)

                @block.gpsimd
                def _(pool):
                    def raise_base(count):
                        pool.wait_ge(s_base, count)
                        nc.gpsimd.tensor_tensor(root[:, :, :], base[:, :, :], powers,
                                                ALU.pow).then_inc(s_root, 1)

                    raise_base(1)
                    pool.wait_ge(s_p0, 1)
                    for i in range(TT):
                        nc.gpsimd.tensor_tensor(
                            p0_v0[:, i, :].rearrange("p (n d) -> p n d", d=HD),
                            v0_all[:, :].rearrange("p (n d) -> p n d", d=HD),
                            p0[:, i, :].unsqueeze(2).broadcast_to([P, H, HD]),
                            ALU.mult).then_inc(s_p0v0, 1)
                    raise_base(2)
                    for ft in range(GT):
                        pool.wait_ge(s_gelu, ft + 1)
                        if ft >= GRING:
                            pool.wait_ge(s_g_acc, ft - GRING + 1)
                        slot = ft % GRING
                        nc.gpsimd.tensor_tensor(g_sq[:, slot, :], g_sb[:, slot, :], g_sb[:, slot, :],
                                                ALU.mult).then_inc(s_g_sq, 1)
                    raise_base(3)

                @block.scalar
                def _(act):
                    def copy(dst, src):
                        return nc.scalar.activation(dst, src, ACT.Copy)

                    for kt in range(KT):
                        act.wait_ge(*full(("xT", kt)))
                        if kt >= XRING:
                            act.wait_ge(s_tok_used, kt - XRING + 1)
                        copy(xT_hi[:, kt % XRING, :], bank[kt % 2][:, :]).then_inc(s_xT_hi, 1)
                    for i in range(TT):
                        act.wait_ge(*full(("h", i)))
                        copy(h[:, i, :], bank[2 + i][:, 0:D]).then_inc(drained[2 + i], 1)

                    def features_hi(stage):
                        for f in range(FT):
                            act.wait_ge(*full(("fT", stage, f)))
                            copy(fT_hi[:, f, :], bank[f][:, :]).then_inc(s_fT_hi, 1)

                    features_hi(0)
                    act.wait_ge(*full(("c",)))
                    copy(cT_hi[:, :], bank[6][:, :]).then_inc(s_half, 1)
                    for w, name in ((0, "q"), (1, "k")):
                        for t in range(FT):
                            act.wait_ge(*full((name, t)))
                            copy(qk[:, w, 0, t, :], bank[bank_of[(name, t)]][:, :]).then_inc(s_half, 1)
                    for u in range(2):
                        act.wait_ge(*full(("v", u)))
                        for i in range(2):
                            last = copy(v[:, 2 * u + i, :, 0:HD],
                                        bank[u][:, i * D:i * D + D].rearrange("p (n d) -> p n d", d=HD))
                        last.then_inc(drained[u], 1)
                    for name, dst in (("rope_q", rope_q), ("rope_k", rope_k)):
                        act.wait_ge(*full((name,)))
                        copy(dst[0:ROPE, :], bank[bank_of[(name,)]][0:ROPE, :]).then_inc(s_half, 1)

                    for step in range(H + 3):
                        hd = step
                        if hd < H:
                            act.wait_ge(s_shift, hd + 1)
                            if hd >= 2:
                                act.wait_ge(*full(("pT", hd - 2, 2)))
                            for i in S_ORDER:
                                u, c = S_AT[i]
                                n = P * (i + 1)
                                src = bank[bank_of[("s", hd, u)]]
                                last = nc.scalar.activation(
                                    probs[:, hd % 2, 512 * u + c:512 * u + c + n], src[:, c:c + n],
                                    ACT.Exp, bias=shift[:, hd, i:i + 1], scale=SCALE)
                                if i != 0:
                                    last.then_inc(drained[bank_of[("s", hd, u)]], 1)
                        hd = step - 1
                        if 0 <= hd < H:
                            act.wait_ge(*full(("pT", hd, 2)))
                            if hd >= 2:
                                act.wait_ge(s_pv, hd - 1)
                            copy(probs_T[:, hd % 2, 1024:PW],
                                 bank[6][:, 0:256]).then_inc(drained[6], 1)
                        hd = step - 3
                        if hd >= 0 and hd % GH == GH - 1:
                            act.wait_ge(s_pv, hd + 1)
                            copy(oT[:, hd // GH, :], bank[7][:, :]).then_inc(drained[7], 1)
                    act.wait_ge(s_p0_in, 1)
                    nc.scalar.activation(p0[:, :, :], denom[:, :, :], ACT.Exp).then_inc(s_p0, 1)
                    features_hi(1)
                    features_hi(2)
                    for ft in range(GT):
                        act.wait_ge(*full(("g", ft)))
                        if ft >= GRING:
                            act.wait_ge(s_g_split, ft - GRING + 1)
                            act.wait_ge(s_g_sq, ft - GRING + 1)
                        nc.scalar.activation(g_sb[:, ft % GRING, :], bank[6 + ft % 2][:, :],
                                             ACT.Gelu).then_inc(s_gelu, 1)

                @block.vector
                def _(dve):
                    steps = [0]

                    def link(ins):
                        steps[0] += 1
                        ins.then_inc(s_dve, 1)
                        dve.wait_ge(s_dve, steps[0])

                    def low(dst, src, hi):
                        return nc.vector.tensor_tensor(dst, src, hi.bitcast(F32), ALU.subtract)

                    for kt in range(KT):
                        dve.wait_ge(s_xT_hi, kt + 1)
                        slot = kt % XRING
                        low(xT_lo[:, slot, :], bank[kt % 2][:, :],
                            xT_hi[:, slot, :]).then_inc(drained[kt % 2], 1)

                    def norm(i, scale):
                        nc.vector.tensor_scalar(xn[:, i, :], h[:, i, :], moments[:, i, 0:1],
                                                scale[:, i:i + 1], ALU.subtract,
                                                ALU.mult).then_inc(s_xn, 1)

                    for i in range(TT):
                        dve.wait_ge(*read(("h", i)))
                        last = nc.vector.bn_stats(stats[:, i, :], h[:, i, :])
                    link(last)
                    for i in range(TT):
                        last = nc.vector.bn_aggr(moments[:, i, :], stats[:, i, :])
                    link(last)
                    rstd = root[:, 0, :]

                    def raise_base(values, count):
                        for n, (value, scale, eps) in enumerate(values):
                            last = nc.vector.tensor_scalar(base[:, n, :], value, scale, eps,
                                                           ALU.mult, ALU.add)
                        last.then_inc(s_base, 1)
                        dve.wait_ge(s_root, count)

                    var = moments[:, :, 1]
                    raise_base([(var, 1.0, LN_EPS), (var, 1.0, 0.0)], 1)
                    for i in range(TT):
                        norm(i, rstd)

                    def features_lo(stage):
                        for f in range(FT):
                            dve.wait_ge(s_fT_hi, FT * stage + f + 1)
                            low(fT_lo[:, f, :], bank[f][:, :], fT_hi[:, f, :]).then_inc(drained[f], 1)

                    features_lo(0)
                    dve.wait_ge(s_half, 1)
                    low(cT_lo[:, :], bank[6][:, :], cT_hi[:, :]).then_inc(drained[6], 1)
                    done = 1
                    for w, name in ((0, "q"), (1, "k")):
                        for t in range(FT):
                            done += 1
                            dve.wait_ge(s_half, done)
                            n = bank_of[(name, t)]
                            low(qk[:, w, 1, t, :], bank[n][:, :], qk[:, w, 0, t, :]).then_inc(drained[n], 1)
                    dve.wait_ge(*full(("rot",)))
                    nc.vector.tensor_tensor(prod[:, :], bank[7][:, :], table("rope"),
                                            ALU.mult).then_inc(drained[7], 1)
                    for name, dst, rows in (("rope_q", rope_q, slice(DR, 2 * DR)),
                                            ("rope_k", rope_k, slice(2 * DR, 3 * DR))):
                        done += 1
                        dve.wait_ge(s_half, done)
                        n = bank_of[(name,)]
                        low(dst[rows, :], bank[n][rows, :], dst[rows, :]).then_inc(drained[n], 1)
                    dve.wait_ge(*full(("s0",)))
                    nc.vector.tensor_scalar(neg_s0[:, :, :],
                                            bank[2][:, 0:TT * H].rearrange("p (i n) -> p i n", n=H),
                                            -SCALE, None, ALU.mult).then_inc(drained[2], 1)
                    for step in range(H + 1):
                        hd = step
                        if hd < H:
                            for i in S_ORDER:
                                u, c = S_AT[i]
                                dve.wait_ge(*full(("s", hd, u)))
                                src = bank[bank_of[("s", hd, u)]]
                                last = nc.vector.reduce_max(row_max[:, hd, i:i + 1],
                                                            src[:, c:c + P * (i + 1)], AX_X)
                            link(last)
                            nc.vector.scalar_tensor_tensor(
                                out=shift[:, hd, :], in0=row_max[:, hd, :], scalar=-SCALE,
                                in1=neg_s0[:, :, hd], op0=ALU.mult, op1=ALU.min).then_inc(s_shift, 1)
                        hd = step - 1
                        if hd >= 0:
                            if hd >= 2:
                                dve.wait_ge(s_pv, hd - 1)
                            for u in range(2):
                                dve.wait_ge(*full(("pT", hd, u)))
                                nc.vector.tensor_copy(probs_T[:, hd % 2, 512 * u:512 * u + 512],
                                                      bank[u][:, :]).then_inc(drained[u], 1)
                    nc.vector.tensor_tensor(denom[:, :, :], neg_s0[:, :, :],
                                            shift[:, :, :].rearrange("p n i -> p i n"),
                                            ALU.subtract)
                    link(nc.vector.engine_nop())
                    link(nc.vector.tensor_scalar(denom[:, :, :], denom[:, :, :], -1.0, None, ALU.mult))
                    nc.vector.engine_nop().then_inc(s_p0_in, 1)
                    dve.wait_ge(s_p0, 1)
                    for i in range(TT):
                        dve.wait_ge(*full(("oTok", i)))
                        o = bank[2 + i][:, :].rearrange("p (n d) -> p n d", d=VW)
                        last = nc.vector.tensor_tensor(denom[:, i, :], o[:, :, HD], p0[:, i, :], ALU.add)
                        link(last)
                        nc.vector.reciprocal(recip[:, i, :], denom[:, i, :])
                        dve.wait_ge(s_p0v0, i + 1)
                        a = xn[:, i, :].rearrange("p (n d) -> p n d", d=HD)
                        w = out_sb[:, i, :].rearrange("p (n d) -> p n d", d=HD)
                        if i == 0:
                            dve.wait_ge(s_stored, 16 * TT * b + 16 * B)
                        steps[0] += 1
                        nc.vector.tensor_tensor(
                            w, o[:, :, 0:HD], p0_v0[:, i, :].rearrange("p (n d) -> p n d", d=HD),
                            ALU.add).then_inc(drained[2 + i], 1)
                        dve.wait_ge(*read(("oTok", i)))
                        steps[0] -= 1
                        nc.vector.tensor_tensor(a, w, recip[:, i, :].unsqueeze(2).broadcast_to([P, H, HD]),
                                                ALU.mult).then_inc(s_xn, 1)
                    features_lo(1)
                    for i in range(TT):
                        dve.wait_ge(*full(("y", i)))
                        nc.vector.tensor_tensor(h[:, i, :], bank[2 + i][:, 0:D], h[:, i, :],
                                                ALU.add).then_inc(drained[2 + i], 1)
                        dve.wait_ge(*read(("y", i)))
                        last = nc.vector.bn_stats(stats[:, i, :], h[:, i, :])
                    link(last)
                    for i in range(TT):
                        last = nc.vector.bn_aggr(moments[:, i, :], stats[:, i, :])
                    link(last)
                    rms, scale2 = col[:, 1, :], col[:, 2, :]
                    raise_base([(var, 1.0, LN_EPS), (var, 1.0, 0.0)], 2)
                    link(nc.vector.tensor_tensor(rms, rstd, root[:, 1, :], ALU.mult))
                    link(nc.vector.tensor_scalar(rms, rms, RMS_EPS, None, ALU.add))
                    link(nc.vector.reciprocal(rms, rms))
                    link(nc.vector.tensor_tensor(scale2, rstd, rms, ALU.mult))
                    for i in range(TT):
                        norm(i, scale2)
                    features_lo(2)
                    for ft in range(GT):
                        slot = ft % GRING
                        dve.wait_ge(s_gelu, ft + 1)
                        if ft >= GRING:
                            dve.wait_ge(s_down, ft - GRING + 1)
                        link(nc.vector.tensor_copy(g_hi[:, slot, :], g_sb[:, slot, :]))
                        low(g_lo[:, slot, :], g_sb[:, slot, :], g_hi[:, slot, :]).then_inc(s_g_split, 1)
                        dve.wait_ge(s_g_sq, ft + 1)
                        if ft == 0:
                            nc.vector.tensor_copy(g_acc[:, :], g_sq[:, slot, :]).then_inc(s_g_acc, 1)
                        else:
                            dve.wait_ge(s_g_acc, ft)
                            nc.vector.tensor_tensor(g_acc[:, :], g_acc[:, :], g_sq[:, slot, :],
                                                    ALU.add).then_inc(s_g_acc, 1)
                    dve.wait_ge(*full(("ss",)))
                    rms, scale3 = col[:, 3, :], col[:, 4, :]
                    raise_base([(bank[0][:, 0:TT], 1.0, 1.0), (bank[0][:, 0:TT], 1.0 / FF, 0.0)], 3)
                    link(nc.vector.tensor_scalar(rms, root[:, 1, :], RMS_EPS, None, ALU.add))
                    link(nc.vector.reciprocal(scale3, rms))
                    for i in range(TT):
                        dve.wait_ge(*full(("d", i)))
                        nc.vector.scalar_tensor_tensor(
                            out=out_sb[:, i, :], in0=bank[2 + i][:, 0:D], scalar=scale3[:, i:i + 1],
                            in1=h[:, i, :], op0=ALU.mult, op1=ALU.add).then_inc(s_out, 1)

                @block.tensor
                def _(pe):
                    def claim(unit):
                        if before[unit] > 0:
                            pe.wait_ge(drained[bank_of[unit]], before[unit])
                        return bank[bank_of[unit]]

                    def product(dst, pairs):
                        for n, (lhsT, rhs) in enumerate(pairs):
                            last = nc.tensor.matmul(dst, lhsT, rhs, start=n == 0,
                                                    stop=n == len(pairs) - 1)
                        return last

                    def transpose_x(kt):
                        dst = claim(("xT", kt))
                        for i in range(TT):
                            last = nc.tensor.transpose(dst[:, i * P:i * P + P],
                                                       x_in[:, i, kt * P:kt * P + P], ident)
                        last.then_inc(filled[kt % 2], 1)

                    pe.wait_ge(s_x, 16 * (b + 1))
                    transpose_x(0)
                    for i in range(TT):
                        claim(("h", i))
                    for kt in range(KT):
                        if kt + 1 < KT:
                            transpose_x(kt + 1)
                        pe.wait_ge(*read(("xT", kt)))
                        slot = kt % XRING
                        for i in range(TT):
                            cols = slice(i * P, i * P + P)
                            for n, (data, w) in enumerate(((xT_hi, tok_hi), (xT_hi, tok_lo), (xT_lo, tok_hi))):
                                last = nc.tensor.matmul(bank[2 + i][:, 0:D], data[:, slot, cols],
                                                        w[:, kt, :], start=kt == 0 and n == 0,
                                                        stop=kt == KT - 1 and n == 2)
                            if kt == KT - 1:
                                last.then_inc(filled[2 + i], 1)
                            elif i == TT - 1:
                                last.then_inc(s_tok_used, 1)

                    def transpose_features(stage):
                        for f in range(FT):
                            claim(("fT", stage, f))
                        for i in range(TT):
                            pe.wait_ge(s_xn, TT * stage + i + 1)
                            for f in range(FT):
                                last = nc.tensor.transpose(bank[f][:, i * P:i * P + P],
                                                           xn[:, i, f * P:f * P + P], ident)
                                if i == TT - 1:
                                    last.then_inc(filled[f], 1)
                        for f in range(FT):
                            pe.wait_ge(*read(("fT", stage, f)))

                    fT = (fT_hi, fT_lo)
                    cT = (cT_hi, cT_lo)

                    def from_features(name, width, first):
                        return [(weight(w_half[a], name, f, width, first, P), fT[c][:, f, :])
                                for f in range(FT) for a, c in HALVES]

                    def from_latent(name, first):
                        return [(weight(w_half[a], name, 0, 0, first, P), cT[c][:, :]) for a, c in HALVES]

                    transpose_features(0)
                    product(claim(("c",))[:, :], from_features("kv_down", DC, 0)).then_inc(filled[6], 1)
                    for t in range(FT):
                        product(claim(("q", t))[:, :], from_features("q", D, t * P)).then_inc(filled[2 + t], 1)
                    pe.wait_ge(*read(("c",)))
                    for t in range(FT):
                        product(claim(("k", t))[:, :], from_latent("k_up", t * P)).then_inc(filled[4 + t], 1)
                    product(claim(("rot",))[:, :],
                            from_features("rot_q", P, 0) + from_latent("rot_k", 0)).then_inc(filled[7], 1)
                    for u in range(2):
                        dst = claim(("v", u))
                        for i in range(2):
                            cols = slice((2 * u + i) * P, (2 * u + i + 1) * P)
                            last = product(dst[:, i * D:i * D + D],
                                           [(cT[c][:, cols], weight(w_half[a], "v_up", 0, 0, 0, D))
                                            for a, c in HALVES])
                        last.then_inc(filled[u], 1)
                    claim(("rope_q",))
                    claim(("rope_k",))
                    product(bank[6][0:ROPE, :], [(table("fold_q"), prod[:, :])]).then_inc(filled[6], 1)
                    product(bank[7][0:ROPE, :], [(table("fold_k"), prod[:, :])]).then_inc(filled[7], 1)
                    dst = claim(("s0",))
                    for t in range(FT):
                        pe.wait_ge(*read(("q", t)))
                    pe.wait_ge(*read(("rope_q",)))
                    for i in range(TT):
                        cols = slice(i * P, i * P + P)
                        last = product(dst[:, i * H:i * H + H],
                                       [(qk[:, 0, c, t, cols], (k0_hi, k0_lo)[a][:, t, :])
                                        for t in range(FT) for a, c in HALVES]
                                       + [(rope_q[0:ROPE, cols], k0_rope[0:ROPE, :])])
                    last.then_inc(filled[2], 1)

                    def scores(hd):
                        g = hd // GH
                        slot = (g % 2) * GH + hd % GH
                        if hd % GH == 0:
                            pe.wait_ge(s_stack[g % 2], 16 * 6 * (g // 2 + 1))
                        for u in range(3):
                            dst = claim(("s", hd, u))
                            for i in (i for i in S_ORDER if S_AT[i][0] == u):
                                c, n = S_AT[i][1], P * (i + 1)
                                cols = slice(i * P, i * P + P)
                                nc.tensor.matmul(dst[:, c:c + n], q_stack[0:ROWS, slot, cols],
                                                 k_stack[0:ROWS, slot, 0:n], start=True, stop=False)
                                nc.tensor.matmul(dst[:, c:c + n], rope_q[0:ROPE, cols],
                                                 rope_k[0:ROPE, 0:n], start=False, stop=False)
                                last = nc.tensor.matmul(dst[:, c + n - P:c + n], ident_b[:, :],
                                                        causal_b[:, :], start=False, stop=True)
                            last.then_inc(filled[bank_of[("s", hd, u)]], 1)

                    def transpose_probs(hd):
                        for u in range(3):
                            pe.wait_ge(*read(("s", hd, u)))
                        for u in range(3):
                            dst = claim(("pT", hd, u))
                            for j in (j for j in (0, 1, 3, 2) if PT_AT[j][0] == u):
                                for i in range(j, TT):
                                    su, sc = S_AT[i]
                                    src = 512 * su + sc + j * P
                                    c = PT_AT[j][1] + (i - j) * P
                                    last = nc.tensor.transpose(dst[:, c:c + P],
                                                               probs[:, hd % 2, src:src + P], ident)
                            last.then_inc(filled[bank_of[("pT", hd, u)]], 1)

                    def sum_values(hd):
                        for u in range(3):
                            pe.wait_ge(*read(("pT", hd, u)))
                        if hd % GH == 0:
                            claim(("o", hd // GH))
                        r = VW * (hd % GH)
                        for j in range(TT):
                            u, c = PT_AT[j]
                            n = T - j * P
                            last = nc.tensor.matmul(bank[7][r:r + VW, j * P:T], v[:, j, hd, :],
                                                    probs_T[:, hd % 2, 512 * u + c:512 * u + c + n],
                                                    start=j == 0, stop=j == TT - 1)
                        last.then_inc(s_pv, 1)

                    for u in range(2):
                        pe.wait_ge(*read(("v", u)))
                    pe.wait_ge(*read(("rope_k",)))
                    for step in range(H + 2):
                        if step < H:
                            scores(step)
                        if 1 <= step <= H:
                            transpose_probs(step - 1)
                        if step >= 2:
                            sum_values(step - 2)

                    pe.wait_ge(*read(("o", NG - 1)))
                    for i in range(TT):
                        dst = claim(("oTok", i))
                        for g in range(NG):
                            last = nc.tensor.transpose(dst[:, g * P:g * P + P],
                                                       oT[:, g, i * P:i * P + P], ident)
                        last.then_inc(filled[2 + i], 1)
                    transpose_features(1)
                    for i in range(TT):
                        cols = slice(i * P, i * P + P)
                        product(claim(("y", i))[:, 0:D],
                                [(fT[c][:, f, cols], weight(w_half[a], "o", f, D, 0, D))
                                 for f in range(FT) for a, c in HALVES]).then_inc(filled[2 + i], 1)
                    transpose_features(2)

                    def up(ft):
                        product(claim(("g", ft))[:, :],
                                [(up_T[:, f, ft * P:ft * P + P], fT[c][:, f, :])
                                 for f in range(FT) for c in range(2)]).then_inc(filled[6 + ft % 2], 1)

                    up(0)
                    for i in range(TT):
                        claim(("d", i))
                    for ft in range(GT):
                        if ft + 1 < GT:
                            if ft + 1 >= 2:
                                pe.wait_ge(s_gelu, ft)
                            up(ft + 1)
                        pe.wait_ge(s_g_split, ft + 1)
                        slot = ft % GRING
                        for i in range(TT):
                            cols = slice(i * P, i * P + P)
                            for n, data in enumerate((g_hi, g_lo)):
                                last = nc.tensor.matmul(bank[2 + i][:, 0:D], data[:, slot, cols],
                                                        down_T[:, ft, :], start=ft == 0 and n == 0,
                                                        stop=ft == GT - 1 and n == 1)
                            if ft == GT - 1:
                                last.then_inc(filled[2 + i], 1)
                            elif i == TT - 1:
                                last.then_inc(s_down, 1)
                    pe.wait_ge(s_g_acc, GT)
                    dst = claim(("ss",))
                    for i in range(TT):
                        last = product(dst[:, i:i + 1], [(g_acc[:, i * P:i * P + P], ones[:, 0:1])])
                    last.then_inc(filled[0], 1)

            nc.all_engine_barrier(sems_to_clear=range(numbers[0], numbers[-1] + 1))
        nc.sync.wait_ge(s_stored, 16 * TT * B + 16 * B)
        nc.sync.wait_ge(s_x, 16 * (B + 1))


_INS = ["x", "cls_tok", "L0_tok_weight", "L0_tok_weighted_sum", "L0_attn_W_kv_down", "L0_attn_W_k_up",
        "L0_attn_W_v_up", "L0_attn_W_q", "L0_attn_W_q_rope", "L0_attn_W_k_rope", "L0_attn_W_o",
        "L0_ffn_w_up", "L0_ffn_w_down"]


def shape_constants(head_count, tokens, head_dim, rope_dim):
    import numpy as np

    at, width = constant_layout(head_count, tokens)
    c = np.zeros((P, width), np.float32)

    def put(name, value):
        first, n = at[name]
        c[:value.shape[0], first:first + n] = value

    r = np.arange(P)
    put("identity", np.eye(P, dtype=np.float32))
    put("causal", np.where(r[None, :] > r[:, None], np.float32(MASKED), np.float32(0)))
    for name, base in (("fold_q", 0), ("fold_k", 2 * rope_dim)):
        m = np.zeros((P, 3 * rope_dim), np.float32)
        for j in range(3 * rope_dim):
            m[base + j % rope_dim, j] = 1
            m[base + rope_dim + j % rope_dim, j] = 1
        put(name, m)
    head_of = np.zeros((P, 2, head_count), np.float32)
    for t in range(2):
        head_of[r, t, (t * P + r) // head_dim] = 1
    put("head_of", head_of.reshape(P, -1))
    put("powers", np.tile(np.repeat(np.float32([-0.5, 0.5]), 4), (P, 1)))
    put("ones", np.ones((P, P), np.float32))
    inv_freq = np.float32(1.0) / np.float32(10000.0) ** (
        np.arange(0, rope_dim, 2, dtype=np.float32) / np.float32(rope_dim))
    angles = np.outer(inv_freq, np.arange(1, tokens + 1, dtype=np.float32)).astype(np.float32)
    cos, sin = np.cos(angles), np.sin(angles)
    put("rope", np.concatenate([cos, cos, sin, sin] * 2, axis=0))
    return c


def kernel(**inputs):
    import numpy as np
    import concourse.bacc as bacc
    from concourse.bass_utils import run_bass_kernel_spmd as run

    nc = bacc.Bacc("TRN2", target_bir_lowering=False, num_devices=1)
    arrays, args = {}, []
    for name in _INS:
        a = np.ascontiguousarray(inputs[name])
        arrays[f"in_{name}"] = a
        args.append(nc.dram_tensor(f"in_{name}", a.shape, mybir.dt.from_np(a.dtype), kind="ExternalInput").ap())
    batch, tokens, dim, _ = inputs["x"].shape
    heads = 16
    c = shape_constants(heads, tokens, dim // heads, inputs["L0_attn_W_q_rope"].shape[1])
    arrays["in_constants"] = c
    args.append(nc.dram_tensor("in_constants", c.shape, F32, kind="ExternalInput").ap())
    args.append(nc.dram_tensor("out_0", (batch, tokens + 1, dim), F32, kind="ExternalOutput").ap())
    vit_tower_kernel(nc, *args)
    r = run(nc, [arrays], core_ids=[0])
    return r.results[0]["out_0"]
```

```python
from contextlib import ExitStack

import concourse.bass as bass
from concourse import mybir

F32 = mybir.dt.float32
F32R = mybir.dt.float32r
BF16 = mybir.dt.bfloat16
ALU = mybir.AluOpType
ACT = mybir.ActivationFunctionType
AX_X = mybir.AxisListType.X

P = 128
LN_EPS = 1e-5
RMS_EPS = 1e-8
MASKED = -1e30


def constant_layout(head_count, tokens):
    widths = {"identity": P, "causal": P, "fold": 64, "select": 2, "head_of": 2 * head_count,
              "ones": P, "powers": 8, "rope": tokens}
    at, first = {}, 0
    for name, width in widths.items():
        at[name] = (first, width)
        first += width
    return at, first


def vit_tower_kernel(nc, x, cls_tok, tok_weight, tok_sum, w_kv_down, w_k_up, w_v_up, w_q,
                     w_q_rope, w_k_rope, w_o, w_ffn_up, w_ffn_down, constants, out):
    B, T, _, DIN = x.shape
    D = cls_tok.shape[2]
    DC = w_kv_down.shape[1]
    DR = w_q_rope.shape[1]
    FF = w_ffn_up.shape[0]
    H = 16
    HD = D // H
    TT = T // P
    FT = D // P
    KT = D * DIN // P
    GT = FF // P
    HALF = DR // 2
    GH = 4
    NG = H // GH
    SCALE = float(HD + DR) ** -0.5
    CONTENT = 3 * HD
    ROWS = CONTENT + DR
    CROSS = 2 * DR + 2
    LAG = 3
    VW = HD + 1
    OW = 32
    RING = 2
    at, n_const = constant_layout(H, T)

    PAIRS = TT // 2
    XU = KT // 2
    GU = GT // 2

    S_AT = {0: (0, 0), 2: (0, P), 3: (1, 0), 1: (2, 0)}
    PT_AT = {0: (0, 0), 1: (1, 0), 3: (1, 3 * P), 2: (2, 0)}
    S_ORDER = (0, 2, 3, 1)
    PT_UNITS = (512, 512, 256)
    PW = sum(PT_UNITS)

    ctx = ExitStack()
    with ctx:
        def sb(name, shape, dt=F32):
            return ctx.enter_context(nc.sbuf_tensor(name, shape, dt))

        def sem(name):
            return ctx.enter_context(nc.semaphore(name))

        bank = [ctx.enter_context(nc.psum_tensor(f"bank{n}", [P, 512], F32)) for n in range(8)]

        const = sb("const", [P, n_const])

        def table(name):
            first, width = at[name]
            return const[:, first:first + width]

        ident = table("identity")
        ones = table("ones")
        powers = table("powers").rearrange("p (k i) -> p k i", k=2)
        ident_b = sb("ident_b", [P, P], BF16)
        causal_b = sb("causal_b", [P, P], BF16)
        tok_hi = sb("tok_hi", [P, KT, D], F32R)
        tok_lo = sb("tok_lo", [P, KT, D], F32R)
        widths = {"kv_down": FT * DC, "k_up": D, "v_up": D, "q": FT * D, "o": FT * D,
                  "rot_q": FT * P, "rot_k": P}
        w_at, n_w = {}, 0
        for name, width in widths.items():
            w_at[name] = n_w
            n_w += width
        w_hi = sb("w_hi", [P, n_w], F32R)
        w_lo = sb("w_lo", [P, n_w], F32R)
        up_T = sb("up_T", [P, FT, FF], F32R)
        down_T = sb("down_T", [P, GT, D], F32R)
        k0_hi = sb("k0_hi", [P, FT, H], F32R)
        k0_lo = sb("k0_lo", [P, FT, H], F32R)
        k0_rope = sb("k0_rope", [P, H])
        v0_all = sb("v0_all", [P, D])

        def weight(half, name, tile, width, first, count):
            a = w_at[name] + tile * width + first
            return half[:, a:a + count]

        x_in = sb("x_in", [P, TT, D * DIN])
        xT_hi = sb("xT_hi", [P, RING, T], F32R)
        xT_lo = sb("xT_lo", [P, RING, T], F32R)
        h = sb("h", [P, 2, TT, D])
        h_next = sb("h_next", [P, TT, D])
        xn = sb("xn", [P, TT, D])
        xn_next = sb("xn_next", [P, TT, D])
        fT_hi = sb("fT_hi", [P, FT, T], F32R)
        fT_lo = sb("fT_lo", [P, FT, T], F32R)
        latent = sb("latent", [P, 2, T], F32R)
        cT_hi, cT_lo = latent[:, 0, :], latent[:, 1, :]
        qk = sb("qk", [P, 2, 2, FT, T], F32R)
        q_stack = sb("q_stack", [P, 2 * GH, T], F32R)
        k_stack = sb("k_stack", [P, 2 * GH, T], F32R)
        prod = sb("prod", [P, T])
        rope = sb("rope", [2 * DR, 2, T], F32R)
        q_cross = sb("q_cross", [P, 2, T], F32R)
        k_cross = sb("k_cross", [P, 2, T], F32R)
        v = sb("v", [P, 2, TT, H * VW + OW - VW])
        probs_T = sb("probs_T", [P, 2, PW])
        oT = sb("oT", [P, NG, T])
        g_sb = sb("g_sb", [P, RING, T])
        g_sq = sb("g_sq", [P, T])
        g_halves = qk[:, :, :, :, :].rearrange("p w a t n -> p (w a t) n")
        g_hi = g_halves[:, 0:RING, :]
        g_lo = g_halves[:, RING:2 * RING, :]
        g_acc = prod
        stats = sb("stats", [P, TT, 6])
        moments = sb("moments", [P, TT, 2])
        stats_next = sb("stats_next", [P, TT, 6])
        moments_next = sb("moments_next", [P, TT, 2])
        col = sb("col", [P, 2, TT])
        base = sb("base", [P, 2, TT])
        root = sb("root", [P, 2, TT])
        base_next = sb("base_next", [P, 1, TT])
        root_next = sb("root_next", [P, 1, TT])
        neg_s0 = sb("neg_s0", [P, 2, TT, H])
        row_max = sb("row_max", [P, 2, TT])
        shift = sb("shift", [P, TT, H], F32R)
        p0 = sb("p0", [P, TT, H])
        p0_v0 = g_sb[:, :, :].rearrange("p s n -> p (s n)").rearrange("p (i n) -> p i n", n=D)
        denom = sb("denom", [P, TT, H])
        recip = sb("recip", [P, TT, H])

        x_sum = h[:, 0].rearrange("p i n -> p (i n)")[:, 0:FT * D] \
            .rearrange("p (t i) -> p t i", t=FT)
        x_wt = col[:, :, :]
        x_flat = x_in[:, :, :].rearrange("p i n -> p (i n)")
        tok_prod = x_flat[:, 0:FT * D * DIN].rearrange("p (t n) -> p t n", t=FT)
        down_raw = x_flat[:, FT * D * DIN:FT * D * DIN + FT * FF]
        up_raw = probs_T[:, :, :].rearrange("p s n -> p (s n)")[:, 0:GT * D]
        above = oT[:, :, :].rearrange("p g n -> p (g n)")
        w_raw = v[:, :, :, :].rearrange("p b i n -> p (b i n)")[:, 0:n_w]
        row = xn
        w_rope_raw = g_sb[:, 0, 0:FT * DR].rearrange("p (t n) -> p t n", n=DR)
        w_rope_k_raw = g_sb[:, 1, 0:DR]
        k_rope_twice = g_sq[:, 0:P]
        tiny = denom[:, :, :].rearrange("p i n -> p (i n)")

        scratch = nc.dram_tensor("qk_scratch", [2, 2, FT, P, T], F32, kind="Internal").ap()
        rope_scratch = nc.dram_tensor("rope_scratch", [2, DR, 2, T], F32, kind="Internal").ap()

        s_weights = sem("weights_loaded")
        s_x = sem("x_loaded")
        s_stored = sem("rows_stored")
        s_tok_prod = sem("tok_product_ready")
        s_abs = sem("abs_sums_ready")
        s_total = sem("abs_total_ready")
        s_ternary = sem("ternary_ready")
        s_setup_full = sem("setup_bank_filled")
        s_setup_hi = sem("setup_bank_copied")
        s_setup_lo = sem("setup_low_half_ready")
        s_weight_raw = sem("rotary_weights_ready")
        s_weight_hi = sem("weight_hi_ready")
        s_weight_lo = sem("weight_lo_ready")
        s_setup_dve = sem("setup_vector_step")
        s_setup_base = sem("setup_power_base_ready")
        s_setup_root = sem("setup_power_ready")
        s_cls_pe = sem("cls_product_ready")
        s_cls_dve = sem("cls_operand_ready")
        s_cls_act = sem("cls_gelu_ready")

        filled = [sem(f"bank{n}_filled") for n in range(8)]
        drained = [sem(f"bank{n}_drained") for n in range(8)]
        s_xT_hi = sem("xT_hi_ready")
        s_tok_used = sem("xT_used")
        s_xn_a = sem("normed_tokens_ready")
        s_xn_b = sem("normed_attention_ready")
        s_fT_hi = sem("fT_hi_ready")
        s_half = sem("proj_hi_ready")
        s_scratch = sem("scratch_written")
        s_stack = [sem(f"stack{n}_loaded") for n in range(2)]
        s_cross = sem("cross_rows_loaded")
        s_shift = sem("shift_ready")
        s_shift_row = sem("shift_rows_ready")
        s_pv = sem("values_summed")
        s_p0_in = sem("p0_exponent_ready")
        s_p0 = sem("p0_ready")
        s_p0v0 = sem("p0_v0_ready")
        s_g_split = sem("g_split_ready")
        s_g_sum = sem("g_squares_summed")
        s_g_sq = sem("g_squares_ready")
        s_down = sem("down_used")
        s_out = sem("out_rows_ready")
        s_base = sem("power_base_ready")
        s_root = sem("power_ready")
        s_base_next = sem("next_power_base_ready")
        s_root_next = sem("next_power_ready")
        s_h_moved = sem("next_tokens_moved")
        s_dve = sem("vector_step")
        cleared = [*filled, *drained, s_xT_hi, s_tok_used, s_xn_a, s_xn_b, s_fT_hi, s_half, s_scratch,
                   *s_stack, s_cross, s_shift, s_shift_row, s_pv, s_p0_in, s_p0, s_p0v0, s_g_split, s_g_sum, s_g_sq, s_down,
                   s_out, s_base, s_root, s_base_next, s_root_next, s_h_moved, s_dve]
        numbers = sorted(s.num for s in cleared)
        assert numbers == list(range(numbers[0], numbers[0] + len(numbers)))

        HALVES = ((0, 0), (1, 0), (0, 1))
        w_half = (w_hi, w_lo)
        x_tiles = x.rearrange("b (i p) c d -> b p i (c d)", p=P)
        out_tiles = out[:, 1:T + 1, :].rearrange("b (i p) n -> b p i n", p=P)
        SETUP_UNITS = 4 + 8
        N_WEIGHTS = 13

        with nc.Block() as block:

            @block.sync
            def _(sp):
                def load(dst, src):
                    sp.dma_start(dst, src).then_inc(s_weights, 16)

                load(const[:, :], constants)
                load(x_sum, tok_sum.rearrange("(t p) i -> p t i", p=P))
                load(x_wt[:, :, :], tok_weight.rearrange("(t p) d -> p t d", p=P))
                load(up_raw.rearrange("p (t n) -> p t n", n=D),
                     w_ffn_up.rearrange("(t p) n -> p t n", p=P))
                load(down_raw.rearrange("p (t n) -> p t n", n=FF),
                     w_ffn_down.rearrange("(t p) n -> p t n", p=P))

                def raw(name, t, n):
                    return w_raw[:, w_at[name]:w_at[name] + t * n].rearrange("p (t n) -> p t n", n=n)

                load(raw("kv_down", FT, DC), w_kv_down.rearrange("(t p) n -> p t n", p=P))
                load(raw("k_up", 1, D)[:, 0, :], w_k_up)
                load(raw("v_up", 1, D)[:, 0, :], w_v_up)
                load(raw("q", FT, D), w_q.rearrange("(t p) n -> p t n", p=P))
                load(raw("o", FT, D), w_o.rearrange("(t p) n -> p t n", p=P))
                load(w_rope_raw, w_q_rope.rearrange("(t p) n -> p t n", p=P))
                load(w_rope_k_raw, w_k_rope)
                load(row[0:1, 0, :], cls_tok[0])
                sp.wait_ge(s_setup_full, SETUP_UNITS)
                sp.dma_start(x_in[:, :, :],
                             x_tiles[0:1].rearrange("b p i n -> p (b i) n")).then_inc(s_x, 16)
                sp.wait_ge(s_cls_dve, 11)
                for b in range(B):
                    sp.dma_start(out[b, 0:1, :], row[0:1, 2, :]).then_inc(s_stored, 16)
                sp.wait_ge(s_stored, 16 * B)

            @block.gpsimd
            def _(pool):
                pool.wait_ge(s_weights, 16 * N_WEIGHTS)
                for n in range(3):
                    pool.wait_ge(s_setup_base, n + 1)
                    nc.gpsimd.tensor_tensor(root[0:1, :, 0:1], base[0:1, :, 0:1], powers[0:1, :, 0:1],
                                            ALU.pow).then_inc(s_setup_root, 1)
                    if n == 1:
                        pool.wait_ge(s_weight_lo, 1)
                        pool.wait_ge(s_cls_pe, 4)
                        nc.gpsimd.memset(v[:, :, :, :], 1.0)

            @block.vector
            def _(dve):
                steps = [0]

                def link(ins):
                    steps[0] += 1
                    ins.then_inc(s_setup_dve, 1)
                    dve.wait_ge(s_setup_dve, steps[0])

                dve.wait_ge(s_weights, 16 * N_WEIGHTS)
                for t in range(FT):
                    for d in range(DIN):
                        last = nc.vector.tensor_scalar(
                            tok_prod[:, t, :].rearrange("p (i d) -> p i d", d=DIN)[:, :, d],
                            x_sum[:, t, :], x_wt[:, t, d:d + 1], None, ALU.mult)
                last.then_inc(s_tok_prod, 1)
                nc.vector.tensor_reduce(tiny[:, 0:1], up_raw, AX_X, ALU.add,
                                        apply_absolute_value=True)
                nc.vector.tensor_reduce(tiny[:, 1:2], down_raw, AX_X, ALU.add,
                                        apply_absolute_value=True).then_inc(s_abs, 1)
                nc.vector.tensor_copy(ident_b[:, :], ident)
                nc.vector.tensor_copy(causal_b[:, :], table("causal"))
                for j in range(2):
                    nc.vector.tensor_copy(
                        k_cross[2 * DR:CROSS, j, :],
                        table("select")[2 * DR:CROSS, j:j + 1].broadcast_to([2, T]))
                a, k = w_at["rot_q"], w_at["rot_k"]
                nc.vector.memset(k_rope_twice, 0.0)
                link(nc.vector.memset(w_raw[:, a:n_w], 0.0))
                rq = w_raw[:, a:a + FT * P].rearrange("p (t n) -> p t n", n=P)
                sq = w_rope_raw
                nc.vector.tensor_copy(rq[:, :, 0:DR], sq)
                nc.vector.tensor_scalar(rq[:, :, DR:DR + HALF], sq[:, :, HALF:DR], -1.0, None, ALU.mult)
                nc.vector.tensor_copy(rq[:, :, DR + HALF:2 * DR], sq[:, :, 0:HALF])
                rk = w_raw[:, k + 2 * DR:k + 4 * DR]
                sk = w_rope_k_raw
                nc.vector.tensor_copy(rk[:, 0:DR], sk)
                nc.vector.tensor_scalar(rk[:, DR:DR + HALF], sk[:, HALF:DR], -1.0, None, ALU.mult)
                nc.vector.tensor_copy(k_rope_twice[:, 0:2 * DR].rearrange("p (r n) -> p r n", r=2),
                                      sk.unsqueeze(1).broadcast_to([P, 2, DR]))
                nc.vector.tensor_copy(rk[:, DR + HALF:2 * DR], sk[:, 0:HALF]).then_inc(s_weight_raw, 1)
                dve.wait_ge(s_total, 1)
                link(nc.vector.tensor_scalar(tiny[:, 2:4], bank[7][:, 0:2], 1.0 / (D * FF), 0.5,
                                             ALU.mult, ALU.mult))
                link(nc.vector.tensor_scalar(tiny[:, 4:6], tiny[:, 2:4], -1.0, None, ALU.mult))
                for n, w in enumerate((up_raw, down_raw)):
                    link(nc.vector.tensor_scalar(above, w, tiny[:, 2 + n:3 + n], None, ALU.is_gt))
                    last = nc.vector.scalar_tensor_tensor(
                        out=w, in0=w, scalar=tiny[:, 4 + n:5 + n], in1=above,
                        op0=ALU.is_lt, op1=ALU.subtract)
                    link(last)
                    nc.vector.tensor_scalar(w, w, -1.0, None, ALU.mult).then_inc(s_ternary, 1)
                for n in range(4):
                    dve.wait_ge(s_setup_hi, n + 1)
                    kt = 2 * n
                    nc.vector.tensor_tensor(
                        tok_lo[:, kt:kt + 2, :],
                        bank[n][:, :].rearrange("p (k o) -> p k o", k=2),
                        tok_hi[:, kt:kt + 2, :].bitcast(F32), ALU.subtract).then_inc(s_setup_lo, 1)
                dve.wait_ge(s_weight_hi, 1)
                nc.vector.tensor_tensor(w_lo[:, :], w_raw[:, :], w_hi[:, :].bitcast(F32),
                                        ALU.subtract).then_inc(s_weight_lo, 1)

                raised = [0]

                def raise_base(values):
                    for n, (value, eps) in enumerate(values):
                        last = nc.vector.tensor_scalar(base[0:1, n, 0:1], value, eps, None, ALU.add)
                    last.then_inc(s_setup_base, 1)
                    raised[0] += 1
                    dve.wait_ge(s_setup_root, raised[0])

                def norm_row(src, dst, rms):
                    link(nc.vector.bn_stats(stats[0:1, 0, :], src))
                    link(nc.vector.bn_aggr(moments[0:1, 0, :], stats[0:1, 0, :]))
                    scale = root[0:1, 0, 0:1]
                    raise_base([(moments[0:1, 0, 1:2], LN_EPS), (moments[0:1, 0, 1:2], 0.0)])
                    if rms:
                        scale = col[0:1, 0, 0:1]
                        link(nc.vector.tensor_tensor(scale, root[0:1, 0, 0:1], root[0:1, 1, 0:1], ALU.mult))
                        link(nc.vector.tensor_scalar(scale, scale, RMS_EPS, None, ALU.add))
                        link(nc.vector.reciprocal(scale, scale))
                        link(nc.vector.tensor_tensor(scale, root[0:1, 0, 0:1], scale, ALU.mult))
                    nc.vector.tensor_scalar(dst, src, moments[0:1, 0, 0:1], scale,
                                            ALU.subtract, ALU.mult).then_inc(s_cls_dve, 1)

                norm_row(row[0:1, 0, :], row[0:1, 2, :], False)
                dve.wait_ge(s_cls_pe, 1)
                nc.vector.tensor_copy(tiny[:, 8:10], bank[7][:, 8:10]).then_inc(s_cls_dve, 1)
                dve.wait_ge(s_cls_pe, 2)
                nc.vector.tensor_copy(tiny[:, 10:11], bank[7][:, 10:11]).then_inc(s_cls_dve, 1)
                dve.wait_ge(s_cls_pe, 3)
                head_of = table("head_of").rearrange("p (t n) -> p t n", t=FT)
                blk = tiny[:, 16:48].rearrange("p (t n) -> p t n", t=FT)
                nc.vector.tensor_copy(tiny[:, 11:14], bank[7][:, 11:14])
                nc.vector.tensor_copy(tiny[:, 14:16], bank[7][:, 14:16])
                link(nc.vector.tensor_copy(row[0:1, 3, :], bank[7][0:1, 256:512]))
                for t in range(FT):
                    last = nc.vector.tensor_scalar(blk[:, t, :], head_of[:, t, :],
                                                   tiny[:, 11 + t:12 + t], None, ALU.mult)
                link(last)
                link(nc.vector.tensor_copy(k0_hi[:, :, :], blk))
                nc.vector.tensor_tensor(k0_lo[:, :, :], blk, k0_hi[:, :, :].bitcast(F32), ALU.subtract)
                nc.vector.tensor_copy(k0_rope[:, :],
                                      tiny[:, 13:14].broadcast_to([P, H])).then_inc(s_cls_dve, 1)
                dve.wait_ge(s_cls_pe, 4)
                nc.vector.tensor_copy(v0_all[:, :], bank[6][:, 0:D])
                link(nc.vector.tensor_tensor(row[0:1, 1, :], bank[6][0:1, 256:512], row[0:1, 0, :],
                                             ALU.add))
                norm_row(row[0:1, 1, :], row[0:1, 2, :], True)
                dve.wait_ge(s_cls_pe, 5)
                nc.vector.tensor_copy(tiny[:, 8:10], bank[7][:, 8:10]).then_inc(s_cls_dve, 1)
                dve.wait_ge(s_cls_act, 1)
                link(nc.vector.tensor_tensor(tiny[:, 56:64], tiny[:, 48:56], tiny[:, 48:56], ALU.mult))
                nc.vector.reduce_sum(tiny[:, 0:1], tiny[:, 56:64], AX_X).then_inc(s_cls_dve, 1)
                dve.wait_ge(s_cls_pe, 7)
                link(nc.vector.tensor_scalar(tiny[0:1, 1:2], bank[7][0:1, 20:21], 1.0 / FF, None,
                                             ALU.mult))
                raise_base([(tiny[0:1, 1:2], 1.0), (tiny[0:1, 1:2], 0.0)])
                link(nc.vector.tensor_scalar(tiny[0:1, 1:2], root[0:1, 1, 0:1], RMS_EPS, None, ALU.add))
                link(nc.vector.reciprocal(tiny[0:1, 2:3], tiny[0:1, 1:2]))
                last = nc.vector.scalar_tensor_tensor(
                    out=row[0:1, 2, :], in0=bank[7][0:1, 256:512], scalar=tiny[0:1, 2:3],
                    in1=row[0:1, 1, :], op0=ALU.mult, op1=ALU.add)
                link(last)
                for _ in range(4):
                    nc.vector.engine_nop().then_inc(s_cls_dve, 1)

            @block.scalar
            def _(act):
                for n in range(SETUP_UNITS):
                    act.wait_ge(s_setup_full, n + 1)
                    if n < 4:
                        dst = tok_hi[:, 2 * n:2 * n + 2, :]
                    elif n < 8:
                        t, half = divmod(n - 4, 2)
                        dst = up_T[:, t:t + 1, 512 * half:512 * half + 512]
                    else:
                        dst = down_T[:, 2 * (n - 8):2 * (n - 8) + 2, :]
                    src = bank[n % 4][:, :].rearrange("p (k o) -> p k o", k=dst.shape[1])
                    nc.scalar.activation(dst, src, ACT.Copy).then_inc(s_setup_hi, 1)
                    if n == 3:
                        act.wait_ge(s_weight_raw, 1)
                        nc.scalar.activation(w_hi[:, :], w_raw[:, :], ACT.Copy).then_inc(s_weight_hi, 1)
                act.wait_ge(s_cls_pe, 6)
                nc.scalar.activation(tiny[:, 48:56], bank[7][:, 48:56], ACT.Gelu).then_inc(s_cls_act, 1)

            @block.tensor
            def _(pe):
                pe.wait_ge(s_weights, 16 * N_WEIGHTS)
                pe.wait_ge(s_abs, 1)
                nc.tensor.matmul(bank[7][:, 0:2], ones, tiny[:, 0:2], start=True,
                                 stop=True).then_inc(s_total, 1)
                pe.wait_ge(s_tok_prod, 1)
                for n in range(SETUP_UNITS):
                    if n >= 4:
                        pe.wait_ge(s_setup_hi, n - 3)
                    if 4 <= n < 8:
                        pe.wait_ge(s_setup_lo, n - 3)
                    if n == 4:
                        pe.wait_ge(s_ternary, 1)
                    if n == 8:
                        pe.wait_ge(s_ternary, 2)
                    for j in range(4):
                        if n < 4:
                            kt, t = 2 * n + j // 2, j % 2
                            src = tok_prod[:, t, kt * P:kt * P + P]
                        elif n < 8:
                            t, half = divmod(n - 4, 2)
                            src = up_raw[:, (4 * half + j) * D + t * P:(4 * half + j) * D + t * P + P]
                        else:
                            gt, t = 2 * (n - 8) + j // 2, j % 2
                            src = down_raw[:, t * FF + gt * P:t * FF + gt * P + P]
                        last = nc.tensor.transpose(bank[n % 4][:, j * P:j * P + P], src, ident)
                    last.then_inc(s_setup_full, 1)

                def mm(dst, pairs):
                    for n, (a, b) in enumerate(pairs):
                        last = nc.tensor.matmul(dst, a, b, start=n == 0, stop=n == len(pairs) - 1)
                    return last

                def raw(name, tile, width, first, count):
                    return weight(w_raw, name, tile, width, first, count)

                one = ones[0:1, 0:1]
                pe.wait_ge(s_weight_raw, 1)
                pe.wait_ge(s_cls_dve, 1)
                for t in range(FT):
                    last = mm(bank[7][:, 8 + t:9 + t], [(row[0:1, 2, t * P:t * P + P], one)])
                last.then_inc(s_cls_pe, 1)
                pe.wait_ge(s_cls_dve, 2)
                mm(bank[7][:, 10:11], [(raw("kv_down", t, DC, 0, DC), tiny[:, 8 + t:9 + t])
                                       for t in range(FT)]).then_inc(s_cls_pe, 1)
                pe.wait_ge(s_cls_dve, 3)
                c0 = tiny[:, 10:11]
                mm(bank[7][0:1, 256:512], [(c0, raw("v_up", 0, D, 0, D))])
                for t in range(FT):
                    mm(bank[7][:, 11 + t:12 + t], [(raw("k_up", 0, D, t * P, P), c0)])
                for t in range(FT):
                    mm(bank[7][:, 14 + t:15 + t], [(raw("v_up", 0, D, t * P, P), c0)])
                mm(bank[7][:, 13:14], [(k_rope_twice, c0)]).then_inc(s_cls_pe, 1)
                pe.wait_ge(s_cls_dve, 4)
                mm(bank[6][:, 0:D], [(ones[0:1, :], row[0:1, 3, :])])
                mm(bank[6][0:1, 256:512], [(tiny[:, 14 + t:15 + t], raw("o", t, D, 0, D))
                                           for t in range(FT)]).then_inc(s_cls_pe, 1)
                pe.wait_ge(s_cls_dve, 5)
                for t in range(FT):
                    last = mm(bank[7][:, 8 + t:9 + t], [(row[0:1, 2, t * P:t * P + P], one)])
                last.then_inc(s_cls_pe, 1)
                pe.wait_ge(s_cls_dve, 6)
                pe.wait_ge(s_setup_hi, SETUP_UNITS)
                for ft in range(GT):
                    last = mm(bank[7][:, 48 + ft:49 + ft],
                              [(up_T[:, t, ft * P:ft * P + P].bitcast(F32), tiny[:, 8 + t:9 + t])
                               for t in range(FT)])
                last.then_inc(s_cls_pe, 1)
                pe.wait_ge(s_cls_dve, 7)
                pe.wait_ge(s_cls_act, 1)
                mm(bank[7][0:1, 20:21], [(tiny[:, 0:1], ones[:, 0:1])])
                mm(bank[7][0:1, 256:512], [(tiny[:, 48 + ft:49 + ft], down_T[:, ft, :].bitcast(F32))
                                           for ft in range(GT)]).then_inc(s_cls_pe, 1)

        STEPS = H + LAG + 1
        SLOTS = 3 * STEPS
        room = [0]
        for step in range(STEPS):
            for _ in range(3):
                room.append(room[-1] + (3 if step <= LAG else 2))

        BACK, BACK_EARLY = TT + 1 + PAIRS + 2 + PAIRS * (GU // 2 + 2) + 1, TT + 1 + PAIRS + 2
        FRONT, FRONT_EARLY = PAIRS * XU + 3 + 11, PAIRS * XU + 3

        def in_turn(part, back, front):
            for n in range(max(BACK_EARLY, FRONT_EARLY)):
                if part["front"] and n < FRONT_EARLY:
                    next(front)
                    yield
                if part["back"] and n < BACK_EARLY:
                    next(back)
                    yield
            if part["back"]:
                for n in range(BACK - BACK_EARLY):
                    next(back)
                    yield
            if part["front"]:
                for n in range(FRONT - FRONT_EARLY):
                    next(front)
                    yield

        def images(parts):
            bank_of, fill_of, read_of, before = {}, {}, {}, {}
            fills, reads = [0] * 8, [0] * 8

            def place(unit, n, own_fill=True):
                bank_of[unit], before[unit] = n, reads[n]
                fills[n] += own_fill
                reads[n] += 1
                fill_of[unit], read_of[unit] = fills[n], reads[n]

            turn = {0: 0, 2: 0, 4: 0}

            def place_in_turn(unit, n):
                place(unit, n + turn[n] % 2)
                turn[n] += 1

            def place_max(unit):
                place_in_turn(unit, 0)

            def place_turn(unit):
                place_in_turn(unit, 4)

            stack_load, loads = {}, [0, 0]

            def place_stack(k, g):
                loads[g % 2] += (6 if g >= 2 else 8) * 16
                stack_load[(k, g)] = loads[g % 2]

            raises, raised = {}, [0]

            def place_raise(*norm):
                raised[0] += 1
                raises[norm] = raised[0]

            def place_back(k):
                for i in range(TT):
                    place_turn(("oTok", k, i))
                    yield
                for f in range(FT):
                    place_turn(("fT1", k, f))
                yield
                for u in range(PAIRS):
                    place_turn(("y", k, u))
                    yield
                yield
                for f in range(FT):
                    place_turn(("fT2", k, f))
                yield
                for p in range(PAIRS):
                    for n in range(GU):
                        place_turn(("g", k, p, n))
                        if n % 2:
                            yield
                    yield
                    place(("d", k, p), 6)
                    place_turn(("ss", k, p))
                    yield
                yield

            def place_front(k):
                for p in range(PAIRS):
                    for n in range(XU):
                        place_turn(("xT", k, p, n))
                        yield
                    place(("h", k, p), 6)
                yield
                yield
                yield
                for f in range(FT):
                    place_turn(("fT0", k, f))
                yield
                for unit in (("c", k), ("q", k, 0), ("q", k, 1), ("k", k, 0), ("k", k, 1),
                             ("rot", k), ("v", k, 0), ("v", k, 1), ("rope", k), ("s0", k)):
                    place_turn(unit)
                    yield

            for k, part in enumerate(parts):
                if part["attend"]:
                    for hd in range(H):
                        place_max(("s", k, hd, 0))
                        if hd >= 2 and hd % 2 == 0:
                            place_max(("m", k, hd // 2 - 1))
                        place_max(("s", k, hd, 1))
                        place_max(("s", k, hd, 2))
                        for u in range(3):
                            place_in_turn(("sT", k, hd, u), 2)
                    place_max(("m", k, H // 2 - 1))
                    for g in range(NG):
                        place(("o", k, g), 7, own_fill=False)
                    for g in range(1, NG):
                        place_stack(k, g)
                for _ in in_turn(part, place_back(k), place_front(k)):
                    pass
                if part["back"]:
                    place_raise("back", k)
                    for p in range(PAIRS):
                        place_raise("ss", k, p)
                if part["front"]:
                    place_stack(k + 1, 0)
            nb = [sum(bool(q["back"]) for q in parts[:k]) for k in range(len(parts) + 1)]
            na = [sum(bool(q["attend"]) for q in parts[:k]) for k in range(len(parts) + 1)]
            nf = [sum(bool(q["front"]) for q in parts[:k]) for k in range(len(parts) + 1)]

            def full(*unit):
                return filled[bank_of[unit]], fill_of[unit]

            def read(*unit):
                return drained[bank_of[unit]], read_of[unit]

            def of(*unit):
                return bank[bank_of[unit]]

            def turns(back, front, k, late):
                part = parts[k]
                n = BACK * bool(part["back"]) + FRONT * bool(part["front"])
                filler = in_turn(part, back(k, *(part["back"] or (0, 0))),
                                 front(k, *(part["front"] or (0, 0))))
                if not part["attend"]:
                    for _ in filler:
                        pass
                    return
                done = 0
                for slot in range(SLOTS):
                    while done < room[max(slot + 1 - late, 0)] * n // room[SLOTS]:
                        next(filler, None)
                        done += 1
                    yield
                for _ in filler:
                    pass

            def run_parts(attend, back, front, late=0):
                for k, part in enumerate(parts):
                    slots = turns(back, front, k, late)
                    if part["attend"]:
                        attend(k, part["attend"][0], lambda slots=slots: next(slots))
                    for _ in slots:
                        pass

            def stored(image_done):
                return 16 * B + 16 * PAIRS * image_done

            with nc.Block() as block:

                @block.sync
                def _(sp):
                    def load_stack(k, g):
                        t, first = divmod(g * GH * HD, P)
                        for w, stack, halves in ((0, q_stack, (0, 1, 0)), (1, k_stack, (0, 0, 1))):
                            for r, half in enumerate(halves):
                                sp.dma_start(
                                    stack[r * HD:(r + 1) * HD,
                                          (g % 2) * GH:(g % 2 + 1) * GH, :].bitcast(F32),
                                    scratch[w, half, t, first:first + GH * HD, :]
                                    .rearrange("(j p) n -> p j n", p=HD)).then_inc(s_stack[g % 2], 16)
                            if g < 2:
                                sp.dma_start(
                                    stack[CONTENT:ROWS, g * GH:(g + 1) * GH, :].bitcast(F32),
                                    rope_scratch[w, :, 0:1, :].broadcast_to([DR, GH, T])
                                    ).then_inc(s_stack[g], 16)

                    def load_cross():
                        for w, cross, halves in ((0, q_cross, (1, 0)), (1, k_cross, (0, 1))):
                            for n, half in enumerate(halves):
                                sp.dma_start(
                                    cross[n * DR:(n + 1) * DR, :, :].bitcast(F32),
                                    rope_scratch[w, :, half:half + 1, :].broadcast_to([DR, 2, T])
                                    ).then_inc(s_cross, 16)

                    def store_rows(k, p, parity, image):
                        sp.wait_ge(s_out, PAIRS * nb[k] + p + 1)
                        sp.dma_start(out_tiles[bass.ds(image, 1), :, 2 * p:2 * p + 2, :]
                                     .rearrange("b p i n -> p (b i) n"),
                                     xn[:, 2 * p:2 * p + 2, :]).then_inc(s_stored, 16)

                    for k, part in enumerate(parts):
                        if part["attend"]:
                            if k and parts[k - 1]["attend"]:
                                sp.wait_ge(*full("sT", k - 1, H - 1, 2))
                            load_stack(k, 1)
                            load_cross()
                        if part["attend"]:
                            sp.wait_ge(*full("sT", k, GH - 1, 2))
                            load_stack(k, 2)
                        if part["front"]:
                            image = part["front"][1]
                            sp.wait_ge(*full("xT", k, PAIRS - 1, XU - 1))
                            sp.dma_start(x_in[:, :, :], x_tiles[bass.ds((image + 1) % B, 1)]
                                         .rearrange("b p i n -> p (b i) n")).then_inc(s_x, 16)
                        if part["attend"]:
                            sp.wait_ge(*full("sT", k, 2 * GH - 1, 2))
                            load_stack(k, 3)
                        if part["back"]:
                            for p in range(PAIRS):
                                store_rows(k, p, *part["back"])
                        if part["front"]:
                            if part["attend"]:
                                sp.wait_ge(s_stack[0], stack_load[(k, 2)])
                                sp.wait_ge(s_stack[1], stack_load[(k, 3)])
                                sp.wait_ge(s_cross, 64 * (na[k] + 1))
                            for w, name in ((0, "q"), (1, "k")):
                                for t in range(FT):
                                    sp.wait_ge(*read(name, k, t))
                                sp.dma_start(scratch[w].rearrange("a t p n -> p (a t) n"),
                                             qk[:, w].bitcast(F32).rearrange("p a t n -> p (a t) n")
                                             ).then_inc(s_scratch, 16)
                            sp.wait_ge(*read("rope", k))
                            sp.dma_start(rope_scratch.rearrange("w p a n -> (w p) a n"),
                                         rope[:, :, :].bitcast(F32)).then_inc(s_scratch, 16)
                            sp.wait_ge(s_scratch, 48 * (nf[k] + 1))
                            if part["attend"]:
                                sp.wait_ge(*full("sT", k, 3 * GH - 1, 2))
                            load_stack(k + 1, 0)
                    if parts[-1]["front"]:
                        sp.wait_ge(s_stack[0], loads[0])

                @block.gpsimd
                def _(pool):
                    steps = [0]

                    def raise_base(cols, *norm):
                        pool.wait_ge(s_base, raises[norm])
                        nc.gpsimd.tensor_tensor(root[:, :, cols], base[:, :, cols], powers[:, :, cols],
                                                ALU.pow).then_inc(s_root, 1)

                    def raise_next(k):
                        pool.wait_ge(s_base_next, nf[k] + 1)
                        nc.gpsimd.tensor_tensor(root_next[:, 0, :], base_next[:, 0, :], powers[:, 0, :],
                                                ALU.pow).then_inc(s_root_next, 1)

                    for k, part in enumerate(parts):
                        if part["back"]:
                            if na[k]:
                                pool.wait_ge(s_p0, na[k])
                            for i in range(TT):
                                nc.gpsimd.tensor_tensor(
                                    p0_v0[:, i, :].rearrange("p (n d) -> p n d", d=HD),
                                    v0_all[:, :].rearrange("p (n d) -> p n d", d=HD),
                                    p0[:, i, :].unsqueeze(2).broadcast_to([P, H, HD]),
                                    ALU.mult).then_inc(s_p0v0, 1)
                            raise_base(slice(0, TT), "back", k)
                            if part["front"]:
                                raise_next(k)
                            for p in range(PAIRS):
                                for n in range(GU):
                                    pool.wait_ge(*read("g", k, p, n))
                                    g = g_sb[:, (p * GU + n) % RING, :]
                                    if n == 0:
                                        if p:
                                            pool.wait_ge(*full("ss", k, p - 1))
                                        nc.gpsimd.tensor_tensor(g_acc[:, :], g, g,
                                                                ALU.mult).then_inc(s_g_sum, 1)
                                        continue
                                    pool.wait_ge(s_g_sum, PAIRS * GU * nb[k] + p * GU + n)
                                    steps[0] += 1
                                    nc.gpsimd.tensor_tensor(g_sq[:, :], g, g, ALU.mult).then_inc(s_g_sq, 1)
                                    pool.wait_ge(s_g_sq, steps[0])
                                    nc.gpsimd.tensor_tensor(g_acc[:, :], g_acc[:, :], g_sq[:, :],
                                                            ALU.add).then_inc(s_g_sum, 1)
                                raise_base(slice(2 * p, 2 * p + 2), "ss", k, p)
                        elif part["front"]:
                            raise_next(k)
                        if part["front"]:
                            if part["back"]:
                                pool.wait_ge(s_out, PAIRS * (nb[k] + 1))
                            for p in range(PAIRS):
                                pool.wait_ge(*read("h", k, p))
                            nc.gpsimd.tensor_copy(h[:, part["front"][0], :, :], h_next[:, :, :]
                                                  ).then_inc(s_h_moved, 1)

                @block.scalar
                def _(act):
                    def copy(dst, src):
                        return nc.scalar.activation(dst, src, ACT.Copy)

                    def attend(k, parity, slot):
                        for step in range(STEPS):
                            slot()
                            if step % 2 == 0 and 2 <= step <= H:
                                m = step // 2 - 1
                                if m >= 2:
                                    act.wait_ge(*full("sT", k, 2 * m - 3, 2))
                                act.wait_ge(*full("m", k, m))
                                copy(q_cross[2 * DR:CROSS, m % 2, :], of("m", k, m)[2 * DR:CROSS, :]
                                     ).then_inc(drained[bank_of[("m", k, m)]], 1)
                            hd = step - LAG
                            for u, n in enumerate(PT_UNITS):
                                if 0 <= hd < H:
                                    if u == 0 and hd >= 2:
                                        act.wait_ge(s_pv, H * na[k] + hd - 1)
                                    act.wait_ge(*full("sT", k, hd, u))
                                    nc.scalar.activation(probs_T[:, hd % 2, 512 * u:512 * u + n],
                                                         of("sT", k, hd, u)[:, 0:n], ACT.Exp,
                                                         scale=SCALE).then_inc(drained[bank_of[("sT", k, hd, u)]], 1)
                                if u == 1:
                                    slot()
                            hd = step - LAG - 1
                            if hd >= 0 and hd % GH == GH - 1:
                                act.wait_ge(s_pv, H * na[k] + hd + 1)
                                copy(oT[:, hd // GH, :], bank[7][:, :]).then_inc(drained[7], 1)
                            slot()
                        act.wait_ge(s_p0_in, na[k] + 1)
                        nc.scalar.activation(p0[:, :, :], denom[:, :, :], ACT.Exp,
                                             scale=SCALE).then_inc(s_p0, 1)

                    def features_hi(k, stage):
                        for f in range(FT):
                            act.wait_ge(*full(stage, k, f))
                            copy(fT_hi[:, f, :], of(stage, k, f)[:, :]).then_inc(s_fT_hi, 1)

                    def back(k, parity, image):
                        for i in range(TT):
                            yield
                        features_hi(k, "fT1")
                        yield
                        yield
                        yield
                        yield
                        features_hi(k, "fT2")
                        yield
                        for p in range(PAIRS):
                            for n in range(GU):
                                u = p * GU + n
                                act.wait_ge(*full("g", k, p, n))
                                if u >= RING:
                                    act.wait_ge(s_g_split, PAIRS * GU * nb[k] + u - RING + 1)
                                    act.wait_ge(s_g_sum, PAIRS * GU * nb[k] + u - RING + 1)
                                nc.scalar.activation(g_sb[:, u % RING, :], of("g", k, p, n)[:, :], ACT.Gelu
                                                     ).then_inc(drained[bank_of[("g", k, p, n)]], 1)
                                if n % 2:
                                    yield
                            yield
                            yield
                        yield

                    def front(k, parity, image):
                        def take_h(p):
                            if nf[k]:
                                act.wait_ge(s_h_moved, nf[k])
                                act.wait_ge(s_xn_a, TT * nf[k])
                            act.wait_ge(*full("h", k, p))
                            copy(h_next[:, 2 * p:2 * p + 2, :].rearrange("p i n -> p (i n)"),
                                 bank[6][:, :]).then_inc(drained[6], 1)

                        for p in range(PAIRS):
                            for n in range(XU):
                                act.wait_ge(*full("xT", k, p, n))
                                u = p * XU + n
                                if u == XU + 1:
                                    act.wait_ge(*full("h", k, 0))
                                elif u >= RING:
                                    act.wait_ge(s_tok_used, (XU - 1) * PAIRS * nf[k] + u - RING + 1 - (u > XU))
                                copy(xT_hi[:, u % RING, :], of("xT", k, p, n)[:, :]).then_inc(s_xT_hi, 1)
                                if u == XU + 1:
                                    take_h(0)
                                yield
                        yield
                        take_h(1)
                        yield
                        yield
                        features_hi(k, "fT0")
                        yield
                        act.wait_ge(*full("c", k))
                        copy(cT_hi, of("c", k)[:, :]).then_inc(s_half, 1)
                        yield
                        for w, name in ((0, "q"), (1, "k")):
                            for t in range(FT):
                                act.wait_ge(*full(name, k, t))
                                copy(qk[:, w, 0, t, :], of(name, k, t)[:, :]).then_inc(s_half, 1)
                                yield
                        yield
                        for u in range(2):
                            act.wait_ge(*full("v", k, u))
                            for i in range(2):
                                last = copy(v[:, parity, 2 * u + i, 0:H * VW]
                                            .rearrange("p (n d) -> p n d", d=VW)[:, :, 0:HD],
                                            of("v", k, u)[:, i * D:i * D + D]
                                            .rearrange("p (n d) -> p n d", d=HD))
                            last.then_inc(drained[bank_of[("v", k, u)]], 1)
                            yield
                        act.wait_ge(*full("rope", k))
                        copy(rope[:, 0, :], of("rope", k)[0:2 * DR, :]).then_inc(s_half, 1)
                        yield
                        yield

                    run_parts(attend, back, front)

                @block.vector
                def _(dve):
                    steps = [0]

                    def link(ins):
                        steps[0] += 1
                        ins.then_inc(s_dve, 1)
                        dve.wait_ge(s_dve, steps[0])

                    def low(dst, src, hi):
                        return nc.vector.tensor_tensor(dst, src, hi.bitcast(F32), ALU.subtract)

                    rstd = root[:, 0, :]
                    var = moments[:, :, 1]

                    def raise_base(values, cols=slice(0, TT)):
                        for n, (value, scale, eps) in enumerate(values):
                            last = nc.vector.tensor_scalar(base[:, n, cols], value, scale, eps,
                                                           ALU.mult, ALU.add)
                        last.then_inc(s_base, 1)

                    def norm(dst, src, moments, scale, i):
                        return nc.vector.tensor_scalar(dst[:, i, :], src[:, i, :], moments[:, i, 0:1],
                                                       scale[:, i:i + 1], ALU.subtract, ALU.mult)

                    def moments_of(tiles, src, stats, moments):
                        for i in tiles:
                            last = nc.vector.bn_stats(stats[:, i, :], src[:, i, :])
                        link(last)
                        for i in tiles:
                            last = nc.vector.bn_aggr(moments[:, i, :], stats[:, i, :])
                        link(last)

                    def features_lo(k, stage):
                        done = FT * (2 * nb[k + (stage == "fT0")] + nf[k] + (stage == "fT2"))
                        for f in range(FT):
                            dve.wait_ge(s_fT_hi, done + f + 1)
                            low(fT_lo[:, f, :], of(stage, k, f)[:, :], fT_hi[:, f, :]
                                ).then_inc(drained[bank_of[(stage, k, f)]], 1)

                    def attend(k, parity, slot):
                        if nf[k]:
                            dve.wait_ge(*read("s0", k - 1))
                        for step in range(STEPS):
                            hd = step
                            for u, tiles in enumerate(((0, 2), (3,), (1,))):
                                if hd < H:
                                    if u == 0 and hd >= 2:
                                        dve.wait_ge(s_shift, H * na[k] + hd - 1)
                                    dve.wait_ge(*full("s", k, hd, u))
                                    for i in tiles:
                                        c = S_AT[i][1]
                                        last = nc.vector.reduce_max(
                                            row_max[:, hd % 2, i:i + 1],
                                            of("s", k, hd, u)[:, c:c + P * (i + 1)], AX_X)
                                    last.then_inc(drained[bank_of[("s", k, hd, u)]], 1)
                                    if u == 2:
                                        dve.wait_ge(*read("s", k, hd, 1))
                                        dve.wait_ge(*read("s", k, hd, 2))
                                        nc.vector.scalar_tensor_tensor(
                                            out=shift[:, :, hd], in0=row_max[:, hd % 2, :], scalar=-1.0,
                                            in1=neg_s0[:, parity, :, hd], op0=ALU.mult,
                                            op1=ALU.min).then_inc(s_shift, 1)
                                slot()
                        dve.wait_ge(s_shift, H * (na[k] + 1))
                        nc.vector.tensor_tensor(denom[:, :, :], shift[:, :, :].bitcast(F32),
                                                neg_s0[:, parity, :, :], ALU.subtract).then_inc(s_p0_in, 1)

                    def back(k, parity, image):
                        if na[k]:
                            dve.wait_ge(s_p0, na[k])
                        for i in range(TT):
                            dve.wait_ge(*full("oTok", k, i))
                            o = of("oTok", k, i)[:, :].rearrange("p (n d) -> p n d", d=OW)
                            link(nc.vector.tensor_tensor(denom[:, i, :], o[:, :, HD], p0[:, i, :], ALU.add))
                            link(nc.vector.reciprocal(recip[:, i, :], denom[:, i, :]))
                            dve.wait_ge(s_p0v0, TT * nb[k] + i + 1)
                            w = p0_v0[:, i, :].rearrange("p (n d) -> p n d", d=HD)
                            nc.vector.tensor_tensor(w, o[:, :, 0:HD], w, ALU.add
                                                    ).then_inc(drained[bank_of[("oTok", k, i)]], 1)
                            dve.wait_ge(*read("oTok", k, i))
                            if i == 0:
                                dve.wait_ge(s_stored, stored(image))
                            nc.vector.tensor_tensor(
                                xn[:, i, :].rearrange("p (n d) -> p n d", d=HD), w,
                                recip[:, i, :].unsqueeze(2).broadcast_to([P, H, HD]),
                                ALU.mult).then_inc(s_xn_b, 1)
                            yield
                        features_lo(k, "fT1")
                        yield
                        if k >= 2 and parts[k - 2]["front"]:
                            dve.wait_ge(s_h_moved, nf[k - 1])
                        for u in range(PAIRS):
                            dve.wait_ge(*full("y", k, u))
                            rows = h[:, parity, 2 * u:2 * u + 2, :].rearrange("p i n -> p (i n)")
                            nc.vector.tensor_tensor(rows, of("y", k, u)[:, :], rows, ALU.add
                                                    ).then_inc(drained[bank_of[("y", k, u)]], 1)
                            dve.wait_ge(*read("y", k, u))
                            moments_of((2 * u, 2 * u + 1), h[:, parity], stats, moments)
                            if u == PAIRS - 1:
                                raise_base([(var, 1.0, LN_EPS), (var, 1.0, 0.0)])
                            yield
                        rms, scale = col[:, 0, :], col[:, 1, :]
                        dve.wait_ge(s_root, raises[("back", k)])
                        link(nc.vector.tensor_tensor(rms, rstd, root[:, 1, :], ALU.mult))
                        link(nc.vector.tensor_scalar(rms, rms, RMS_EPS, None, ALU.add))
                        link(nc.vector.reciprocal(rms, rms))
                        link(nc.vector.tensor_tensor(scale, rstd, rms, ALU.mult))
                        for i in range(TT):
                            norm(xn, h[:, parity], moments, scale, i).then_inc(s_xn_b, 1)
                        yield
                        features_lo(k, "fT2")
                        yield
                        if nf[k]:
                            dve.wait_ge(s_scratch, 48 * nf[k])
                        for p in range(PAIRS):
                            for n in range(GU):
                                u = p * GU + n
                                dve.wait_ge(*read("g", k, p, n))
                                if u == GU + 1:
                                    dve.wait_ge(*full("d", k, 0))
                                elif u >= RING:
                                    dve.wait_ge(s_down, (GU - 1) * PAIRS * nb[k] + u - RING + 1 - (u > GU))
                                g = g_sb[:, u % RING, :]
                                link(nc.vector.tensor_copy(g_hi[:, u % RING, :], g))
                                low(g_lo[:, u % RING, :], g, g_hi[:, u % RING, :]).then_inc(s_g_split, 1)
                                if p and n == 1:
                                    final(k, parity, 0)
                                if n % 2:
                                    yield
                            yield
                            cols = slice(2 * p, 2 * p + 2)
                            dve.wait_ge(*full("ss", k, p))
                            ss = of("ss", k, p)[:, 0:2]
                            nc.vector.tensor_scalar(base[:, 0, cols], ss, 1.0, 1.0, ALU.mult, ALU.add)
                            nc.vector.tensor_scalar(base[:, 1, cols], ss, 1.0 / FF, None, ALU.mult
                                                    ).then_inc(drained[bank_of[("ss", k, p)]], 1)
                            dve.wait_ge(*read("ss", k, p))
                            nc.vector.engine_nop().then_inc(s_base, 1)
                            yield
                        final(k, parity, 1)
                        yield

                    def final(k, parity, p):
                        cols = slice(2 * p, 2 * p + 2)
                        rms, scale = col[:, 0, cols], col[:, 1, cols]
                        dve.wait_ge(s_root, raises[("ss", k, p)])
                        link(nc.vector.tensor_scalar(rms, root[:, 1, cols], RMS_EPS, None, ALU.add))
                        link(nc.vector.reciprocal(scale, rms))
                        dve.wait_ge(*full("d", k, p))
                        for i in range(2):
                            last = nc.vector.scalar_tensor_tensor(
                                out=xn[:, 2 * p + i, :], in0=bank[6][:, i * D:i * D + D],
                                scalar=scale[:, i:i + 1], in1=h[:, parity, 2 * p + i, :],
                                op0=ALU.mult, op1=ALU.add)
                        last.then_inc(drained[6], 1)
                        dve.wait_ge(*read("d", k, p))
                        nc.vector.engine_nop().then_inc(s_out, 1)

                    def front(k, parity, image):
                        done = PAIRS * XU * nf[k]
                        for p in range(PAIRS):
                            for n in range(XU):
                                u = p * XU + n
                                dve.wait_ge(s_xT_hi, done + u + 1)
                                low(xT_lo[:, u % RING, :], of("xT", k, p, n)[:, :], xT_hi[:, u % RING, :]
                                    ).then_inc(drained[bank_of[("xT", k, p, n)]], 1)
                                if p and n == 2:
                                    dve.wait_ge(*read("h", k, 0))
                                    moments_of((0, 1), h_next, stats_next, moments_next)
                                yield
                        yield
                        dve.wait_ge(*read("h", k, 1))
                        moments_of((2, 3), h_next, stats_next, moments_next)
                        nc.vector.tensor_scalar(base_next[:, 0, :], moments_next[:, :, 1], 1.0, LN_EPS,
                                                ALU.mult, ALU.add).then_inc(s_base_next, 1)
                        yield
                        dve.wait_ge(s_root_next, nf[k] + 1)
                        for i in range(TT):
                            norm(xn_next, h_next, moments_next, root_next[:, 0, :], i).then_inc(s_xn_a, 1)
                        yield
                        features_lo(k, "fT0")
                        yield
                        done = 6 * nf[k] + 1
                        dve.wait_ge(s_half, done)
                        low(cT_lo, of("c", k)[:, :], cT_hi).then_inc(drained[bank_of[("c", k)]], 1)
                        yield
                        for w, name in ((0, "q"), (1, "k")):
                            for t in range(FT):
                                done += 1
                                dve.wait_ge(s_half, done)
                                low(qk[:, w, 1, t, :], of(name, k, t)[:, :],
                                    qk[:, w, 0, t, :]).then_inc(drained[bank_of[(name, k, t)]], 1)
                                yield
                        dve.wait_ge(*full("rot", k))
                        nc.vector.tensor_tensor(prod[:, :], of("rot", k)[:, :], table("rope"),
                                                ALU.mult).then_inc(drained[bank_of[("rot", k)]], 1)
                        yield
                        yield
                        yield
                        dve.wait_ge(s_half, done + 1)
                        low(rope[:, 1, :], of("rope", k)[0:2 * DR, :], rope[:, 0, :]
                            ).then_inc(drained[bank_of[("rope", k)]], 1)
                        yield
                        dve.wait_ge(*full("s0", k))
                        nc.vector.tensor_scalar(neg_s0[:, parity, :, :],
                                                of("s0", k)[:, 0:TT * H].rearrange("p (i n) -> p i n", n=H),
                                                -1.0, None, ALU.mult
                                                ).then_inc(drained[bank_of[("s0", k)]], 1)
                        yield

                    run_parts(attend, back, front, late=1)

                @block.tensor
                def _(pe):
                    fT = (fT_hi, fT_lo)
                    cT = (cT_hi, cT_lo)

                    def claim(*unit):
                        if before[unit] > 0:
                            pe.wait_ge(drained[bank_of[unit]], before[unit])
                        return bank[bank_of[unit]]

                    def product(dst, pairs):
                        for n, (lhsT, rhs) in enumerate(pairs):
                            last = nc.tensor.matmul(dst, lhsT, rhs, start=n == 0,
                                                    stop=n == len(pairs) - 1)
                        return last

                    def fill(unit, dst, pairs):
                        product(dst, pairs).then_inc(filled[bank_of[unit]], 1)

                    def from_features(name, width, first):
                        return [(weight(w_half[a], name, f, width, first, P), fT[c][:, f, :])
                                for f in range(FT) for a, c in HALVES]

                    def from_latent(name, first):
                        return [(weight(w_half[a], name, 0, 0, first, P), cT[c]) for a, c in HALVES]

                    def transpose_features(k, stage, rows, ready, count):
                        for f in range(FT):
                            claim(stage, k, f)
                        for i in range(TT):
                            pe.wait_ge(ready, count + i + 1)
                            for f in range(FT):
                                last = nc.tensor.transpose(of(stage, k, f)[:, i * P:i * P + P],
                                                           rows[:, i, f * P:f * P + P], ident)
                                if i == TT - 1:
                                    last.then_inc(filled[bank_of[(stage, k, f)]], 1)

                    def features_split(k, stage):
                        for f in range(FT):
                            pe.wait_ge(*read(stage, k, f))

                    def scores(k, hd, u):
                        g = hd // GH
                        slot = (g % 2) * GH + hd % GH
                        if u == 0 and hd % GH == 0 and (k, g) in stack_load:
                            pe.wait_ge(s_stack[g % 2], stack_load[(k, g)])
                        dst = claim("s", k, hd, u)
                        for i in (i for i in S_ORDER if S_AT[i][0] == u):
                            c, n = S_AT[i][1], P * (i + 1)
                            nc.tensor.matmul(dst[:, c:c + n], q_stack[0:ROWS, slot, i * P:i * P + P],
                                             k_stack[0:ROWS, slot, 0:n], start=True, stop=False)
                            last = nc.tensor.matmul(dst[:, c + n - P:c + n], ident_b[:, :],
                                                    causal_b[:, :], start=False, stop=True)
                        last.then_inc(filled[bank_of[("s", k, hd, u)]], 1)

                    def shift_rows(k, m):
                        pe.wait_ge(s_shift, H * na[k] + 2 * m + 2)
                        dst = claim("m", k, m)
                        for i in range(TT):
                            last = nc.tensor.matmul(dst[2 * DR:CROSS, i * P:i * P + P],
                                                    shift[:, i, 2 * m:2 * m + 2].bitcast(F32), ident,
                                                    start=True, stop=True)
                        last.then_inc(filled[bank_of[("m", k, m)]], 1)

                    def transposed_scores(k, hd, u):
                        slot = (hd // GH % 2) * GH + hd % GH
                        if u == 0 and hd == 0:
                            pe.wait_ge(s_cross, 64 * (na[k] + 1))
                        if u == 0 and hd % 2 == 0:
                            pe.wait_ge(*read("m", k, hd // 2))
                        dst = claim("sT", k, hd, u)
                        for j in (j for j in (0, 1, 3, 2) if PT_AT[j][0] == u):
                            c, n = PT_AT[j][1], T - j * P
                            keys = slice(j * P, j * P + P)
                            nc.tensor.matmul(dst[:, c:c + n], k_stack[0:ROWS, slot, keys],
                                             q_stack[0:ROWS, slot, j * P:T], start=True, stop=False)
                            nc.tensor.matmul(dst[:, c:c + n], k_cross[0:CROSS, hd % 2, keys],
                                             q_cross[0:CROSS, hd // 2 % 2, j * P:T],
                                             start=False, stop=False)
                            last = nc.tensor.matmul(dst[:, c:c + P], causal_b[:, :], ident_b[:, :],
                                                    start=False, stop=True)
                        last.then_inc(filled[bank_of[("sT", k, hd, u)]], 1)

                    def sum_values(k, parity, hd):
                        if hd % GH == 0:
                            claim("o", k, hd // GH)
                        r = OW * (hd % GH)
                        for u in range(3):
                            pe.wait_ge(*read("sT", k, hd, u))
                        for j in range(TT):
                            u, c = PT_AT[j]
                            last = nc.tensor.matmul(bank[7][r:r + OW, j * P:T],
                                                    v[:, parity, j, hd * VW:hd * VW + OW],
                                                    probs_T[:, hd % 2, 512 * u + c:512 * u + c + T - j * P],
                                                    start=j == 0, stop=j == TT - 1)
                        last.then_inc(s_pv, 1)

                    def attend(k, parity, slot):
                        if nf[k]:
                            for u in range(2):
                                pe.wait_ge(*read("v", k - 1, u))
                        for step in range(STEPS):
                            lagging = LAG <= step < H + LAG
                            if step < H:
                                scores(k, step, 0)
                            slot()
                            if step % 2 == 0 and 2 <= step <= H:
                                shift_rows(k, step // 2 - 1)
                            if step < H:
                                scores(k, step, 1)
                            for u in range(2):
                                if lagging:
                                    transposed_scores(k, step - LAG, u)
                            slot()
                            if step < H:
                                scores(k, step, 2)
                            if lagging:
                                transposed_scores(k, step - LAG, 2)
                            if step > LAG:
                                sum_values(k, parity, step - LAG - 1)
                            slot()

                    def back(k, parity, image):
                        if na[k]:
                            pe.wait_ge(*read("o", k - 1, NG - 1))
                        for i in range(TT):
                            dst = claim("oTok", k, i)
                            for g in range(NG):
                                last = nc.tensor.transpose(dst[:, g * P:g * P + P],
                                                           oT[:, g, i * P:i * P + P], ident)
                            last.then_inc(filled[bank_of[("oTok", k, i)]], 1)
                            yield
                        transpose_features(k, "fT1", xn, s_xn_b, 2 * TT * nb[k])
                        yield
                        features_split(k, "fT1")
                        for u in range(PAIRS):
                            dst = claim("y", k, u)
                            for j in range(2):
                                cols = slice((2 * u + j) * P, (2 * u + j + 1) * P)
                                last = product(dst[:, j * D:j * D + D],
                                               [(fT[c][:, f, cols], weight(w_half[a], "o", f, D, 0, D))
                                                for f in range(FT) for a, c in HALVES])
                            last.then_inc(filled[bank_of[("y", k, u)]], 1)
                            yield
                        yield
                        transpose_features(k, "fT2", xn, s_xn_b, 2 * TT * nb[k] + TT)
                        yield
                        features_split(k, "fT2")

                        def up(p, n):
                            dst = claim("g", k, p, n)
                            for j in range(2):
                                ft = 2 * n + j
                                last = product(dst[:, j * 256:j * 256 + 256],
                                               [(up_T[:, f, ft * P:ft * P + P],
                                                 fT[c][:, f, p * 256:p * 256 + 256])
                                                for f in range(FT) for c in range(2)])
                            last.then_inc(filled[bank_of[("g", k, p, n)]], 1)

                        def down(p, n):
                            u = p * GU + n
                            pe.wait_ge(s_g_split, PAIRS * GU * nb[k] + u + 1)
                            dst = claim("d", k, p)
                            for j in range(2):
                                for i in range(2):
                                    at = j * 256 + i * P
                                    for c, data in enumerate((g_hi, g_lo)):
                                        last = nc.tensor.matmul(
                                            dst[:, i * D:i * D + D], data[:, u % RING, at:at + P],
                                            down_T[:, 2 * n + j, :], start=n + j + i + c == 0,
                                            stop=n == GU - 1 and j + c == 2, skip_group_check=True)
                            last.then_inc(filled[6] if n == GU - 1 else s_down, 1)

                        for p in range(PAIRS):
                            for n in range(0, GU, 2):
                                if n:
                                    down(p, n - 2)
                                    down(p, n - 1)
                                up(p, n)
                                up(p, n + 1)
                                yield
                            down(p, GU - 2)
                            down(p, GU - 1)
                            yield
                            pe.wait_ge(s_g_sum, PAIRS * GU * nb[k] + (p + 1) * GU)
                            dst = claim("ss", k, p)
                            for i in range(2):
                                last = product(dst[:, i:i + 1],
                                               [(g_acc[:, j * 256 + i * P:j * 256 + i * P + P], ones[:, 0:1])
                                                for j in range(2)])
                            last.then_inc(filled[bank_of[("ss", k, p)]], 1)
                            yield
                        yield

                    def front(k, parity, image):
                        def transpose_x(p, n):
                            dst = claim("xT", k, p, n)
                            for j in range(2):
                                for i in range(2):
                                    kt = 2 * n + j
                                    at = j * 256 + i * P
                                    last = nc.tensor.transpose(dst[:, at:at + P],
                                                               x_in[:, 2 * p + i, kt * P:kt * P + P], ident)
                            last.then_inc(filled[bank_of[("xT", k, p, n)]], 1)

                        def tokens(p, n):
                            u = p * XU + n
                            pe.wait_ge(*read("xT", k, p, n))
                            dst = claim("h", k, p)
                            for j in range(2):
                                for i in range(2):
                                    at = j * 256 + i * P
                                    for c, (data, w) in enumerate(((xT_hi, tok_hi), (xT_hi, tok_lo),
                                                                   (xT_lo, tok_hi))):
                                        last = nc.tensor.matmul(
                                            dst[:, i * D:i * D + D], data[:, u % RING, at:at + P],
                                            w[:, 2 * n + j, :], start=n + j + i + c == 0,
                                            stop=n == XU - 1 and j == 1 and c == 2, skip_group_check=True)
                            last.then_inc(filled[6] if n == XU - 1 else s_tok_used, 1)

                        pe.wait_ge(s_x, 16 * (image + 1))
                        units = [(p, n) for p in range(PAIRS) for n in range(XU)]
                        for n, unit in enumerate(units):
                            if n >= 2:
                                tokens(*units[n - 2])
                            transpose_x(*unit)
                            yield
                        for unit in units[-2:]:
                            tokens(*unit)
                            yield
                        yield
                        transpose_features(k, "fT0", xn_next, s_xn_a, TT * nf[k])
                        yield
                        features_split(k, "fT0")
                        fill(("c", k), claim("c", k)[:, :], from_features("kv_down", DC, 0))
                        yield
                        for t in range(FT):
                            fill(("q", k, t), claim("q", k, t)[:, :], from_features("q", D, t * P))
                            yield
                        pe.wait_ge(*read("c", k))
                        for t in range(FT):
                            fill(("k", k, t), claim("k", k, t)[:, :], from_latent("k_up", t * P))
                            yield
                        fill(("rot", k), claim("rot", k)[:, :],
                             from_features("rot_q", P, 0) + from_latent("rot_k", 0))
                        yield
                        for u in range(2):
                            dst = claim("v", k, u)
                            for i in range(2):
                                cols = slice((2 * u + i) * P, (2 * u + i + 1) * P)
                                last = product(dst[:, i * D:i * D + D],
                                               [(cT[c][:, cols], weight(w_half[a], "v_up", 0, 0, 0, D))
                                                for a, c in HALVES])
                            last.then_inc(filled[bank_of[("v", k, u)]], 1)
                            yield
                        pe.wait_ge(*read("rot", k))
                        fill(("rope", k), claim("rope", k)[0:2 * DR, :], [(table("fold"), prod[:, :])])
                        yield
                        for t in range(FT):
                            pe.wait_ge(*read("q", k, t))
                        dst = claim("s0", k)
                        for i in range(TT):
                            cols = slice(i * P, i * P + P)
                            last = product(dst[:, i * H:i * H + H],
                                           [(qk[:, 0, c, t, cols], (k0_hi, k0_lo)[a][:, t, :])
                                            for t in range(FT) for a, c in HALVES]
                                           + [(prod[:, cols], k0_rope[:, :])])
                        last.then_inc(filled[bank_of[("s0", k)]], 1)
                        yield

                    run_parts(attend, back, front)

            nc.all_engine_barrier(sems_to_clear=range(numbers[0], numbers[-1] + 1))

        def part(attend=None, back=None, front=None):
            def image(b):
                return None if b is None else b if isinstance(b, tuple) else (b % 2, b)
            return {"attend": image(attend), "back": image(back), "front": image(front)}

        images([part(front=0)])
        images([part(attend=0, front=1)])
        with nc.Fori(1, B - 1, 2) as b:
            images([part(attend=(1, b), back=(0, b - 1), front=(0, b + 1)),
                    part(attend=(0, b + 1), back=(1, b), front=(1, b + 2))])
        images([part(attend=B - 1, back=B - 2)])
        images([part(back=B - 1)])
        nc.sync.wait_ge(s_stored, 16 * B + 16 * PAIRS * B)
        nc.sync.wait_ge(s_x, 16 * (B + 1))

_INS = ["x", "cls_tok", "L0_tok_weight", "L0_tok_weighted_sum", "L0_attn_W_kv_down", "L0_attn_W_k_up",
        "L0_attn_W_v_up", "L0_attn_W_q", "L0_attn_W_q_rope", "L0_attn_W_k_rope", "L0_attn_W_o",
        "L0_ffn_w_up", "L0_ffn_w_down"]


def shape_constants(head_count, tokens, head_dim, rope_dim):
    import numpy as np

    at, width = constant_layout(head_count, tokens)
    c = np.zeros((P, width), np.float32)

    def put(name, value):
        first, n = at[name]
        c[:value.shape[0], first:first + n] = value

    r = np.arange(P)
    put("identity", np.eye(P, dtype=np.float32))
    put("causal", np.where(r[None, :] > r[:, None], np.float32(MASKED), np.float32(0)))
    fold = np.zeros((P, 2 * rope_dim), np.float32)
    select = np.zeros((P, 2), np.float32)
    for j in range(2 * rope_dim):
        fold[2 * rope_dim * (j // rope_dim) + j % rope_dim, j] = 1
        fold[2 * rope_dim * (j // rope_dim) + rope_dim + j % rope_dim, j] = 1
    put("fold", fold)
    for j in range(2):
        select[2 * rope_dim + j, j] = 1
    put("select", select)
    head_of = np.zeros((P, 2, head_count), np.float32)
    for t in range(2):
        head_of[r, t, (t * P + r) // head_dim] = 1
    put("head_of", head_of.reshape(P, -1))
    put("powers", np.tile(np.repeat(np.float32([-0.5, 0.5]), 4), (P, 1)))
    put("ones", np.ones((P, P), np.float32))
    inv_freq = np.float32(1.0) / np.float32(10000.0) ** (
        np.arange(0, rope_dim, 2, dtype=np.float32) / np.float32(rope_dim))
    angles = np.outer(inv_freq, np.arange(1, tokens + 1, dtype=np.float32)).astype(np.float32)
    cos, sin = np.cos(angles), np.sin(angles)
    put("rope", np.concatenate([cos, cos, sin, sin] * 2, axis=0))
    return c


def kernel(**inputs):
    import numpy as np
    import concourse.bacc as bacc
    from concourse.bass_utils import run_bass_kernel_spmd as run

    nc = bacc.Bacc("TRN2", target_bir_lowering=False, num_devices=1)
    arrays, args = {}, []
    for name in _INS:
        a = np.ascontiguousarray(inputs[name])
        arrays[f"in_{name}"] = a
        args.append(nc.dram_tensor(f"in_{name}", a.shape, mybir.dt.from_np(a.dtype), kind="ExternalInput").ap())
    batch, tokens, dim, _ = inputs["x"].shape
    heads = 16
    c = shape_constants(heads, tokens, dim // heads, inputs["L0_attn_W_q_rope"].shape[1])
    arrays["in_constants"] = c
    args.append(nc.dram_tensor("in_constants", c.shape, F32, kind="ExternalInput").ap())
    args.append(nc.dram_tensor("out_0", (batch, tokens + 1, dim), F32, kind="ExternalOutput").ap())
    vit_tower_kernel(nc, *args)
    r = run(nc, [arrays], core_ids=[0])
    return r.results[0]["out_0"]
```

```python
from contextlib import ExitStack

import concourse.bass as bass
from concourse import mybir

F32 = mybir.dt.float32
F32R = mybir.dt.float32r
BF16 = mybir.dt.bfloat16
ALU = mybir.AluOpType
ACT = mybir.ActivationFunctionType
AX_X = mybir.AxisListType.X

P = 128
LN_EPS = 1e-5
RMS_EPS = 1e-8
MASKED = -1e30


def constant_layout(head_count, tokens):
    widths = {"identity": P, "causal": P, "fold": 64, "select": 2, "head_of": 2 * head_count,
              "ones": P, "powers": 8, "rope": tokens}
    at, first = {}, 0
    for name, width in widths.items():
        at[name] = (first, width)
        first += width
    return at, first


def vit_tower_kernel(nc, x, cls_tok, tok_weight, tok_sum, w_kv_down, w_k_up, w_v_up, w_q,
                     w_q_rope, w_k_rope, w_o, w_ffn_up, w_ffn_down, constants, out):
    B, T, _, DIN = x.shape
    D = cls_tok.shape[2]
    DC = w_kv_down.shape[1]
    DR = w_q_rope.shape[1]
    FF = w_ffn_up.shape[0]
    H = 16
    HD = D // H
    TT = T // P
    FT = D // P
    KT = D * DIN // P
    GT = FF // P
    HALF = DR // 2
    GH = 4
    NG = H // GH
    SCALE = float(HD + DR) ** -0.5
    CONTENT = 3 * HD
    ROWS = CONTENT + DR
    CROSS = 2 * DR + 2
    LAG = 3
    VW = HD + 1
    OW = 32
    RING = 2
    at, n_const = constant_layout(H, T)

    PAIRS = TT // 2
    XU = KT // 2
    GU = GT // 2

    S_AT = {0: (0, 3 * P), 2: (0, 0), 3: (1, 0), 1: (2, 0)}
    PT_AT = {0: (0, 0), 1: (1, P), 3: (1, 0), 2: (2, 0)}
    S_ORDER = (2, 0, 3, 1)
    PT_UNITS = (512, 512, 256)
    PW = sum(PT_UNITS)

    ctx = ExitStack()
    with ctx:
        def sb(name, shape, dt=F32):
            return ctx.enter_context(nc.sbuf_tensor(name, shape, dt))

        def sem(name):
            return ctx.enter_context(nc.semaphore(name))

        bank = [ctx.enter_context(nc.psum_tensor(f"bank{n}", [P, 512], F32)) for n in range(8)]

        const = sb("const", [P, n_const])

        def table(name):
            first, width = at[name]
            return const[:, first:first + width]

        ident = table("identity")
        ones = table("ones")
        powers = table("powers").rearrange("p (k i) -> p k i", k=2)
        ident_b = sb("ident_b", [P, P], BF16)
        causal_b = sb("causal_b", [P, P], BF16)
        tok_hi = sb("tok_hi", [P, KT, D], F32R)
        tok_lo = sb("tok_lo", [P, KT, D], F32R)
        widths = {"kv_down": FT * DC, "k_up": D, "v_up": D, "q": FT * D, "o": FT * D,
                  "rot_q": FT * P, "rot_k": P}
        w_at, n_w = {}, 0
        for name, width in widths.items():
            w_at[name] = n_w
            n_w += width
        w_hi = sb("w_hi", [P, n_w], F32R)
        w_lo = sb("w_lo", [P, n_w], F32R)
        up_T = sb("up_T", [P, FT, FF], F32R)
        down_T = sb("down_T", [P, GT, D], F32R)
        k0_hi = sb("k0_hi", [P, FT, H], F32R)
        k0_lo = sb("k0_lo", [P, FT, H], F32R)
        k0_rope = sb("k0_rope", [P, H])
        v0_all = sb("v0_all", [P, D])

        def weight(half, name, tile, width, first, count):
            a = w_at[name] + tile * width + first
            return half[:, a:a + count]

        x_in = sb("x_in", [P, TT, D * DIN])
        xT_hi = sb("xT_hi", [P, RING, T], F32R)
        xT_lo = sb("xT_lo", [P, RING, T], F32R)
        h = sb("h", [P, 2, TT, D])
        h_next = sb("h_next", [P, TT, D])
        xn = sb("xn", [P, TT, D])
        xn_next = sb("xn_next", [P, TT, D])
        fT_hi = sb("fT_hi", [P, FT, T], F32R)
        fT_lo = sb("fT_lo", [P, FT, T], F32R)
        latent = sb("latent", [P, 2, T], F32R)
        cT_hi, cT_lo = latent[:, 0, :], latent[:, 1, :]
        qk = sb("qk", [P, 2, 2, FT, T], F32R)
        q_stack = sb("q_stack", [P, 2 * GH, T], F32R)
        k_stack = sb("k_stack", [P, 2 * GH, T], F32R)
        prod = sb("prod", [P, T])
        rope = sb("rope", [2 * DR, 2, T], F32R)
        q_cross = sb("q_cross", [P, 2, T], F32R)
        k_cross = sb("k_cross", [P, 2, T], F32R)
        v = sb("v", [P, 2, TT, H * VW + OW - VW])
        probs_T = sb("probs_T", [P, 2, PW])
        oT = sb("oT", [P, NG, T])
        g_sb = sb("g_sb", [P, RING, T])
        g_sq = sb("g_sq", [P, T])
        g_halves = qk[:, :, :, :, :].rearrange("p w a t n -> p (w a t) n")
        g_hi = g_halves[:, 0:RING, :]
        g_lo = g_halves[:, RING:2 * RING, :]
        g_acc = prod
        stats = sb("stats", [P, TT, 6])
        moments = sb("moments", [P, TT, 2])
        stats_next = sb("stats_next", [P, TT, 6])
        moments_next = sb("moments_next", [P, TT, 2])
        col = sb("col", [P, 2, TT])
        base = sb("base", [P, 2, TT])
        root = sb("root", [P, 2, TT])
        base_next = sb("base_next", [P, 1, TT])
        root_next = sb("root_next", [P, 1, TT])
        neg_s0 = sb("neg_s0", [P, 2, TT, H])
        row_max = sb("row_max", [P, 2, TT])
        shift = sb("shift", [P, TT, H], F32R)
        p0 = sb("p0", [P, TT, H])
        p0_v0 = g_sb[:, :, :].rearrange("p s n -> p (s n)").rearrange("p (i n) -> p i n", n=D)
        denom = sb("denom", [P, TT, H])
        recip = sb("recip", [P, TT, H])

        x_sum = h[:, 0].rearrange("p i n -> p (i n)")[:, 0:FT * D] \
            .rearrange("p (t i) -> p t i", t=FT)
        x_wt = col[:, :, :]
        x_flat = x_in[:, :, :].rearrange("p i n -> p (i n)")
        tok_prod = x_flat[:, 0:FT * D * DIN].rearrange("p (t n) -> p t n", t=FT)
        down_raw = x_flat[:, FT * D * DIN:FT * D * DIN + FT * FF]
        up_raw = probs_T[:, :, :].rearrange("p s n -> p (s n)")[:, 0:GT * D]
        above = oT[:, :, :].rearrange("p g n -> p (g n)")
        w_raw = v[:, :, :, :].rearrange("p b i n -> p (b i n)")[:, 0:n_w]
        row = xn
        w_rope_raw = g_sb[:, 0, 0:FT * DR].rearrange("p (t n) -> p t n", n=DR)
        w_rope_k_raw = g_sb[:, 1, 0:DR]
        k_rope_twice = g_sq[:, 0:P]
        tiny = denom[:, :, :].rearrange("p i n -> p (i n)")

        scratch = nc.dram_tensor("qk_scratch", [2, 2, 2, FT, P, T], F32, kind="Internal").ap()
        rope_scratch = nc.dram_tensor("rope_scratch", [2, 2, DR, 2, T], F32, kind="Internal").ap()

        s_weights = sem("weights_loaded")
        s_x = sem("x_loaded")
        s_stored = sem("rows_stored")
        s_tok_prod = sem("tok_product_ready")
        s_abs = sem("abs_sums_ready")
        s_total = sem("abs_total_ready")
        s_ternary = sem("ternary_ready")
        s_setup_full = sem("setup_bank_filled")
        s_setup_hi = sem("setup_bank_copied")
        s_setup_lo = sem("setup_low_half_ready")
        s_weight_raw = sem("rotary_weights_ready")
        s_weight_hi = sem("weight_hi_ready")
        s_weight_lo = sem("weight_lo_ready")
        s_setup_dve = sem("setup_vector_step")
        s_setup_base = sem("setup_power_base_ready")
        s_setup_root = sem("setup_power_ready")
        s_cls_pe = sem("cls_product_ready")
        s_cls_dve = sem("cls_operand_ready")
        s_cls_act = sem("cls_gelu_ready")

        filled = [sem(f"bank{n}_filled") for n in range(8)]
        drained = [sem(f"bank{n}_drained") for n in range(8)]
        s_xT_hi = sem("xT_hi_ready")
        s_tok_used = sem("xT_used")
        s_xn_a = sem("normed_tokens_ready")
        s_xn_b = sem("normed_attention_ready")
        s_fT_hi = sem("fT_hi_ready")
        s_half = sem("proj_hi_ready")
        s_scratch = sem("scratch_written")
        s_stack = [sem(f"stack{n}_loaded") for n in range(2)]
        s_cross = sem("cross_rows_loaded")
        s_shift = sem("shift_ready")
        s_shift_row = sem("shift_rows_ready")
        s_pv = sem("values_summed")
        s_p0_in = sem("p0_exponent_ready")
        s_p0 = sem("p0_ready")
        s_p0v0 = sem("p0_v0_ready")
        s_g_split = sem("g_split_ready")
        s_g_sum = sem("g_squares_summed")
        s_g_sq = sem("g_squares_ready")
        s_down = sem("down_used")
        s_out = sem("out_rows_ready")
        s_base = sem("power_base_ready")
        s_root = sem("power_ready")
        s_base_next = sem("next_power_base_ready")
        s_root_next = sem("next_power_ready")
        s_h_moved = sem("next_tokens_moved")
        s_dve = sem("vector_step")
        cleared = [*filled, *drained, s_xT_hi, s_tok_used, s_xn_a, s_xn_b, s_fT_hi, s_half, s_scratch,
                   *s_stack, s_cross, s_shift, s_shift_row, s_pv, s_p0_in, s_p0, s_p0v0, s_g_split, s_g_sum, s_g_sq, s_down,
                   s_out, s_base, s_root, s_base_next, s_root_next, s_h_moved, s_dve]
        numbers = sorted(s.num for s in cleared)
        assert numbers == list(range(numbers[0], numbers[0] + len(numbers)))

        HALVES = ((0, 0), (1, 0), (0, 1))
        w_half = (w_hi, w_lo)
        x_tiles = x.rearrange("b (i p) c d -> b p i (c d)", p=P)
        out_tiles = out[:, 1:T + 1, :].rearrange("b (i p) n -> b p i n", p=P)
        SETUP_UNITS = 4 + 8
        N_WEIGHTS = 13

        with nc.Block() as block:

            @block.sync
            def _(sp):
                def load(dst, src):
                    sp.dma_start(dst, src).then_inc(s_weights, 16)

                load(const[:, :], constants)
                load(x_sum, tok_sum.rearrange("(t p) i -> p t i", p=P))
                load(x_wt[:, :, :], tok_weight.rearrange("(t p) d -> p t d", p=P))
                load(up_raw.rearrange("p (t n) -> p t n", n=D),
                     w_ffn_up.rearrange("(t p) n -> p t n", p=P))
                load(down_raw.rearrange("p (t n) -> p t n", n=FF),
                     w_ffn_down.rearrange("(t p) n -> p t n", p=P))

                def raw(name, t, n):
                    return w_raw[:, w_at[name]:w_at[name] + t * n].rearrange("p (t n) -> p t n", n=n)

                load(raw("kv_down", FT, DC), w_kv_down.rearrange("(t p) n -> p t n", p=P))
                load(raw("k_up", 1, D)[:, 0, :], w_k_up)
                load(raw("v_up", 1, D)[:, 0, :], w_v_up)
                load(raw("q", FT, D), w_q.rearrange("(t p) n -> p t n", p=P))
                load(raw("o", FT, D), w_o.rearrange("(t p) n -> p t n", p=P))
                load(w_rope_raw, w_q_rope.rearrange("(t p) n -> p t n", p=P))
                load(w_rope_k_raw, w_k_rope)
                load(row[0:1, 0, :], cls_tok[0])
                sp.wait_ge(s_setup_full, SETUP_UNITS)
                sp.dma_start(x_in[:, :, :],
                             x_tiles[0:1].rearrange("b p i n -> p (b i) n")).then_inc(s_x, 16)
                sp.wait_ge(s_cls_dve, 11)
                for b in range(B):
                    sp.dma_start(out[b, 0:1, :], row[0:1, 2, :]).then_inc(s_stored, 16)
                sp.wait_ge(s_stored, 16 * B)

            @block.gpsimd
            def _(pool):
                pool.wait_ge(s_weights, 16 * N_WEIGHTS)
                for n in range(3):
                    pool.wait_ge(s_setup_base, n + 1)
                    nc.gpsimd.tensor_tensor(root[0:1, :, 0:1], base[0:1, :, 0:1], powers[0:1, :, 0:1],
                                            ALU.pow).then_inc(s_setup_root, 1)
                    if n == 1:
                        pool.wait_ge(s_weight_lo, 1)
                        pool.wait_ge(s_cls_pe, 4)
                        nc.gpsimd.memset(v[:, :, :, :], 1.0)

            @block.vector
            def _(dve):
                steps = [0]

                def link(ins):
                    steps[0] += 1
                    ins.then_inc(s_setup_dve, 1)
                    dve.wait_ge(s_setup_dve, steps[0])

                dve.wait_ge(s_weights, 16 * N_WEIGHTS)
                for t in range(FT):
                    for d in range(DIN):
                        last = nc.vector.tensor_scalar(
                            tok_prod[:, t, :].rearrange("p (i d) -> p i d", d=DIN)[:, :, d],
                            x_sum[:, t, :], x_wt[:, t, d:d + 1], None, ALU.mult)
                last.then_inc(s_tok_prod, 1)
                nc.vector.tensor_reduce(tiny[:, 0:1], up_raw, AX_X, ALU.add,
                                        apply_absolute_value=True)
                nc.vector.tensor_reduce(tiny[:, 1:2], down_raw, AX_X, ALU.add,
                                        apply_absolute_value=True).then_inc(s_abs, 1)
                nc.vector.tensor_copy(ident_b[:, :], ident)
                nc.vector.tensor_copy(causal_b[:, :], table("causal"))
                for j in range(2):
                    nc.vector.tensor_copy(
                        k_cross[2 * DR:CROSS, j, :],
                        table("select")[2 * DR:CROSS, j:j + 1].broadcast_to([2, T]))
                a, k = w_at["rot_q"], w_at["rot_k"]
                nc.vector.memset(k_rope_twice, 0.0)
                link(nc.vector.memset(w_raw[:, a:n_w], 0.0))
                rq = w_raw[:, a:a + FT * P].rearrange("p (t n) -> p t n", n=P)
                sq = w_rope_raw
                nc.vector.tensor_copy(rq[:, :, 0:DR], sq)
                nc.vector.tensor_scalar(rq[:, :, DR:DR + HALF], sq[:, :, HALF:DR], -1.0, None, ALU.mult)
                nc.vector.tensor_copy(rq[:, :, DR + HALF:2 * DR], sq[:, :, 0:HALF])
                rk = w_raw[:, k + 2 * DR:k + 4 * DR]
                sk = w_rope_k_raw
                nc.vector.tensor_copy(rk[:, 0:DR], sk)
                nc.vector.tensor_scalar(rk[:, DR:DR + HALF], sk[:, HALF:DR], -1.0, None, ALU.mult)
                nc.vector.tensor_copy(k_rope_twice[:, 0:2 * DR].rearrange("p (r n) -> p r n", r=2),
                                      sk.unsqueeze(1).broadcast_to([P, 2, DR]))
                nc.vector.tensor_copy(rk[:, DR + HALF:2 * DR], sk[:, 0:HALF]).then_inc(s_weight_raw, 1)
                dve.wait_ge(s_total, 1)
                link(nc.vector.tensor_scalar(tiny[:, 2:4], bank[7][:, 0:2], 1.0 / (D * FF), 0.5,
                                             ALU.mult, ALU.mult))
                link(nc.vector.tensor_scalar(tiny[:, 4:6], tiny[:, 2:4], -1.0, None, ALU.mult))
                for n, w in enumerate((up_raw, down_raw)):
                    link(nc.vector.tensor_scalar(above, w, tiny[:, 2 + n:3 + n], None, ALU.is_gt))
                    last = nc.vector.scalar_tensor_tensor(
                        out=w, in0=w, scalar=tiny[:, 4 + n:5 + n], in1=above,
                        op0=ALU.is_lt, op1=ALU.subtract)
                    link(last)
                    nc.vector.tensor_scalar(w, w, -1.0, None, ALU.mult).then_inc(s_ternary, 1)
                for n in range(4):
                    dve.wait_ge(s_setup_hi, n + 1)
                    kt = 2 * n
                    nc.vector.tensor_tensor(
                        tok_lo[:, kt:kt + 2, :],
                        bank[n][:, :].rearrange("p (k o) -> p k o", k=2),
                        tok_hi[:, kt:kt + 2, :].bitcast(F32), ALU.subtract).then_inc(s_setup_lo, 1)
                dve.wait_ge(s_weight_hi, 1)
                nc.vector.tensor_tensor(w_lo[:, :], w_raw[:, :], w_hi[:, :].bitcast(F32),
                                        ALU.subtract).then_inc(s_weight_lo, 1)

                raised = [0]

                def raise_base(values):
                    for n, (value, eps) in enumerate(values):
                        last = nc.vector.tensor_scalar(base[0:1, n, 0:1], value, eps, None, ALU.add)
                    last.then_inc(s_setup_base, 1)
                    raised[0] += 1
                    dve.wait_ge(s_setup_root, raised[0])

                def norm_row(src, dst, rms):
                    link(nc.vector.bn_stats(stats[0:1, 0, :], src))
                    link(nc.vector.bn_aggr(moments[0:1, 0, :], stats[0:1, 0, :]))
                    scale = root[0:1, 0, 0:1]
                    raise_base([(moments[0:1, 0, 1:2], LN_EPS), (moments[0:1, 0, 1:2], 0.0)])
                    if rms:
                        scale = col[0:1, 0, 0:1]
                        link(nc.vector.tensor_tensor(scale, root[0:1, 0, 0:1], root[0:1, 1, 0:1], ALU.mult))
                        link(nc.vector.tensor_scalar(scale, scale, RMS_EPS, None, ALU.add))
                        link(nc.vector.reciprocal(scale, scale))
                        link(nc.vector.tensor_tensor(scale, root[0:1, 0, 0:1], scale, ALU.mult))
                    nc.vector.tensor_scalar(dst, src, moments[0:1, 0, 0:1], scale,
                                            ALU.subtract, ALU.mult).then_inc(s_cls_dve, 1)

                norm_row(row[0:1, 0, :], row[0:1, 2, :], False)
                dve.wait_ge(s_cls_pe, 1)
                nc.vector.tensor_copy(tiny[:, 8:10], bank[7][:, 8:10]).then_inc(s_cls_dve, 1)
                dve.wait_ge(s_cls_pe, 2)
                nc.vector.tensor_copy(tiny[:, 10:11], bank[7][:, 10:11]).then_inc(s_cls_dve, 1)
                dve.wait_ge(s_cls_pe, 3)
                head_of = table("head_of").rearrange("p (t n) -> p t n", t=FT)
                blk = tiny[:, 16:48].rearrange("p (t n) -> p t n", t=FT)
                nc.vector.tensor_copy(tiny[:, 11:14], bank[7][:, 11:14])
                nc.vector.tensor_copy(tiny[:, 14:16], bank[7][:, 14:16])
                link(nc.vector.tensor_copy(row[0:1, 3, :], bank[7][0:1, 256:512]))
                for t in range(FT):
                    last = nc.vector.tensor_scalar(blk[:, t, :], head_of[:, t, :],
                                                   tiny[:, 11 + t:12 + t], None, ALU.mult)
                link(last)
                link(nc.vector.tensor_copy(k0_hi[:, :, :], blk))
                nc.vector.tensor_tensor(k0_lo[:, :, :], blk, k0_hi[:, :, :].bitcast(F32), ALU.subtract)
                nc.vector.tensor_copy(k0_rope[:, :],
                                      tiny[:, 13:14].broadcast_to([P, H])).then_inc(s_cls_dve, 1)
                dve.wait_ge(s_cls_pe, 4)
                nc.vector.tensor_copy(v0_all[:, :], bank[6][:, 0:D])
                link(nc.vector.tensor_tensor(row[0:1, 1, :], bank[6][0:1, 256:512], row[0:1, 0, :],
                                             ALU.add))
                norm_row(row[0:1, 1, :], row[0:1, 2, :], True)
                dve.wait_ge(s_cls_pe, 5)
                nc.vector.tensor_copy(tiny[:, 8:10], bank[7][:, 8:10]).then_inc(s_cls_dve, 1)
                dve.wait_ge(s_cls_act, 1)
                link(nc.vector.tensor_tensor(tiny[:, 56:64], tiny[:, 48:56], tiny[:, 48:56], ALU.mult))
                nc.vector.reduce_sum(tiny[:, 0:1], tiny[:, 56:64], AX_X).then_inc(s_cls_dve, 1)
                dve.wait_ge(s_cls_pe, 7)
                link(nc.vector.tensor_scalar(tiny[0:1, 1:2], bank[7][0:1, 20:21], 1.0 / FF, None,
                                             ALU.mult))
                raise_base([(tiny[0:1, 1:2], 1.0), (tiny[0:1, 1:2], 0.0)])
                link(nc.vector.tensor_scalar(tiny[0:1, 1:2], root[0:1, 1, 0:1], RMS_EPS, None, ALU.add))
                link(nc.vector.reciprocal(tiny[0:1, 2:3], tiny[0:1, 1:2]))
                last = nc.vector.scalar_tensor_tensor(
                    out=row[0:1, 2, :], in0=bank[7][0:1, 256:512], scalar=tiny[0:1, 2:3],
                    in1=row[0:1, 1, :], op0=ALU.mult, op1=ALU.add)
                link(last)
                for _ in range(4):
                    nc.vector.engine_nop().then_inc(s_cls_dve, 1)

            @block.scalar
            def _(act):
                for n in range(SETUP_UNITS):
                    act.wait_ge(s_setup_full, n + 1)
                    if n < 4:
                        dst = tok_hi[:, 2 * n:2 * n + 2, :]
                    elif n < 8:
                        t, half = divmod(n - 4, 2)
                        dst = up_T[:, t:t + 1, 512 * half:512 * half + 512]
                    else:
                        dst = down_T[:, 2 * (n - 8):2 * (n - 8) + 2, :]
                    src = bank[n % 4][:, :].rearrange("p (k o) -> p k o", k=dst.shape[1])
                    nc.scalar.activation(dst, src, ACT.Copy).then_inc(s_setup_hi, 1)
                    if n == 3:
                        act.wait_ge(s_weight_raw, 1)
                        nc.scalar.activation(w_hi[:, :], w_raw[:, :], ACT.Copy).then_inc(s_weight_hi, 1)
                act.wait_ge(s_cls_pe, 6)
                nc.scalar.activation(tiny[:, 48:56], bank[7][:, 48:56], ACT.Gelu).then_inc(s_cls_act, 1)

            @block.tensor
            def _(pe):
                pe.wait_ge(s_weights, 16 * N_WEIGHTS)
                pe.wait_ge(s_abs, 1)
                nc.tensor.matmul(bank[7][:, 0:2], ones, tiny[:, 0:2], start=True,
                                 stop=True).then_inc(s_total, 1)
                pe.wait_ge(s_tok_prod, 1)
                for n in range(SETUP_UNITS):
                    if n >= 4:
                        pe.wait_ge(s_setup_hi, n - 3)
                    if 4 <= n < 8:
                        pe.wait_ge(s_setup_lo, n - 3)
                    if n == 4:
                        pe.wait_ge(s_ternary, 1)
                    if n == 8:
                        pe.wait_ge(s_ternary, 2)
                    for j in range(4):
                        if n < 4:
                            kt, t = 2 * n + j // 2, j % 2
                            src = tok_prod[:, t, kt * P:kt * P + P]
                        elif n < 8:
                            t, half = divmod(n - 4, 2)
                            src = up_raw[:, (4 * half + j) * D + t * P:(4 * half + j) * D + t * P + P]
                        else:
                            gt, t = 2 * (n - 8) + j // 2, j % 2
                            src = down_raw[:, t * FF + gt * P:t * FF + gt * P + P]
                        last = nc.tensor.transpose(bank[n % 4][:, j * P:j * P + P], src, ident)
                    last.then_inc(s_setup_full, 1)

                def mm(dst, pairs):
                    for n, (a, b) in enumerate(pairs):
                        last = nc.tensor.matmul(dst, a, b, start=n == 0, stop=n == len(pairs) - 1)
                    return last

                def raw(name, tile, width, first, count):
                    return weight(w_raw, name, tile, width, first, count)

                one = ones[0:1, 0:1]
                pe.wait_ge(s_weight_raw, 1)
                pe.wait_ge(s_cls_dve, 1)
                for t in range(FT):
                    last = mm(bank[7][:, 8 + t:9 + t], [(row[0:1, 2, t * P:t * P + P], one)])
                last.then_inc(s_cls_pe, 1)
                pe.wait_ge(s_cls_dve, 2)
                mm(bank[7][:, 10:11], [(raw("kv_down", t, DC, 0, DC), tiny[:, 8 + t:9 + t])
                                       for t in range(FT)]).then_inc(s_cls_pe, 1)
                pe.wait_ge(s_cls_dve, 3)
                c0 = tiny[:, 10:11]
                mm(bank[7][0:1, 256:512], [(c0, raw("v_up", 0, D, 0, D))])
                for t in range(FT):
                    mm(bank[7][:, 11 + t:12 + t], [(raw("k_up", 0, D, t * P, P), c0)])
                for t in range(FT):
                    mm(bank[7][:, 14 + t:15 + t], [(raw("v_up", 0, D, t * P, P), c0)])
                mm(bank[7][:, 13:14], [(k_rope_twice, c0)]).then_inc(s_cls_pe, 1)
                pe.wait_ge(s_cls_dve, 4)
                mm(bank[6][:, 0:D], [(ones[0:1, :], row[0:1, 3, :])])
                mm(bank[6][0:1, 256:512], [(tiny[:, 14 + t:15 + t], raw("o", t, D, 0, D))
                                           for t in range(FT)]).then_inc(s_cls_pe, 1)
                pe.wait_ge(s_cls_dve, 5)
                for t in range(FT):
                    last = mm(bank[7][:, 8 + t:9 + t], [(row[0:1, 2, t * P:t * P + P], one)])
                last.then_inc(s_cls_pe, 1)
                pe.wait_ge(s_cls_dve, 6)
                pe.wait_ge(s_setup_hi, SETUP_UNITS)
                for ft in range(GT):
                    last = mm(bank[7][:, 48 + ft:49 + ft],
                              [(up_T[:, t, ft * P:ft * P + P].bitcast(F32), tiny[:, 8 + t:9 + t])
                               for t in range(FT)])
                last.then_inc(s_cls_pe, 1)
                pe.wait_ge(s_cls_dve, 7)
                pe.wait_ge(s_cls_act, 1)
                mm(bank[7][0:1, 20:21], [(tiny[:, 0:1], ones[:, 0:1])])
                mm(bank[7][0:1, 256:512], [(tiny[:, 48 + ft:49 + ft], down_T[:, ft, :].bitcast(F32))
                                           for ft in range(GT)]).then_inc(s_cls_pe, 1)

        SLOTS = 3 * H
        SCHEDULE = ("f f . f f . f f f f . f f f . f "
                    "b f b f bf b f f f b fb f b f bf b "
                    "b . b . b . b . b . b . b . b b").split()
        BACK, FRONT = TT + 4 + PAIRS * (GU // 2 + 3), PAIRS * XU + 14
        assert len(SCHEDULE) == SLOTS and "".join(SCHEDULE).count("b") == BACK
        assert "".join(SCHEDULE).count("f") == FRONT

        def images(parts):
            bank_of, fill_of, read_of, before = {}, {}, {}, {}
            fills, reads = [0] * 8, [0] * 8

            def place(unit, n, own_fill=True):
                bank_of[unit], before[unit] = n, reads[n]
                fills[n] += own_fill
                reads[n] += 1
                fill_of[unit], read_of[unit] = fills[n], reads[n]

            turn = {0: 0, 2: 0, 4: 0}

            def place_in_turn(unit, n):
                place(unit, n + turn[n] % 2)
                turn[n] += 1

            def place_turn(unit):
                place_in_turn(unit, 4)

            stack_load, loads = {}, [0, 0]

            def place_stack(k, g):
                loads[g % 2] += (6 if g >= 2 else 8) * 16
                stack_load[(k, g)] = loads[g % 2]

            raises, raised = {}, [0]

            def place_raise(*norm):
                raised[0] += 1
                raises[norm] = raised[0]

            def place_back(k):
                for i in range(TT):
                    place_turn(("oTok", k, i))
                    yield
                for f in range(FT):
                    place_turn(("fT1", k, f))
                yield
                for u in range(PAIRS):
                    place_turn(("y", k, u))
                    yield
                yield
                for f in range(FT):
                    place_turn(("fT2", k, f))
                yield
                for p in range(PAIRS):
                    for n in range(GU):
                        place_turn(("g", k, p, n))
                        if n % 2:
                            yield
                    yield
                    place(("d", k, p), 6)
                    place_turn(("ss", k, p))
                    yield
                yield

            def place_front(k):
                for p in range(PAIRS):
                    for n in range(XU):
                        place_turn(("xT", k, p, n))
                        yield
                    place(("h", k, p), 6)
                yield
                yield
                yield
                for f in range(FT):
                    place_turn(("fT0", k, f))
                yield
                for unit in (("c", k), ("q", k, 0), ("q", k, 1), ("k", k, 0), ("k", k, 1),
                             ("rot", k), ("v", k, 0), ("v", k, 1), ("rope", k), ("s0", k)):
                    place_turn(unit)
                    yield

            attended = [k for k, part in enumerate(parts) if part["attend"]]

            def head_at(step):
                if 0 <= step < H * len(attended):
                    return attended[step // H], step % H

            def pair_at(step):
                if step % 2 == 0 and head_at(step - 1):
                    k, hd = head_at(step - 1)
                    return k, hd // 2

            def steps_of(k):
                first = H * attended.index(k)
                return range(first, first + H + (LAG + 1) * (k == attended[-1]))

            for step in range(H * len(attended) + 1):
                if head_at(step):
                    place_in_turn(("s", *head_at(step), 0), 0)
                if pair_at(step):
                    place_in_turn(("m", *pair_at(step)), 0)
                if head_at(step):
                    place_in_turn(("s", *head_at(step), 1), 0)
                    place_in_turn(("s", *head_at(step), 2), 0)
                    for u in range(3):
                        place_in_turn(("sT", *head_at(step), u), 2)
            for k, part in enumerate(parts):
                if part["attend"]:
                    for g in range(NG):
                        place(("o", k, g), 7, own_fill=False)
                    for g in range(1, NG):
                        place_stack(k, g)
                fillers = {"b": place_back(k), "f": place_front(k)}
                for which in "".join(SCHEDULE):
                    if which in fillers and part[{"b": "back", "f": "front"}[which]]:
                        next(fillers[which])
                if part["back"]:
                    place_raise("back", k)
                    for p in range(PAIRS):
                        place_raise("ss", k, p)
                if part["front"]:
                    place_stack(k + 1, 0)
            nb = [sum(bool(q["back"]) for q in parts[:k]) for k in range(len(parts) + 1)]
            na = [sum(bool(q["attend"]) for q in parts[:k]) for k in range(len(parts) + 1)]
            nf = [sum(bool(q["front"]) for q in parts[:k]) for k in range(len(parts) + 1)]

            def full(*unit):
                return filled[bank_of[unit]], fill_of[unit]

            def read(*unit):
                return drained[bank_of[unit]], read_of[unit]

            def of(*unit):
                return bank[bank_of[unit]]

            def turns(back, front, k):
                part = parts[k]
                filler = {"b": back(k, *part["back"]) if part["back"] else None,
                          "f": front(k, *part["front"]) if part["front"] else None}

                def take(chunks):
                    for which in chunks:
                        if which in filler and filler[which]:
                            next(filler[which])

                if not part["attend"]:
                    take("".join(SCHEDULE))
                    return
                for slot in range(3 * len(steps_of(k))):
                    if slot < SLOTS:
                        take(SCHEDULE[slot])
                    yield

            def run_parts(attend, back, front):
                for k, part in enumerate(parts):
                    slots = turns(back, front, k)
                    if part["attend"]:
                        attend(k, part["attend"][0], lambda slots=slots: next(slots))
                    for _ in slots:
                        pass

            def stored(image_done):
                return 16 * B + 16 * PAIRS * image_done

            with nc.Block() as block:

                @block.sync
                def _(sp):
                    def load_stack(parity, g):
                        t, first = divmod(g * GH * HD, P)
                        for w, stack, halves in ((0, q_stack, (0, 1, 0)), (1, k_stack, (0, 0, 1))):
                            for r, half in enumerate(halves):
                                sp.dma_start(
                                    stack[r * HD:(r + 1) * HD,
                                          (g % 2) * GH:(g % 2 + 1) * GH, :].bitcast(F32),
                                    scratch[parity, w, half, t, first:first + GH * HD, :]
                                    .rearrange("(j p) n -> p j n", p=HD)).then_inc(s_stack[g % 2], 16)
                            if g < 2:
                                sp.dma_start(
                                    stack[CONTENT:ROWS, g * GH:(g + 1) * GH, :].bitcast(F32),
                                    rope_scratch[parity, w, :, 0:1, :].broadcast_to([DR, GH, T])
                                    ).then_inc(s_stack[g], 16)

                    def load_cross(parity):
                        for w, cross, halves in ((0, q_cross, (1, 0)), (1, k_cross, (0, 1))):
                            for n, half in enumerate(halves):
                                sp.dma_start(
                                    cross[n * DR:(n + 1) * DR, :, :].bitcast(F32),
                                    rope_scratch[parity, w, :, half:half + 1, :].broadcast_to([DR, 2, T])
                                    ).then_inc(s_cross, 16)

                    def store_rows(k, p, parity, image):
                        sp.wait_ge(s_out, PAIRS * nb[k] + p + 1)
                        sp.dma_start(out_tiles[bass.ds(image, 1), :, 2 * p:2 * p + 2, :]
                                     .rearrange("b p i n -> p (b i) n"),
                                     xn[:, 2 * p:2 * p + 2, :]).then_inc(s_stored, 16)

                    for k, part in enumerate(parts):
                        if part["attend"]:
                            if k and parts[k - 1]["attend"]:
                                sp.wait_ge(*full("sT", k - 1, H - 1, 2))
                            load_cross(part["attend"][0])
                            load_stack(part["attend"][0], 1)
                        if part["front"]:
                            image = part["front"][1]
                            sp.wait_ge(*full("xT", k, PAIRS - 1, XU - 1))
                            sp.dma_start(x_in[:, :, :], x_tiles[bass.ds((image + 1) % B, 1)]
                                         .rearrange("b p i n -> p (b i) n")).then_inc(s_x, 16)
                        def load_later(g):
                            sp.wait_ge(*full("sT", k, (g - 1) * GH - 1, 2))
                            load_stack(part["attend"][0], g)

                        if part["attend"]:
                            load_later(2)
                        if part["front"]:
                            parity = part["front"][0]
                            if k and parts[k - 1]["attend"]:
                                sp.wait_ge(s_stack[0], stack_load[(k - 1, 2)])
                                sp.wait_ge(s_stack[1], stack_load[(k - 1, 3)])
                                sp.wait_ge(s_cross, 64 * na[k])
                            for w, name in ((0, "q"), (1, "k")):
                                for t in range(FT):
                                    sp.wait_ge(*read(name, k, t))
                                sp.dma_start(scratch[parity, w].rearrange("a t p n -> p (a t) n"),
                                             qk[:, w].bitcast(F32).rearrange("p a t n -> p (a t) n")
                                             ).then_inc(s_scratch, 16)
                            sp.wait_ge(*read("rope", k))
                            sp.dma_start(rope_scratch[parity].rearrange("w p a n -> (w p) a n"),
                                         rope[:, :, :].bitcast(F32)).then_inc(s_scratch, 16)
                        if part["attend"]:
                            load_later(3)
                        if part["front"]:
                            sp.wait_ge(s_scratch, 48 * (nf[k] + 1))
                        if part["back"]:
                            store_rows(k, 0, *part["back"])
                        if part["front"]:
                            if part["attend"]:
                                sp.wait_ge(*full("sT", k, 3 * GH - 1, 2))
                            load_stack(part["front"][0], 0)
                        if part["back"]:
                            store_rows(k, 1, *part["back"])
                    if parts[-1]["front"]:
                        sp.wait_ge(s_stack[0], loads[0])

                @block.gpsimd
                def _(pool):
                    steps = [0]

                    def raise_base(cols, *norm):
                        pool.wait_ge(s_base, raises[norm])
                        nc.gpsimd.tensor_tensor(root[:, :, cols], base[:, :, cols], powers[:, :, cols],
                                                ALU.pow).then_inc(s_root, 1)

                    def raise_next(k):
                        pool.wait_ge(s_base_next, nf[k] + 1)
                        nc.gpsimd.tensor_tensor(root_next[:, 0, :], base_next[:, 0, :], powers[:, 0, :],
                                                ALU.pow).then_inc(s_root_next, 1)

                    for k, part in enumerate(parts):
                        if part["front"]:
                            raise_next(k)
                        if part["back"]:
                            if na[k]:
                                pool.wait_ge(s_p0, na[k])
                            for i in range(TT):
                                nc.gpsimd.tensor_tensor(
                                    p0_v0[:, i, :].rearrange("p (n d) -> p n d", d=HD),
                                    v0_all[:, :].rearrange("p (n d) -> p n d", d=HD),
                                    p0[:, i, :].unsqueeze(2).broadcast_to([P, H, HD]),
                                    ALU.mult).then_inc(s_p0v0, 1)
                            raise_base(slice(0, TT), "back", k)
                            for p in range(PAIRS):
                                for n in range(GU):
                                    pool.wait_ge(*read("g", k, p, n))
                                    g = g_sb[:, (p * GU + n) % RING, :]
                                    if n == 0:
                                        if part["front"] and p == 0:
                                            pool.wait_ge(*full("s0", k))
                                        if p:
                                            pool.wait_ge(*full("ss", k, p - 1))
                                        nc.gpsimd.tensor_tensor(g_acc[:, :], g, g,
                                                                ALU.mult).then_inc(s_g_sum, 1)
                                        continue
                                    pool.wait_ge(s_g_sum, PAIRS * GU * nb[k] + p * GU + n)
                                    steps[0] += 1
                                    nc.gpsimd.tensor_tensor(g_sq[:, :], g, g, ALU.mult).then_inc(s_g_sq, 1)
                                    pool.wait_ge(s_g_sq, steps[0])
                                    nc.gpsimd.tensor_tensor(g_acc[:, :], g_acc[:, :], g_sq[:, :],
                                                            ALU.add).then_inc(s_g_sum, 1)
                                raise_base(slice(2 * p, 2 * p + 2), "ss", k, p)
                        if part["front"]:
                            if part["back"]:
                                pool.wait_ge(s_out, PAIRS * (nb[k] + 1))
                            for p in range(PAIRS):
                                pool.wait_ge(*read("h", k, p))
                            nc.gpsimd.tensor_copy(h[:, part["front"][0], :, :], h_next[:, :, :]
                                                  ).then_inc(s_h_moved, 1)

                @block.scalar
                def _(act):
                    def copy(dst, src):
                        return nc.scalar.activation(dst, src, ACT.Copy)

                    def attend(k, parity, slot):
                        for step in steps_of(k):
                            slot()
                            if pair_at(step):
                                m = step // 2 - 1
                                if m >= 2:
                                    act.wait_ge(*full("sT", *head_at(2 * m - 3), 2))
                                unit = ("m", *pair_at(step))
                                act.wait_ge(*full(*unit))
                                copy(q_cross[2 * DR:CROSS, m % 2, :], of(*unit)[2 * DR:CROSS, :]
                                     ).then_inc(drained[bank_of[unit]], 1)
                            if step % H == 0 and step:
                                act.wait_ge(s_p0_in, step // H)
                                nc.scalar.activation(p0[:, :, :], denom[:, :, :], ACT.Exp,
                                                     scale=SCALE).then_inc(s_p0, 1)
                            head = head_at(step - LAG)
                            for u, n in enumerate(PT_UNITS):
                                if head:
                                    at = step - LAG
                                    if u == 0 and at >= 2:
                                        act.wait_ge(s_pv, at - 1)
                                    act.wait_ge(*full("sT", *head, u))
                                    nc.scalar.activation(
                                        probs_T[:, at % 2, 512 * u:512 * u + n],
                                        of("sT", *head, u)[:, 0:n], ACT.Exp,
                                        scale=SCALE).then_inc(drained[bank_of[("sT", *head, u)]], 1)
                                if u == 1:
                                    slot()
                            at = step - LAG - 1
                            if head_at(at) and at % GH == GH - 1:
                                now, hd = head_at(at)
                                act.wait_ge(s_pv, at + 1)
                                if hd == GH - 1 and parts[now]["back"]:
                                    act.wait_ge(*full("oTok", now, TT - 1))
                                copy(oT[:, hd // GH, :], bank[7][:, :]).then_inc(drained[7], 1)
                            slot()

                    def features_hi(k, stage):
                        for f in range(FT):
                            act.wait_ge(*full(stage, k, f))
                            copy(fT_hi[:, f, :], of(stage, k, f)[:, :]).then_inc(s_fT_hi, 1)

                    def back(k, parity, image):
                        for i in range(TT):
                            yield
                        if parts[k]["front"]:
                            act.wait_ge(*full("rot", k))
                        features_hi(k, "fT1")
                        yield
                        yield
                        yield
                        yield
                        features_hi(k, "fT2")
                        yield
                        for p in range(PAIRS):
                            for n in range(GU):
                                u = p * GU + n
                                act.wait_ge(*full("g", k, p, n))
                                if u >= RING:
                                    act.wait_ge(s_g_split, PAIRS * GU * nb[k] + u - RING + 1)
                                    act.wait_ge(s_g_sum, PAIRS * GU * nb[k] + u - RING + 1)
                                nc.scalar.activation(g_sb[:, u % RING, :], of("g", k, p, n)[:, :], ACT.Gelu
                                                     ).then_inc(drained[bank_of[("g", k, p, n)]], 1)
                                if n % 2:
                                    yield
                            yield
                            yield
                        yield

                    def front(k, parity, image):
                        def take_h(p):
                            if nf[k]:
                                act.wait_ge(s_h_moved, nf[k])
                                act.wait_ge(s_xn_a, TT * nf[k])
                            act.wait_ge(*full("h", k, p))
                            copy(h_next[:, 2 * p:2 * p + 2, :].rearrange("p i n -> p (i n)"),
                                 bank[6][:, :]).then_inc(drained[6], 1)

                        for p in range(PAIRS):
                            for n in range(XU):
                                act.wait_ge(*full("xT", k, p, n))
                                u = p * XU + n
                                if u == XU + 1:
                                    act.wait_ge(*full("h", k, 0))
                                elif u >= RING:
                                    act.wait_ge(s_tok_used, (XU - 1) * PAIRS * nf[k] + u - RING + 1 - (u > XU))
                                copy(xT_hi[:, u % RING, :], of("xT", k, p, n)[:, :]).then_inc(s_xT_hi, 1)
                                if u == XU + 1:
                                    take_h(0)
                                yield
                        yield
                        take_h(1)
                        yield
                        yield
                        if nb[k]:
                            act.wait_ge(*full("g", k - 1, PAIRS - 1, GU - 1))
                        features_hi(k, "fT0")
                        yield
                        act.wait_ge(*full("c", k))
                        copy(cT_hi, of("c", k)[:, :]).then_inc(s_half, 1)
                        yield
                        if nb[k]:
                            act.wait_ge(*full("d", k - 1, PAIRS - 1))
                        for w, name in ((0, "q"), (1, "k")):
                            for t in range(FT):
                                act.wait_ge(*full(name, k, t))
                                copy(qk[:, w, 0, t, :], of(name, k, t)[:, :]).then_inc(s_half, 1)
                                yield
                        yield
                        for u in range(2):
                            act.wait_ge(*full("v", k, u))
                            for i in range(2):
                                last = copy(v[:, parity, 2 * u + i, 0:H * VW]
                                            .rearrange("p (n d) -> p n d", d=VW)[:, :, 0:HD],
                                            of("v", k, u)[:, i * D:i * D + D]
                                            .rearrange("p (n d) -> p n d", d=HD))
                            last.then_inc(drained[bank_of[("v", k, u)]], 1)
                            yield
                        act.wait_ge(*full("rope", k))
                        copy(rope[:, 0, :], of("rope", k)[0:2 * DR, :]).then_inc(s_half, 1)
                        yield
                        yield

                    run_parts(attend, back, front)

                @block.vector
                def _(dve):
                    steps = [0]

                    def link(ins):
                        steps[0] += 1
                        ins.then_inc(s_dve, 1)
                        dve.wait_ge(s_dve, steps[0])

                    def low(dst, src, hi):
                        return nc.vector.tensor_tensor(dst, src, hi.bitcast(F32), ALU.subtract)

                    rstd = root[:, 0, :]
                    var = moments[:, :, 1]

                    def raise_base(values, cols=slice(0, TT)):
                        for n, (value, scale, eps) in enumerate(values):
                            last = nc.vector.tensor_scalar(base[:, n, cols], value, scale, eps,
                                                           ALU.mult, ALU.add)
                        last.then_inc(s_base, 1)

                    def norm(dst, src, moments, scale, i):
                        return nc.vector.tensor_scalar(dst[:, i, :], src[:, i, :], moments[:, i, 0:1],
                                                       scale[:, i:i + 1], ALU.subtract, ALU.mult)

                    def moments_of(tiles, src, stats, moments):
                        for i in tiles:
                            last = nc.vector.bn_stats(stats[:, i, :], src[:, i, :])
                        link(last)
                        for i in tiles:
                            last = nc.vector.bn_aggr(moments[:, i, :], stats[:, i, :])
                        link(last)

                    def features_lo(k, stage):
                        done = FT * (2 * nb[k] + nf[k + (stage != "fT0")] + (stage == "fT2"))
                        for f in range(FT):
                            dve.wait_ge(s_fT_hi, done + f + 1)
                            low(fT_lo[:, f, :], of(stage, k, f)[:, :], fT_hi[:, f, :]
                                ).then_inc(drained[bank_of[(stage, k, f)]], 1)

                    def p0_exponent(k, parity):
                        dve.wait_ge(s_shift, H * (na[k] + 1))
                        nc.vector.tensor_tensor(denom[:, :, :], shift[:, :, :].bitcast(F32),
                                                neg_s0[:, parity, :, :], ALU.subtract).then_inc(s_p0_in, 1)

                    def attend(k, parity, slot):
                        if nf[k]:
                            dve.wait_ge(*read("s0", k - 1))
                        for step in steps_of(k):
                            hd = step % H
                            for u, tiles in enumerate(((2, 0), (3,), (1,))):
                                if head_at(step):
                                    if u == 0 and step >= 2:
                                        dve.wait_ge(s_shift, step - 1)
                                    dve.wait_ge(*full("s", k, hd, u))
                                    for i in tiles:
                                        c = S_AT[i][1]
                                        last = nc.vector.reduce_max(
                                            row_max[:, hd % 2, i:i + 1],
                                            of("s", k, hd, u)[:, c:c + P * (i + 1)], AX_X)
                                    last.then_inc(drained[bank_of[("s", k, hd, u)]], 1)
                                    if u == 2:
                                        dve.wait_ge(*read("s", k, hd, 1))
                                        dve.wait_ge(*read("s", k, hd, 2))
                                        nc.vector.scalar_tensor_tensor(
                                            out=shift[:, :, hd], in0=row_max[:, hd % 2, :], scalar=-1.0,
                                            in1=neg_s0[:, parity, :, hd], op0=ALU.mult,
                                            op1=ALU.min).then_inc(s_shift, 1)
                                        if hd == H - 1:
                                            p0_exponent(k, parity)
                                slot()

                    def back(k, parity, image):
                        if na[k]:
                            dve.wait_ge(s_p0, na[k])
                        for i in range(TT):
                            dve.wait_ge(*full("oTok", k, i))
                            o = of("oTok", k, i)[:, :].rearrange("p (n d) -> p n d", d=OW)
                            link(nc.vector.tensor_tensor(denom[:, i, :], o[:, :, HD], p0[:, i, :], ALU.add))
                            link(nc.vector.reciprocal(recip[:, i, :], denom[:, i, :]))
                            dve.wait_ge(s_p0v0, TT * nb[k] + i + 1)
                            w = p0_v0[:, i, :].rearrange("p (n d) -> p n d", d=HD)
                            nc.vector.tensor_tensor(w, o[:, :, 0:HD], w, ALU.add
                                                    ).then_inc(drained[bank_of[("oTok", k, i)]], 1)
                            dve.wait_ge(*read("oTok", k, i))
                            if i == 0:
                                dve.wait_ge(s_stored, stored(image))
                            nc.vector.tensor_tensor(
                                xn[:, i, :].rearrange("p (n d) -> p n d", d=HD), w,
                                recip[:, i, :].unsqueeze(2).broadcast_to([P, H, HD]),
                                ALU.mult).then_inc(s_xn_b, 1)
                            yield
                        features_lo(k, "fT1")
                        yield
                        if k >= 2 and parts[k - 2]["front"]:
                            dve.wait_ge(s_h_moved, nf[k - 1])
                        for u in range(PAIRS):
                            dve.wait_ge(*full("y", k, u))
                            rows = h[:, parity, 2 * u:2 * u + 2, :].rearrange("p i n -> p (i n)")
                            nc.vector.tensor_tensor(rows, of("y", k, u)[:, :], rows, ALU.add
                                                    ).then_inc(drained[bank_of[("y", k, u)]], 1)
                            dve.wait_ge(*read("y", k, u))
                            moments_of((2 * u, 2 * u + 1), h[:, parity], stats, moments)
                            if u == PAIRS - 1:
                                raise_base([(var, 1.0, LN_EPS), (var, 1.0, 0.0)])
                            yield
                        rms, scale = col[:, 0, :], col[:, 1, :]
                        dve.wait_ge(s_root, raises[("back", k)])
                        link(nc.vector.tensor_tensor(rms, rstd, root[:, 1, :], ALU.mult))
                        link(nc.vector.tensor_scalar(rms, rms, RMS_EPS, None, ALU.add))
                        link(nc.vector.reciprocal(rms, rms))
                        link(nc.vector.tensor_tensor(scale, rstd, rms, ALU.mult))
                        for i in range(TT):
                            norm(xn, h[:, parity], moments, scale, i).then_inc(s_xn_b, 1)
                        yield
                        features_lo(k, "fT2")
                        yield
                        if parts[k]["front"]:
                            dve.wait_ge(*read("s0", k))
                            dve.wait_ge(s_scratch, 48 * (nf[k] + 1))
                        for p in range(PAIRS):
                            for n in range(GU):
                                u = p * GU + n
                                dve.wait_ge(*read("g", k, p, n))
                                if u == GU + 1:
                                    dve.wait_ge(*full("d", k, 0))
                                elif u >= RING:
                                    dve.wait_ge(s_down, (GU - 1) * PAIRS * nb[k] + u - RING + 1 - (u > GU))
                                g = g_sb[:, u % RING, :]
                                link(nc.vector.tensor_copy(g_hi[:, u % RING, :], g))
                                low(g_lo[:, u % RING, :], g, g_hi[:, u % RING, :]).then_inc(s_g_split, 1)
                                if p and n == 1:
                                    final(k, parity, 0)
                                if n % 2:
                                    yield
                            yield
                            cols = slice(2 * p, 2 * p + 2)
                            dve.wait_ge(*full("ss", k, p))
                            ss = of("ss", k, p)[:, 0:2]
                            nc.vector.tensor_scalar(base[:, 0, cols], ss, 1.0, 1.0, ALU.mult, ALU.add)
                            nc.vector.tensor_scalar(base[:, 1, cols], ss, 1.0 / FF, None, ALU.mult
                                                    ).then_inc(drained[bank_of[("ss", k, p)]], 1)
                            dve.wait_ge(*read("ss", k, p))
                            nc.vector.engine_nop().then_inc(s_base, 1)
                            yield
                        final(k, parity, 1)
                        yield

                    def final(k, parity, p):
                        cols = slice(2 * p, 2 * p + 2)
                        rms, scale = col[:, 0, cols], col[:, 1, cols]
                        dve.wait_ge(s_root, raises[("ss", k, p)])
                        link(nc.vector.tensor_scalar(rms, root[:, 1, cols], RMS_EPS, None, ALU.add))
                        link(nc.vector.reciprocal(scale, rms))
                        dve.wait_ge(*full("d", k, p))
                        for i in range(2):
                            last = nc.vector.scalar_tensor_tensor(
                                out=xn[:, 2 * p + i, :], in0=bank[6][:, i * D:i * D + D],
                                scalar=scale[:, i:i + 1], in1=h[:, parity, 2 * p + i, :],
                                op0=ALU.mult, op1=ALU.add)
                        last.then_inc(drained[6], 1)
                        dve.wait_ge(*read("d", k, p))
                        nc.vector.engine_nop().then_inc(s_out, 1)

                    def front(k, parity, image):
                        done = PAIRS * XU * nf[k]
                        for p in range(PAIRS):
                            for n in range(XU):
                                u = p * XU + n
                                dve.wait_ge(s_xT_hi, done + u + 1)
                                low(xT_lo[:, u % RING, :], of("xT", k, p, n)[:, :], xT_hi[:, u % RING, :]
                                    ).then_inc(drained[bank_of[("xT", k, p, n)]], 1)
                                if p and n == 2:
                                    dve.wait_ge(*read("h", k, 0))
                                    moments_of((0, 1), h_next, stats_next, moments_next)
                                yield
                        yield
                        dve.wait_ge(*read("h", k, 1))
                        moments_of((2, 3), h_next, stats_next, moments_next)
                        nc.vector.tensor_scalar(base_next[:, 0, :], moments_next[:, :, 1], 1.0, LN_EPS,
                                                ALU.mult, ALU.add).then_inc(s_base_next, 1)
                        yield
                        dve.wait_ge(s_root_next, nf[k] + 1)
                        for i in range(TT):
                            norm(xn_next, h_next, moments_next, root_next[:, 0, :], i).then_inc(s_xn_a, 1)
                        yield
                        features_lo(k, "fT0")
                        yield
                        done = 6 * nf[k] + 1
                        dve.wait_ge(s_half, done)
                        low(cT_lo, of("c", k)[:, :], cT_hi).then_inc(drained[bank_of[("c", k)]], 1)
                        yield
                        for w, name in ((0, "q"), (1, "k")):
                            for t in range(FT):
                                done += 1
                                dve.wait_ge(s_half, done)
                                low(qk[:, w, 1, t, :], of(name, k, t)[:, :],
                                    qk[:, w, 0, t, :]).then_inc(drained[bank_of[(name, k, t)]], 1)
                                yield
                        dve.wait_ge(*full("rot", k))
                        nc.vector.tensor_tensor(prod[:, :], of("rot", k)[:, :], table("rope"),
                                                ALU.mult).then_inc(drained[bank_of[("rot", k)]], 1)
                        yield
                        yield
                        yield
                        dve.wait_ge(s_half, done + 1)
                        low(rope[:, 1, :], of("rope", k)[0:2 * DR, :], rope[:, 0, :]
                            ).then_inc(drained[bank_of[("rope", k)]], 1)
                        yield
                        dve.wait_ge(*full("s0", k))
                        nc.vector.tensor_scalar(neg_s0[:, parity, :, :],
                                                of("s0", k)[:, 0:TT * H].rearrange("p (i n) -> p i n", n=H),
                                                -1.0, None, ALU.mult
                                                ).then_inc(drained[bank_of[("s0", k)]], 1)
                        yield

                    run_parts(attend, back, front)

                @block.tensor
                def _(pe):
                    fT = (fT_hi, fT_lo)
                    cT = (cT_hi, cT_lo)

                    def claim(*unit):
                        if before[unit] > 0:
                            pe.wait_ge(drained[bank_of[unit]], before[unit])
                        return bank[bank_of[unit]]

                    def product(dst, pairs):
                        for n, (lhsT, rhs) in enumerate(pairs):
                            last = nc.tensor.matmul(dst, lhsT, rhs, start=n == 0,
                                                    stop=n == len(pairs) - 1)
                        return last

                    def fill(unit, dst, pairs):
                        product(dst, pairs).then_inc(filled[bank_of[unit]], 1)

                    def from_features(name, width, first):
                        return [(weight(w_half[a], name, f, width, first, P), fT[c][:, f, :])
                                for f in range(FT) for a, c in HALVES]

                    def from_latent(name, first):
                        return [(weight(w_half[a], name, 0, 0, first, P), cT[c]) for a, c in HALVES]

                    def transpose_features(k, stage, rows, ready, count):
                        for f in range(FT):
                            claim(stage, k, f)
                        for i in range(TT):
                            pe.wait_ge(ready, count + i + 1)
                            for f in range(FT):
                                last = nc.tensor.transpose(of(stage, k, f)[:, i * P:i * P + P],
                                                           rows[:, i, f * P:f * P + P], ident)
                                if i == TT - 1:
                                    last.then_inc(filled[bank_of[(stage, k, f)]], 1)

                    def features_split(k, stage):
                        for f in range(FT):
                            pe.wait_ge(*read(stage, k, f))

                    def scores(k, hd, u):
                        g = hd // GH
                        slot = (g % 2) * GH + hd % GH
                        if u == 0 and hd % GH == 0 and (k, g) in stack_load:
                            pe.wait_ge(s_stack[g % 2], stack_load[(k, g)])
                        dst = claim("s", k, hd, u)
                        tiles = [i for i in S_ORDER if S_AT[i][0] == u]
                        for i in tiles:
                            c, n = S_AT[i][1], P * (i + 1)
                            nc.tensor.matmul(dst[:, c:c + n], q_stack[0:ROWS, slot, i * P:i * P + P],
                                             k_stack[0:ROWS, slot, 0:n], start=i == tiles[0], stop=False,
                                             skip_group_check=True)
                        c = S_AT[tiles[0]][1] + P * tiles[0]
                        last = nc.tensor.matmul(dst[:, c:c + P * len(tiles)], ident_b[:, :],
                                                causal_b[:, :].unsqueeze(1).broadcast_to([P, len(tiles), P]), start=False, stop=True,
                                                skip_group_check=True)
                        last.then_inc(filled[bank_of[("s", k, hd, u)]], 1)

                    def shift_rows(k, m):
                        pe.wait_ge(s_shift, H * na[k] + 2 * m + 2)
                        dst = claim("m", k, m)
                        for i in range(TT):
                            last = nc.tensor.matmul(dst[2 * DR:CROSS, i * P:i * P + P],
                                                    shift[:, i, 2 * m:2 * m + 2].bitcast(F32), ident,
                                                    start=True, stop=True)
                        last.then_inc(filled[bank_of[("m", k, m)]], 1)

                    def transposed_scores(k, hd, u):
                        slot = (hd // GH % 2) * GH + hd % GH
                        if u == 0 and hd == 0:
                            pe.wait_ge(s_cross, 64 * (na[k] + 1))
                        if u == 0 and hd % 2 == 0:
                            pe.wait_ge(*read("m", k, hd // 2))
                        dst = claim("sT", k, hd, u)
                        tiles = [j for j in (0, 3, 1, 2) if PT_AT[j][0] == u]
                        for j in tiles:
                            c, n = PT_AT[j][1], T - j * P
                            keys = slice(j * P, j * P + P)
                            nc.tensor.matmul(dst[:, c:c + n], k_stack[0:ROWS, slot, keys],
                                             q_stack[0:ROWS, slot, j * P:T],
                                             start=j == tiles[0], stop=False,
                                             skip_group_check=True)
                            nc.tensor.matmul(dst[:, c:c + n], k_cross[0:CROSS, hd % 2, keys],
                                             q_cross[0:CROSS, hd // 2 % 2, j * P:T],
                                             start=False, stop=False, skip_group_check=True)
                        last = nc.tensor.matmul(dst[:, 0:P * len(tiles)], causal_b[:, :],
                                                ident_b[:, :].unsqueeze(1).broadcast_to([P, len(tiles), P]), start=False, stop=True,
                                                skip_group_check=True)
                        last.then_inc(filled[bank_of[("sT", k, hd, u)]], 1)

                    def sum_values(k, parity, hd):
                        if hd % GH == 0:
                            claim("o", k, hd // GH)
                        r = OW * (hd % GH)
                        for u in range(3):
                            pe.wait_ge(*read("sT", k, hd, u))
                        for j in range(TT):
                            u, c = PT_AT[j]
                            last = nc.tensor.matmul(bank[7][r:r + OW, j * P:T],
                                                    v[:, parity, j, hd * VW:hd * VW + OW],
                                                    probs_T[:, hd % 2, 512 * u + c:512 * u + c + T - j * P],
                                                    start=j == 0, stop=j == TT - 1)
                        last.then_inc(s_pv, 1)

                    def attend(k, parity, slot):
                        for step in steps_of(k):
                            head, last_head = head_at(step - LAG), head_at(step - LAG - 1)
                            if head_at(step):
                                scores(*head_at(step), 0)
                            slot()
                            if pair_at(step):
                                shift_rows(*pair_at(step))
                            if head_at(step):
                                scores(*head_at(step), 1)
                            for u in range(2):
                                if head:
                                    transposed_scores(*head, u)
                            slot()
                            if head_at(step):
                                scores(*head_at(step), 2)
                            if head:
                                transposed_scores(*head, 2)
                            if last_head:
                                part, hd = last_head
                                if nf[part] and hd == 0:
                                    for u in range(2):
                                        pe.wait_ge(*read("v", part - 1, u))
                                sum_values(part, parts[part]["attend"][0], hd)
                            slot()

                    def back(k, parity, image):
                        if na[k]:
                            pe.wait_ge(*read("o", k - 1, NG - 1))
                        for i in range(TT):
                            dst = claim("oTok", k, i)
                            for g in range(NG):
                                last = nc.tensor.transpose(dst[:, g * P:g * P + P],
                                                           oT[:, g, i * P:i * P + P], ident)
                            last.then_inc(filled[bank_of[("oTok", k, i)]], 1)
                            yield
                        transpose_features(k, "fT1", xn, s_xn_b, 2 * TT * nb[k])
                        yield
                        features_split(k, "fT1")
                        for u in range(PAIRS):
                            dst = claim("y", k, u)
                            for j in range(2):
                                cols = slice((2 * u + j) * P, (2 * u + j + 1) * P)
                                last = product(dst[:, j * D:j * D + D],
                                               [(fT[c][:, f, cols], weight(w_half[a], "o", f, D, 0, D))
                                                for f in range(FT) for a, c in HALVES])
                            last.then_inc(filled[bank_of[("y", k, u)]], 1)
                            yield
                        yield
                        transpose_features(k, "fT2", xn, s_xn_b, 2 * TT * nb[k] + TT)
                        yield
                        features_split(k, "fT2")

                        def up(p, n):
                            dst = claim("g", k, p, n)
                            for j in range(2):
                                ft = 2 * n + j
                                last = product(dst[:, j * 256:j * 256 + 256],
                                               [(up_T[:, f, ft * P:ft * P + P],
                                                 fT[c][:, f, p * 256:p * 256 + 256])
                                                for f in range(FT) for c in range(2)])
                            last.then_inc(filled[bank_of[("g", k, p, n)]], 1)

                        def down(p, n):
                            u = p * GU + n
                            pe.wait_ge(s_g_split, PAIRS * GU * nb[k] + u + 1)
                            dst = claim("d", k, p)
                            for j in range(2):
                                for i in range(2):
                                    at = j * 256 + i * P
                                    for c, data in enumerate((g_hi, g_lo)):
                                        last = nc.tensor.matmul(
                                            dst[:, i * D:i * D + D], data[:, u % RING, at:at + P],
                                            down_T[:, 2 * n + j, :], start=n + j + i + c == 0,
                                            stop=n == GU - 1 and j + c == 2, skip_group_check=True)
                            last.then_inc(filled[6] if n == GU - 1 else s_down, 1)

                        for p in range(PAIRS):
                            for n in range(0, GU, 2):
                                up(p, n)
                                up(p, n + 1)
                                if n:
                                    down(p, n - 2)
                                    down(p, n - 1)
                                yield
                            down(p, GU - 2)
                            down(p, GU - 1)
                            yield
                            pe.wait_ge(s_g_sum, PAIRS * GU * nb[k] + (p + 1) * GU)
                            dst = claim("ss", k, p)
                            for i in range(2):
                                last = product(dst[:, i:i + 1],
                                               [(g_acc[:, j * 256 + i * P:j * 256 + i * P + P], ones[:, 0:1])
                                                for j in range(2)])
                            last.then_inc(filled[bank_of[("ss", k, p)]], 1)
                            yield
                        yield

                    def front(k, parity, image):
                        def transpose_x(p, n):
                            dst = claim("xT", k, p, n)
                            for j in range(2):
                                for i in range(2):
                                    kt = 2 * n + j
                                    at = j * 256 + i * P
                                    last = nc.tensor.transpose(dst[:, at:at + P],
                                                               x_in[:, 2 * p + i, kt * P:kt * P + P], ident)
                            last.then_inc(filled[bank_of[("xT", k, p, n)]], 1)

                        def tokens(p, n):
                            u = p * XU + n
                            pe.wait_ge(*read("xT", k, p, n))
                            dst = claim("h", k, p)
                            for j in range(2):
                                for i in range(2):
                                    at = j * 256 + i * P
                                    for c, (data, w) in enumerate(((xT_hi, tok_hi), (xT_hi, tok_lo),
                                                                   (xT_lo, tok_hi))):
                                        last = nc.tensor.matmul(
                                            dst[:, i * D:i * D + D], data[:, u % RING, at:at + P],
                                            w[:, 2 * n + j, :], start=n + j + i + c == 0,
                                            stop=n == XU - 1 and j == 1 and c == 2, skip_group_check=True)
                            last.then_inc(filled[6] if n == XU - 1 else s_tok_used, 1)

                        pe.wait_ge(s_x, 16 * (image + 1))
                        units = [(p, n) for p in range(PAIRS) for n in range(XU)]
                        for n, unit in enumerate(units):
                            if n >= 2:
                                tokens(*units[n - 2])
                            transpose_x(*unit)
                            yield
                        for unit in units[-2:]:
                            tokens(*unit)
                            yield
                        yield
                        transpose_features(k, "fT0", xn_next, s_xn_a, TT * nf[k])
                        yield
                        features_split(k, "fT0")
                        fill(("c", k), claim("c", k)[:, :], from_features("kv_down", DC, 0))
                        yield
                        for t in range(FT):
                            fill(("q", k, t), claim("q", k, t)[:, :], from_features("q", D, t * P))
                            yield
                        pe.wait_ge(*read("c", k))
                        for t in range(FT):
                            fill(("k", k, t), claim("k", k, t)[:, :], from_latent("k_up", t * P))
                            yield
                        fill(("rot", k), claim("rot", k)[:, :],
                             from_features("rot_q", P, 0) + from_latent("rot_k", 0))
                        yield
                        for u in range(2):
                            dst = claim("v", k, u)
                            for i in range(2):
                                cols = slice((2 * u + i) * P, (2 * u + i + 1) * P)
                                last = product(dst[:, i * D:i * D + D],
                                               [(cT[c][:, cols], weight(w_half[a], "v_up", 0, 0, 0, D))
                                                for a, c in HALVES])
                            last.then_inc(filled[bank_of[("v", k, u)]], 1)
                            yield
                        pe.wait_ge(*read("rot", k))
                        fill(("rope", k), claim("rope", k)[0:2 * DR, :], [(table("fold"), prod[:, :])])
                        yield
                        for t in range(FT):
                            pe.wait_ge(*read("q", k, t))
                        dst = claim("s0", k)
                        for i in range(TT):
                            cols = slice(i * P, i * P + P)
                            last = product(dst[:, i * H:i * H + H],
                                           [(qk[:, 0, c, t, cols], (k0_hi, k0_lo)[a][:, t, :])
                                            for t in range(FT) for a, c in HALVES]
                                           + [(prod[:, cols], k0_rope[:, :])])
                        last.then_inc(filled[bank_of[("s0", k)]], 1)
                        yield

                    run_parts(attend, back, front)

            nc.all_engine_barrier(sems_to_clear=range(numbers[0], numbers[-1] + 1))

        def part(attend=None, back=None, front=None):
            def image(b):
                return None if b is None else b if isinstance(b, tuple) else (b % 2, b)
            return {"attend": image(attend), "back": image(back), "front": image(front)}

        PER_BLOCK = 4
        looped = (B - 2) // PER_BLOCK * PER_BLOCK
        images([part(front=0), part(attend=0, front=1)])
        with nc.Fori(1, 1 + looped, PER_BLOCK) as b:
            images([part(attend=((1 + n) % 2, b + n), back=(n % 2, b + n - 1), front=(n % 2, b + n + 1))
                    for n in range(PER_BLOCK)])
        images([part(attend=b, back=b - 1, front=b + 1) for b in range(1 + looped, B - 1)]
               + [part(attend=B - 1, back=B - 2), part(back=B - 1)])
        nc.sync.wait_ge(s_stored, 16 * B + 16 * PAIRS * B)
        nc.sync.wait_ge(s_x, 16 * (B + 1))

_INS = ["x", "cls_tok", "L0_tok_weight", "L0_tok_weighted_sum", "L0_attn_W_kv_down", "L0_attn_W_k_up",
        "L0_attn_W_v_up", "L0_attn_W_q", "L0_attn_W_q_rope", "L0_attn_W_k_rope", "L0_attn_W_o",
        "L0_ffn_w_up", "L0_ffn_w_down"]


def shape_constants(head_count, tokens, head_dim, rope_dim):
    import numpy as np

    at, width = constant_layout(head_count, tokens)
    c = np.zeros((P, width), np.float32)

    def put(name, value):
        first, n = at[name]
        c[:value.shape[0], first:first + n] = value

    r = np.arange(P)
    put("identity", np.eye(P, dtype=np.float32))
    put("causal", np.where(r[None, :] > r[:, None], np.float32(MASKED), np.float32(0)))
    fold = np.zeros((P, 2 * rope_dim), np.float32)
    select = np.zeros((P, 2), np.float32)
    for j in range(2 * rope_dim):
        fold[2 * rope_dim * (j // rope_dim) + j % rope_dim, j] = 1
        fold[2 * rope_dim * (j // rope_dim) + rope_dim + j % rope_dim, j] = 1
    put("fold", fold)
    for j in range(2):
        select[2 * rope_dim + j, j] = 1
    put("select", select)
    head_of = np.zeros((P, 2, head_count), np.float32)
    for t in range(2):
        head_of[r, t, (t * P + r) // head_dim] = 1
    put("head_of", head_of.reshape(P, -1))
    put("powers", np.tile(np.repeat(np.float32([-0.5, 0.5]), 4), (P, 1)))
    put("ones", np.ones((P, P), np.float32))
    inv_freq = np.float32(1.0) / np.float32(10000.0) ** (
        np.arange(0, rope_dim, 2, dtype=np.float32) / np.float32(rope_dim))
    angles = np.outer(inv_freq, np.arange(1, tokens + 1, dtype=np.float32)).astype(np.float32)
    cos, sin = np.cos(angles), np.sin(angles)
    put("rope", np.concatenate([cos, cos, sin, sin] * 2, axis=0))
    return c


def kernel(**inputs):
    import numpy as np
    import concourse.bacc as bacc
    from concourse.bass_utils import run_bass_kernel_spmd as run

    nc = bacc.Bacc("TRN2", target_bir_lowering=False, num_devices=1)
    arrays, args = {}, []
    for name in _INS:
        a = np.ascontiguousarray(inputs[name])
        arrays[f"in_{name}"] = a
        args.append(nc.dram_tensor(f"in_{name}", a.shape, mybir.dt.from_np(a.dtype), kind="ExternalInput").ap())
    batch, tokens, dim, _ = inputs["x"].shape
    heads = 16
    c = shape_constants(heads, tokens, dim // heads, inputs["L0_attn_W_q_rope"].shape[1])
    arrays["in_constants"] = c
    args.append(nc.dram_tensor("in_constants", c.shape, F32, kind="ExternalInput").ap())
    args.append(nc.dram_tensor("out_0", (batch, tokens + 1, dim), F32, kind="ExternalOutput").ap())
    vit_tower_kernel(nc, *args)
    r = run(nc, [arrays], core_ids=[0])
    return r.results[0]["out_0"]
```
